# Optimizing a Trainium2 kernel written in Bass

```python
import numpy as np
import jax
import jax.numpy as jnp

def _softmax(x, axis=-1):
    return jax.nn.softmax(x, axis=axis)

def _gelu(x):
    return jax.nn.gelu(x, approximate=True)

def _silu(x):
    return jax.nn.silu(x)

def _sigmoid(x):
    return jax.nn.sigmoid(x)

def _layernorm(x, axis=-1, eps=1e-05):
    m = jnp.mean(x, axis=axis, keepdims=True)
    v = jnp.var(x, axis=axis, keepdims=True)
    return (x - m) / jnp.sqrt(v + eps)

def _scatter_add(tgt, idx, src, axis=0):
    return tgt.at[idx].add(src)

def _segment_sum(src, seg, n):
    return jax.ops.segment_sum(src, seg, n)
kernel_name = 'mk_vit_tower_cls_d1_tok_img1024_r4_2ec99f'

def setup_inputs(seed: int=0):
    np.random.seed(seed)
    _w = jnp.asarray

    def _rec_inputs():
        import jax
        import jax.numpy as jnp
        _rk = jax.random.key(seed)
        x = -0.00016672 + 0.999947 * jax.random.normal(jax.random.fold_in(_rk, 1), (32, 3, 96, 96), jnp.float32)
        cls_tok = 0.02 * jax.random.normal(jax.random.fold_in(_rk, 5), (1, 1, 256), jnp.float32)
        return (x, cls_tok)
    x, cls_tok = _rec_inputs()

    def _L0_tok_setup():
        import jax, jax.numpy as jnp
        import numpy as np
        IMG = 96
        PATCH = 16
        CIN = 3
        EMBED = 256
        NP_ = (IMG // PATCH) ** 2
        key = jax.random.key(seed)
        k1, k2, k3, k4, k5 = jax.random.split(key, 5)
        x = jax.random.normal(k1, (64, CIN, IMG, IMG), dtype=jnp.float32)
        d_in = PATCH * PATCH * CIN
        W = jax.random.normal(k2, (d_in, EMBED), dtype=jnp.float32) / np.sqrt(d_in)
        b = jax.random.normal(k3, (EMBED,), dtype=jnp.float32) * 0.01
        class_token = jax.random.normal(k4, (1, 1, EMBED), dtype=jnp.float32)
        pos_emb = jax.random.normal(k5, (1, NP_ + 1, EMBED), dtype=jnp.float32)
        return {'x': x, 'W': W, 'b': b, 'class_token': class_token, 'pos_emb': pos_emb}
    _L0_tok_all = _L0_tok_setup()
    _L0_tok_in = {k: v for k, v in _L0_tok_all.items() if k in ('W', 'b', 'class_token', 'pos_emb')}
    del _L0_tok_all

    def _L0_attn_setup():
        import jax, jax.numpy as jnp
        import numpy as np
        EMB, HEADS, HIDDEN = (256, 16, 64)
        BS, N = (2, 512)
        key = jax.random.key(seed)
        ks = jax.random.split(key, 7)
        s_in = 1.0 / np.sqrt(EMB)
        s_u = 1.0 / np.sqrt(HEADS * HIDDEN)
        return {'x': jax.random.normal(ks[0], (BS, N, EMB), dtype=jnp.float32), 'w_q': jax.random.uniform(ks[1], (EMB, HEADS * HIDDEN), jnp.float32, -s_in, s_in), 'w_k': jax.random.uniform(ks[2], (EMB, HEADS * HIDDEN), jnp.float32, -s_in, s_in), 'w_v': jax.random.uniform(ks[3], (EMB, HEADS * HIDDEN), jnp.float32, -s_in, s_in), 'w_u': jax.random.uniform(ks[4], (HEADS * HIDDEN, EMB), jnp.float32, -s_u, s_u), 'b_u': jax.random.uniform(ks[5], (EMB,), jnp.float32, -s_u, s_u)}
    _L0_attn_all = _L0_attn_setup()
    _L0_attn_in = {k: v for k, v in _L0_attn_all.items() if k in ('w_q', 'w_k', 'w_v', 'w_u', 'b_u')}
    del _L0_attn_all

    def _L0_ffn_setup():
        import jax, jax.numpy as jnp
        import numpy as np
        B, S, D = (2, 512, 256)
        M = 512
        E = 8
        TOP_K = 2
        key = jax.random.key(seed)
        ks = jax.random.split(key, 5)
        std = 0.02
        return {'residual': jax.random.normal(ks[0], (B, S, D), jnp.float32), 'W_router': jax.random.normal(ks[1], (D, E), jnp.float32) * std, 'W_gate': jax.random.normal(ks[2], (E, D, M), jnp.float32) * std, 'b_gate': jnp.zeros((E, M), jnp.float32), 'W_up': jax.random.normal(ks[3], (E, D, M), jnp.float32) * std, 'b_up': jnp.zeros((E, M), jnp.float32), 'W_out': jax.random.normal(ks[4], (E, M, D), jnp.float32) * std, 'b_out': jnp.zeros((E, D), jnp.float32)}
    _L0_ffn_all = _L0_ffn_setup()
    _L0_ffn_in = {k: v for k, v in _L0_ffn_all.items() if k in ('W_router', 'W_gate', 'b_gate', 'W_up', 'b_up', 'W_out', 'b_out')}
    del _L0_ffn_all
    return {'x': x, 'cls_tok': cls_tok, 'L0_tok_W': _L0_tok_in['W'], 'L0_tok_b': _L0_tok_in['b'], 'L0_tok_class_token': _L0_tok_in['class_token'], 'L0_tok_pos_emb': _L0_tok_in['pos_emb'], 'L0_attn_w_q': _L0_attn_in['w_q'], 'L0_attn_w_k': _L0_attn_in['w_k'], 'L0_attn_w_v': _L0_attn_in['w_v'], 'L0_attn_w_u': _L0_attn_in['w_u'], 'L0_attn_b_u': _L0_attn_in['b_u'], 'L0_ffn_W_router': _L0_ffn_in['W_router'], 'L0_ffn_W_gate': _L0_ffn_in['W_gate'], 'L0_ffn_b_gate': _L0_ffn_in['b_gate'], 'L0_ffn_W_up': _L0_ffn_in['W_up'], 'L0_ffn_b_up': _L0_ffn_in['b_up'], 'L0_ffn_W_out': _L0_ffn_in['W_out'], 'L0_ffn_b_out': _L0_ffn_in['b_out']}

def reference(x, cls_tok, L0_tok_W, L0_tok_b, L0_tok_class_token, L0_tok_pos_emb, L0_attn_w_q, L0_attn_w_k, L0_attn_w_v, L0_attn_w_u, L0_attn_b_u, L0_ffn_W_router, L0_ffn_W_gate, L0_ffn_b_gate, L0_ffn_W_up, L0_ffn_b_up, L0_ffn_W_out, L0_ffn_b_out):
    import jax
    import jax.numpy as jnp

    def _L0_tok_ref(x, W, b, class_token, pos_emb):
        import jax, jax.numpy as jnp
        import numpy as np
        IMG = 96
        PATCH = 16
        CIN = 3
        EMBED = 256
        NP_ = (IMG // PATCH) ** 2
        B = x.shape[0]
        Hp = IMG // PATCH
        patches = x.reshape(B, CIN, Hp, PATCH, Hp, PATCH)
        patches = patches.transpose(0, 2, 4, 1, 3, 5).reshape(B, Hp * Hp, CIN * PATCH * PATCH)
        patch_emb = jnp.einsum('bnd,de->bne', patches, W) + b
        cls = jnp.broadcast_to(class_token, (B, 1, EMBED))
        emb = jnp.concatenate([cls, patch_emb], axis=1) + pos_emb
        return emb

    def _L0_attn_ref(x, w_q, w_k, w_v, w_u, b_u):
        import jax, jax.numpy as jnp
        import numpy as np
        EMB, HEADS, HIDDEN = (256, 16, 64)
        BS, N = (2, 512)
        bs, n, emb = x.shape
        h, hd = (HEADS, HIDDEN)
        q = (x @ w_q).reshape(bs, n, h, hd)
        k = (x @ w_k).reshape(bs, n, h, hd)
        v = (x @ w_v).reshape(bs, n, h, hd)
        scale = 1.0 / jnp.sqrt(jnp.asarray(hd, dtype=x.dtype))
        q = q * scale
        k = k * scale
        dot = jnp.einsum('bqhd,bkhd->bhqk', q, k)
        causal = jnp.tril(jnp.ones((n, n), dtype=bool))
        dot = jnp.where(causal, dot, jnp.asarray(-jnp.inf, dtype=dot.dtype))
        att = jax.nn.softmax(dot, axis=-1)
        out = jnp.einsum('bhqk,bkhd->bqhd', att, v).reshape(bs, n, h * hd)
        return out @ w_u + b_u

    def _L0_ffn_ref(residual, W_router, W_gate, b_gate, W_up, b_up, W_out, b_out):
        import jax, jax.numpy as jnp
        import numpy as np
        B, S, D = (2, 512, 256)
        M = 512
        E = 8
        TOP_K = 2
        router_logits = jnp.einsum('bsd,de->bse', residual, W_router)
        router_probs = jax.nn.softmax(router_logits, axis=-1)
        top_k_probs, top_k_idx = jax.lax.top_k(router_probs, TOP_K)
        top_k_probs = top_k_probs / (jnp.sum(top_k_probs, -1, keepdims=True) + 1e-08)
        one_hot = jax.nn.one_hot(top_k_idx, E, dtype=residual.dtype)
        expert_weights = jnp.einsum('bsk,bske->bse', top_k_probs, one_hot)
        gate = jax.nn.silu(jnp.einsum('bsd,edm->ebsm', residual, W_gate) + b_gate[:, None, None, :])
        up = jnp.einsum('bsd,edm->ebsm', residual, W_up) + b_up[:, None, None, :]
        hidden = gate * up
        expert_out = jnp.einsum('ebsm,emd->ebsd', hidden, W_out) + b_out[:, None, None, :]
        output = jnp.einsum('bse,ebsd->bsd', expert_weights, expert_out)
        return output
    h = _L0_tok_ref(x, L0_tok_W, L0_tok_b, L0_tok_class_token, L0_tok_pos_emb)
    h = jnp.concatenate([jnp.broadcast_to(cls_tok, (h.shape[0], 1, h.shape[2])), h], axis=1)
    h = h + _L0_attn_ref(_layernorm(h, axis=-1), L0_attn_w_q, L0_attn_w_k, L0_attn_w_v, L0_attn_w_u, L0_attn_b_u)
    h = h + _L0_ffn_ref(_layernorm(h, axis=-1), L0_ffn_W_router, L0_ffn_W_gate, L0_ffn_b_gate, L0_ffn_W_up, L0_ffn_b_up, L0_ffn_W_out, L0_ffn_b_out)
    return h

_drawn_inputs = setup_inputs


def setup_inputs(seed=0):
    import zlib

    import numpy as np

    out = dict(_drawn_inputs(seed))
    spreads = {'L0_ffn_b_gate': (0.0, 0.8), 'L0_ffn_b_up': (0.0, 0.8), 'L0_ffn_b_out': (0.0, 0.311)}
    factors = {'L0_tok_b': 7.102,
     'L0_attn_w_q': 8.0,
     'L0_attn_w_k': 8.0,
     'L0_attn_b_u': 4.007,
     'L0_ffn_W_gate': 4.471,
     'L0_ffn_W_up': 4.442,
     'L0_ffn_W_out': 4.241}
    for name, (base, spread) in spreads.items():
        noise = np.random.default_rng([zlib.crc32(name.encode()), seed]).standard_normal(out[name].shape)
        drawn = base * np.exp(spread * noise) if base else spread * noise
        out[name] = jnp.asarray(drawn.astype(out[name].dtype))
    for name, factor in factors.items():
        out[name] = (out[name] * factor).astype(out[name].dtype)
    return out
```

```python
from contextlib import ExitStack

import concourse.bass as bass
from concourse import mybir

F32 = mybir.dt.float32
F32R = mybir.dt.float32r
BF16 = mybir.dt.bfloat16
U32 = mybir.dt.uint32
I32 = mybir.dt.int32
ALU = mybir.AluOpType
ACT = mybir.ActivationFunctionType
AX = mybir.AxisListType

P = 128
IMAGES, CHANNELS, SIDE = 32, 3, 96
PATCH = 16
GRID = SIDE // PATCH
EMB = 256
TOK = GRID * GRID + 2
HEADS, HD = 16, 64
EXPERTS, MID = 8, 512
EPS = 1e-5

GROUPS = 4
GI = IMAGES // GROUPS
GT = GI * TOK
SUBS = (3, 3, 2)
NSUB = len(SUBS)
NS = [n * TOK for n in SUBS]
AT = [0, NS[0], NS[0] + NS[1]]
BLOCKS = GROUPS * NSUB
BM = NS[0]
EK = EMB // P
CK = CHANNELS * PATCH * PATCH // P
HK = HEADS * HD // P
MK = MID // P
NQ = NSUB * 4
XP = GI * GRID
SCALE = 1.0 / HD
NEG = -1.0e30

NDSET = 24 + (IMAGES * TOK + P - 1) // P - 1
CHOOSE, PLACE, LN = 26, 9, 12
TOKENS = IMAGES * TOK
REGION = (TOKENS + P - 1) // P * P + P
MAXNB = (TOKENS + P - 1) // P
MAXBLOCKS = (2 * TOKENS + EXPERTS * P) // P


def vit_tower(nc, x, cls_tok, tok_W, tok_b, tok_class, tok_pos, w_q, w_k, w_v, w_u, b_u,
              W_router, W_gate, b_gate, W_up, b_up, W_out, b_out, out):
    ctx = ExitStack()
    only_a = ExitStack()
    Xs = nc.dram_tensor("Xs", (EXPERTS * REGION, EMB), F32, kind="Internal").ap()
    Ys = nc.dram_tensor("Ys", ((MAXBLOCKS + 1) * P, EMB), F32, kind="Internal").ap()
    with ctx:
        def sb(name, shape, dt=F32, where=ctx):
            return where.enter_context(nc.sbuf_tensor(name, shape, dt))

        def sem(name):
            return ctx.enter_context(nc.semaphore(name))

        raw = [sb(f"raw{i}", [P, 3072]) for i in range(2)]
        H = sb("H", [P, BLOCKS, EMB])
        zero = sb("zero", [P, EMB])
        ident = sb("ident", [P, P])
        lower = sb("lower", [P, P])
        ones = sb("ones", [P, P])
        iota = sb("iota", [P, EXPERTS])
        region = sb("region", [P, EXPERTS])
        yshift = sb("yshift", [P, EXPERTS])
        before = sb("before", [P, EXPERTS, EXPERTS])
        steps128 = sb("steps128", [P, MAXNB])
        carry = sb("carry", [P, EXPERTS])
        live = sb("live", [P, 1])
        xn2 = sb("xn2", [P, NSUB, EMB])
        LG = sb("LG", [P, NSUB, EXPERTS])
        sh = sb("sh", [P, NSUB, EXPERTS])
        ex = sb("ex", [P, NSUB, EXPERTS])
        pr = sb("pr", [P, NSUB, EXPERTS])
        pw = sb("pw", [P, NSUB, EXPERTS])
        tmp8 = sb("tmp8", [P, NSUB, EXPERTS])
        sm = sb("sm", [P, NSUB])
        ri = sb("ri", [P, NSUB])
        top = sb("top", [P, NSUB, 8])
        tpr = sb("tpr", [P, NSUB, 8])
        tix = sb("tix", [P, NSUB, 8], U32)
        tif = sb("tif", [P, NSUB, 2])
        lohi = sb("lohi", [P, 2, NSUB])
        A = sb("A", [P, NSUB, EXPERTS])
        rk = sb("rk", [P, NSUB, EXPERTS])
        pos_i = sb("pos_i", [P, 2, NSUB], U32)
        hot = sb("hot", [P, GROUPS + 1, 2, NSUB, EXPERTS])
        posf = sb("posf", [P, GROUPS + 1, 2, NSUB])
        wst = sb("wst", [P, GROUPS + 1, 2, NSUB])
        posy = sb("posy", [P, GROUPS, 2, NSUB])
        posy_i = sb("posy_i", [P, GROUPS, 2, NSUB], U32)
        cnt = sb("cnt", [P, EXPERTS])
        nbc = sb("nbc", [P, EXPERTS, MAXNB])
        nb = sb("nb", [P, EXPERTS])
        st8 = sb("st8", [P, EXPERTS, EXPERTS])
        st = sb("st", [P, EXPERTS])
        sty = sb("sty", [P, EXPERTS])
        tab = sb("tab", [P, 3, EXPERTS], I32)
        ty = sb("ty", [P, GROUPS, 2, NSUB, EXPERTS])
        def a(name, shape, dt=F32):
            return sb(name, shape, dt, only_a)
        Wth, Wtl = (a(n, [P, CK, EMB], F32R) for n in ("Wth", "Wtl"))
        Wqh, Wql = (a(n, [P, EK, HEADS * HD], F32R) for n in ("Wqh", "Wql"))
        Wkh, Wkl = (a(n, [P, EK, HEADS * HD], F32R) for n in ("Wkh", "Wkl"))
        Wvh, Wvl = (a(n, [P, EK, HEADS * HD], F32R) for n in ("Wvh", "Wvl"))
        Wuh, Wul = (a(n, [P, HK, EMB], F32R) for n in ("Wuh", "Wul"))
        Wr = a("Wr", [P, EK, EXPERTS])
        Wrh, Wrl = (a(n, [P, EK, EXPERTS], F32R) for n in ("Wrh", "Wrl"))
        X = a("X", [XP, CHANNELS, PATCH * SIDE])
        Xr = raw[0][0:XP, 1536:3072].rearrange("p (r w n) -> p r w n", r=2, w=GRID)
        pTh, pTl = (a(n, [P, 2, GI, TOK], F32R) for n in ("pTh", "pTl"))
        pos = a("pos", [BM, EMB])
        pos2 = a("pos2", [BM, EMB])
        bu = a("bu", [BM, EMB])
        xn = a("xn", [BM, NSUB, EMB])
        xTh, xTl = (a(n, [P, EK, GT], F32R) for n in ("xTh", "xTl"))
        stats = a("stats", [BM, NSUB, 6])
        mv = a("mv", [BM, NSUB, 2])
        veps = a("veps", [BM, NSUB])
        rstd = a("rstd", [BM, NSUB])
        minus_half = a("minus_half", [BM, NSUB])
        QT = a("QT", [P, HK, GT])
        KT = a("KT", [P, HK, GT])
        V = a("V", [BM, NSUB, HEADS, HD + 1])
        mask = a("mask", [BM, 4, BM], BF16)
        mask2 = a("mask2", [BM, 4, NS[2]], BF16)
        identb = a("identb", [BM, BM], BF16)
        rowmax = a("rowmax", [BM, 2, 4])
        nmax = a("nmax", [BM, 2, 4])
        Pr = a("Pr", [BM, 2, 4 * BM])
        PT = a("PT", [BM, 2, 4 * BM])
        rsum = a("rsum", [BM, 2, 4])
        O = a("O", [BM, HK, 2, HD])
        OTh, OTl = (a(n, [P, HK, BM], F32R) for n in ("OTh", "OTl"))
        only_a.close()
        Wgh, Wgl, Wph, Wpl = ([sb(f"{n}{i}", [P, EK, MID], F32R) for i in range(2)]
                              for n in ("Wgh", "Wgl", "Wph", "Wpl"))
        bgu = [sb(f"bgu{i}", [P, 2, MID]) for i in range(2)]
        bo = sb("bo", [P, EXPERTS, EMB])
        Woh, Wol = (sb(n, [P, EXPERTS, MK * EMB], F32R) for n in ("Woh", "Wol"))
        xs = sb("xs", [P, EMB])
        bTh, bTl = (sb(n, [P, EK * P], F32R) for n in ("bTh", "bTl"))
        gsum = sb("gsum", [P, MID])
        usum = sb("usum", [P, MID])
        gact = sb("gact", [P, MID])
        hid = sb("hid", [P, MID])
        hTh, hTl = (sb(n, [P, MK * P], F32R) for n in ("hTh", "hTl"))
        ysb = sb("ysb", [P, EMB])
        gath = [r[:].rearrange("p (b e) -> p b e", e=EMB) for r in raw]

        bank = [ctx.enter_context(nc.psum_tensor(f"bank{i}", [P, 512], F32)) for i in range(8)]
        mmb, tpb = bank[0:6], bank[6:8]

        s_carrier = sem("s_carrier")
        s_x = sem("s_x")
        s_xr = sem("s_xr")
        s_wt = sem("s_wt")
        s_wa = [sem(f"s_wa{i}") for i in range(4)]
        s_pos = sem("s_pos")
        s_pos2 = sem("s_pos2")
        s_bu = sem("s_bu")
        s_ys0 = sem("s_ys0")
        s_raw = [sem(f"s_raw{i}") for i in range(2)]
        s_raw2 = [sem(f"s_raw2_{i}") for i in range(2)]
        s_bias = [sem(f"s_bias{i}") for i in range(2)]
        s_bo = sem("s_bo")
        s_scat = sem("s_scat")
        s_sent = sem("s_sent")
        s_tail = sem("s_tail")
        s_xs = sem("s_xs")
        s_yst = sem("s_yst")
        s_gath = [[sem(f"s_gath{k}_{g}") for g in range(GROUPS)] for k in range(2)]
        s_out = sem("s_out")
        s_set = sem("s_set")
        s_dset = sem("s_dset")
        s_wahi = sem("s_wahi")
        s_walo = sem("s_walo")
        s_wthi = sem("s_wthi")
        s_wtlo = sem("s_wtlo")
        s_posadd = sem("s_posadd")
        s_tp = sem("s_tp")
        s_tphi = sem("s_tphi")
        s_tpfree = sem("s_tpfree")
        s_mm = sem("s_mm")
        s_mmact = sem("s_mmact")
        s_mmdve = sem("s_mmdve")
        s_ln = sem("s_ln")
        s_ve = sem("s_ve")
        s_rstd = sem("s_rstd")
        s_xn = sem("s_xn")
        s_hb = sem("s_hb")
        s_rm = sem("s_rm")
        s_nm = sem("s_nm")
        s_rs = sem("s_rs")
        s_lg = sem("s_lg")
        s_sh = sem("s_sh")
        s_rexp = sem("s_rexp")
        s_ro = sem("s_ro")
        s_A = sem("s_A")
        s_pos_i = sem("s_pos_i")
        s_carry = sem("s_carry")
        s_cnt = sem("s_cnt")
        s_tab = sem("s_tab")
        s_tb = sem("s_tb")
        s_posy = sem("s_posy")
        s_whi_a = sem("s_whi_a")
        s_whi_d = sem("s_whi_d")
        s_wlo = sem("s_wlo")
        s_bT = sem("s_bT")
        s_bThi = sem("s_bThi")
        s_bTlo = sem("s_bTlo")
        s_g = sem("s_g")
        s_u = sem("s_u")
        s_gs = sem("s_gs")
        s_us = sem("s_us")
        s_silu = sem("s_silu")
        s_hid = sem("s_hid")
        s_hT = sem("s_hT")
        s_hThi = sem("s_hThi")
        s_hTlo = sem("s_hTlo")
        s_y = sem("s_y")
        s_ysb = sem("s_ysb")
        s_add = sem("s_add")

        mm_uses = [("emb", s) for s in range(NSUB)]
        mm_uses += [(w, m) for w in "qk" for m in range(HK)]
        mm_uses += [("v", n) for n in range(2 * NSUB)]
        mm_uses += [("rank", 0)]
        tp_uses = [("x", c) for c in range(CK)] + [("xT", s) for s in range(NSUB)]
        steps = []
        for t in range(NQ + 6):
            if t < NQ:
                steps.append(("S", t))
            if 1 <= t <= NQ:
                steps.append(("PT", t - 1))
            if 2 <= t <= NQ + 1:
                steps.append(("AV", t - 2))
            if t >= 4 and t % 2 == 0 and t - 4 < NQ:
                steps.append(("OT", (t - 4) // 2))
            if t >= 7 and (t - 7) % 4 == 0 and (t - 7) // 4 < NSUB:
                steps.append(("proj", (t - 7) // 4))
            if t >= 9 and (t - 9) % 4 == 0 and (t - 9) // 4 < NSUB:
                steps.append(("x2T", (t - 9) // 4))
        steps.append(("route", 0))
        mm_uses += [u for u in steps if u[0] in ("S", "AV", "proj", "route")]
        tp_uses += [u for u in steps if u[0] in ("PT", "OT", "x2T")]

        def taker(use):
            kind, n = use
            return "act" if kind == "S" or (kind in "qkv" and n % 2 == 0) else "dve"

        PER = {e: sum(taker(u) == e for u in mm_uses) for e in ("act", "dve")}
        MMS, TPS = len(mm_uses), len(tp_uses)
        assert MMS % len(mmb) == 0 and TPS % len(tpb) == 0 and len(set(mm_uses)) == MMS
        HIS = [u for u in tp_uses if u[0] != "PT"]

        def taken(n):
            e = taker(mm_uses[n])
            return e, sum(taker(u) == e for u in mm_uses[:n + 1])

        def mm_bank(use):
            return mmb[mm_uses.index(use) % len(mmb)]

        def tp_bank(use):
            return tpb[tp_uses.index(use) % len(tpb)]

        def mm_free(pe, g, use):
            n = mm_uses.index(use) - len(mmb)
            e, k = taken(n % MMS)
            pe.wait_ge(s_mmact if e == "act" else s_mmdve, (g + 1) * PER[e] + k - (PER[e] if n < 0 else 0))

        def mm_full(eng, g, use):
            eng.wait_ge(s_mm, g * MMS + mm_uses.index(use) + 1)

        def mm_done(eng, g, use):
            e, k = taken(mm_uses.index(use))
            eng.wait_ge(s_mmact if e == "act" else s_mmdve, (g + 1) * PER[e] + k)

        def tp_free(pe, g, use):
            pe.wait_ge(s_tpfree, g * TPS + tp_uses.index(use) + 1)

        def tp_full(eng, g, use):
            eng.wait_ge(s_tp, g * TPS + tp_uses.index(use) + 1)

        def tp_done(eng, g, use):
            eng.wait_ge(s_tpfree, g * TPS + tp_uses.index(use) + 3)

        def tp_hi(eng, g, use):
            eng.wait_ge(s_tphi, g * len(HIS) + HIS.index(use) + 1)

        WA = [(w_q, Wqh, Wql, raw[1][:, 0:2048]),
              (w_k, Wkh, Wkl, QT[:].rearrange("p m t -> p (m t)")[:, 0:2048]),
              (w_v, Wvh, Wvl, KT[:].rearrange("p m t -> p (m t)")[:, 0:2048]),
              (w_u, Wuh, Wul, raw[1][:, 0:2048])]
        XD = x.rearrange("(g b) c (h i) w -> g b h c (i w)", g=GROUPS, i=PATCH)
        outd = out.rearrange("b t e -> (b t) e")

        def wait_first(eng, s, value):
            eng.wait_ge(s, value)
            eng.sem_inc(s_carrier, 1)

        def flat(t):
            return t[:].rearrange("p k n -> p (k n)")

        def load_expert(eng, e, k, done):
            for j, (w, kk) in enumerate(((W_gate, EK), (W_up, EK), (W_out, MK))):
                eng.dma_start(raw[k][:, j * 1024:(j + 1) * 1024].rearrange("p (k n) -> p k n", k=kk),
                              w[bass.ds(e, 1)].rearrange("a (k p) n -> p (a k) n", p=P)).then_inc(done[k], 16)

        def raw_there(eng, e, k):
            if isinstance(e, int) and e < 2:
                eng.wait_ge(s_raw[k], 48)
            else:
                eng.wait_ge(s_raw2[k], (e - k) * 24)

        def load_bias(eng, e, k):
            for j, b in enumerate((b_gate, b_up)):
                eng.dma_start(bgu[k][:, j, :], b[bass.ds(e, 1)].broadcast_to([P, MID])).then_inc(s_bias[k], 16)

        def bounds(eng, e):
            first = eng.value_load(tab[0:1, 1, bass.ds(e, 1)], min_val=0, max_val=MAXBLOCKS)
            end = eng.value_load(tab[0:1, 2, bass.ds(e, 1)], min_val=1, max_val=MAXBLOCKS)
            return first, end

        def expert_before(eng, e, first, j):
            return ((e - 1 + (j > first)) * (j > 0)).with_bounds(min_val=0, max_val=EXPERTS - 1)

        def end_of_all(eng):
            return eng.value_load(tab[0:1, 2, EXPERTS - 1:EXPERTS], min_val=1, max_val=MAXBLOCKS)

        def x_view(c):
            return tp_bank(("x", c))[:, 0:GRID * XP].rearrange("p (w b h) -> p b h w", w=GRID, b=GI)

        def pT_view(t, c):
            return t[:, c % 2, :, 2:TOK].rearrange("p b (h w) -> p b h w", w=GRID)

        def xT_view(use, s):
            return tp_bank(use)[:, 0:EK * NS[s]].rearrange("p (k t) -> p k t", k=EK)

        def v_dst(n):
            s, half = n // 2, n % 2
            return V[0:NS[s], s, half * 8:half * 8 + 8, 0:HD]

        def v_src(n):
            return mm_bank(("v", n))[0:NS[n // 2], :].rearrange("p (h d) -> p h d", d=HD)

        block = ctx.enter_context(nc.Block())

        @block.sync
        def _(sp):
            def load_x(g):
                for b in range(GI):
                    sp.dma_start(X[b * GRID:(b + 1) * GRID],
                                 XD[bass.ds(g, 1), b].rearrange("a h c n -> (a h) c n")).then_inc(s_x, 16)

            load_x(0)
            sp.dma_start(raw[0][:, 0:CK * EMB].rearrange("p (c e) -> p c e", c=CK),
                         tok_W.rearrange("(c p) e -> p c e", p=P)).then_inc(s_wt, 16)
            sp.dma_start(Wr[:], W_router.rearrange("(k p) e -> p k e", p=P)).then_inc(s_wt, 16)
            for n, (w, _, _, src) in enumerate(WA):
                if n == 3:
                    sp.wait_ge(s_walo, 1)
                sp.dma_start(src.rearrange("p (k n) -> p k n", k=w.shape[0] // P),
                             w.rearrange("(k p) n -> p k n", p=P)).then_inc(s_wa[n], 16)
            sp.wait_ge(s_dset, 2)
            sp.dma_start(Ys.rearrange("(b p) e -> p b e", p=P),
                          zero[:].rearrange("p (b e) -> p b e", b=1).broadcast_to([P, MAXBLOCKS + 1, EMB])
                          ).then_inc(s_ys0, 16)
            with sp.Fori(0, GROUPS - 1) as g:
                sp.wait_ge(s_xr, g * CK + CK)
                load_x(g + 1)
            sp.wait_ge(s_walo, 4)
            load_expert(sp, 1, 1, s_raw)
            sp.wait_ge(s_tp, (GROUPS - 1) * TPS + CK)
            load_expert(sp, 0, 0, s_raw)
            sp.wait_ge(s_mm, (GROUPS - 1) * MMS + mm_uses.index(("v", 2 * NSUB - 1)) + 1)
            for e in range(2):
                load_bias(sp, e, e)
            sp.dma_start(bo[:], b_out.rearrange("(a e) n -> a e n", a=1).broadcast_to([P, EXPERTS, EMB])
                         ).then_inc(s_bo, 16)
            sp.wait_ge(s_tab, 1)
            sp.wait_ge(s_scat, 96 * (GROUPS + 1))
            for e in range(EXPERTS):
                count = sp.value_load(tab[0:1, 0, e:e + 1], min_val=0, max_val=TOKENS)
                sp.dma_start(Xs[bass.ds(count + e * REGION, P), :], zero[:]).then_inc(s_tail, 16)
            sp.wait_ge(s_tail, 16 * EXPERTS)
            with sp.Fori(0, EXPERTS) as e:
                first, end = bounds(sp, e)
                with sp.Fori(first, end) as j:
                    row = (e * REGION + (j - first) * P).with_bounds(min_val=0, max_val=EXPERTS * REGION - P)
                    sp.wait_ge(s_bT, j + 1)
                    sp.dma_start(xs[:], Xs[bass.ds(row, P), :]).then_inc(s_xs, 16)
            sp.wait_ge(s_bT, end_of_all(sp) + 1)
            sp.dma_start(xs[:], W_out[0, 0:P, :]).then_inc(s_xs, 16)
            for b in range(BLOCKS):
                sp.wait_ge(s_add, BLOCKS + b + 1)
                n = NS[b % NSUB]
                t0 = b // NSUB * GT + AT[b % NSUB]
                sp.dma_start(outd[t0:t0 + n, :], H[0:n, b, :]).then_inc(s_out, 16)
            sp.wait_ge(s_out, 16 * BLOCKS)

        @block.gpsimd
        def _(pool):
            pool.memset(ident[:], 0.0).then_inc(s_set, 1)
            pool.memset(identb[:], 0.0).then_inc(s_set, 1)
            pool.memset(mask[:], 0.0).then_inc(s_set, 1)
            pool.memset(lower[:], 1.0).then_inc(s_set, 1)
            pool.memset(before[:], 1.0).then_inc(s_set, 1)
            pool.wait_ge(s_set, 5)
            pool.affine_select(out=ident[:], in_=ident[:], compare_op=ALU.not_equal, fill=1.0, base=0,
                               pattern=[[-1, P]], channel_multiplier=1).then_inc(s_set, 1)
            pool.affine_select(out=identb[:], in_=identb[:], compare_op=ALU.not_equal, fill=1.0, base=0,
                               pattern=[[-1, BM]], channel_multiplier=1).then_inc(s_set, 1)
            pool.affine_select(out=lower[:], in_=lower[:], compare_op=ALU.is_gt, fill=0.0, base=0,
                               pattern=[[1, P]], channel_multiplier=-1).then_inc(s_set, 1)
            pool.affine_select(out=before[:], in_=before[:], compare_op=ALU.is_gt, fill=0.0, base=0,
                               pattern=[[1, EXPERTS], [-1, EXPERTS]], channel_multiplier=0).then_inc(s_set, 1)
            m = mask[:]
            pool.affine_select(out=m, in_=m, compare_op=ALU.is_ge, fill=NEG, base=0,
                               pattern=[[0, 4], [-1, BM]], channel_multiplier=1).then_inc(s_set, 1)
            for h in range(4):
                pool.wait_ge(s_set, 10 + h)
                mh = mask[:, h, :].rearrange("p (j k) -> p j k", k=TOK)
                pool.affine_select(out=mh, in_=mh, compare_op=ALU.is_ge, fill=NEG, base=TOK - 1,
                                   pattern=[[TOK, 3], [0, TOK]], channel_multiplier=-1).then_inc(s_set, 1)
            pool.wait_ge(s_set, 14)
            pool.tensor_copy(mask2[:], mask[:, :, 0:NS[2]]).then_inc(s_set, 1)
            pool.wait_ge(s_dset, NDSET)
            pool.wait_ge(s_bu, 16)
            pool.sem_inc(s_sent, 1)

            def scatter(turn):
                wait_first(pool, s_pos_i, 2 * turn + 2)
                for k in range(2):
                    for s in range(NSUB):
                        pool.indirect_dma_start(
                            out=Xs, out_offset=bass.IndirectOffsetOnAxis(ap=pos_i[0:NS[s], k, s:s + 1], axis=0),
                            in_=xn2[0:NS[s], s, :], in_offset=None).then_inc(s_scat, 16)
                pool.wait_ge(s_scat, 96 * turn + 96)
                pool.sem_inc(s_sent, 1)

            with pool.Fori(0, GROUPS) as g:
                pool.wait_ge(s_ve, g * 4 + 1)
                pool.tensor_tensor(rstd[:], veps[:], minus_half[:], ALU.pow).then_inc(s_rstd, 1)
                for s in range(NSUB):
                    pool.wait_ge(s_xn, g * 6 + s + 1)
                    hb = H[0:NS[s], g * NSUB + s, :]
                    pool.tensor_tensor(hb, hb, bu[0:NS[s], :], ALU.add).then_inc(s_hb, 1)
                scatter(g)
                for s in range(NSUB):
                    pool.wait_ge(s_ve, g * 4 + s + 2)
                    pool.tensor_tensor(rstd[:, s:s + 1], veps[:, s:s + 1], minus_half[:, s:s + 1],
                                       ALU.pow).then_inc(s_rstd, 1)
            scatter(GROUPS)

            def split_lo(e, k):
                for j, (hi, lo) in enumerate((
                        (flat(Wgh[k]), flat(Wgl[k])), (flat(Wph[k]), flat(Wpl[k])),
                        (Woh[:, bass.ds(e, 1), :].rearrange("p a n -> p (a n)"),
                         Wol[:, bass.ds(e, 1), :].rearrange("p a n -> p (a n)")))):
                    if j == 0:
                        pool.wait_ge(s_whi_a, e + 1)
                    if j == 1:
                        pool.wait_ge(s_whi_d, e * 2 + 1)
                    if j == 2:
                        pool.wait_ge(s_whi_d, e * 2 + 2)
                    pool.tensor_tensor(lo, raw[k][:, j * 1024:(j + 1) * 1024], hi.bitcast(F32),
                                       ALU.subtract).then_inc(s_wlo, 1)

            with pool.Fori(0, EXPERTS // 2 - 1) as ep:
                for k in range(2):
                    split_lo(ep * 2 + k, k)
                    pool.wait_ge(s_wlo, (ep * 2 + k) * 3 + 3)
                    load_expert(pool, ep * 2 + k + 2, k, s_raw2)
            for k in range(2):
                split_lo(EXPERTS - 2 + k, k)
            pool.wait_ge(s_wlo, EXPERTS * 3)
            pool.wait_ge(s_posy, 1)
            last = pool.value_load(tab[0:1, 1, EXPERTS - 1:EXPERTS], min_val=1, max_val=MAXBLOCKS)
            end = end_of_all(pool)
            for k, done in ((0, last), (1, end)):
                wait_first(pool, s_yst, done * 16 + 17)
                for b in range(BLOCKS):
                    n, s = NS[b % NSUB], b % NSUB
                    pool.indirect_dma_start(
                        out=gath[k][0:n, b, :], out_offset=None, in_=Ys,
                        in_offset=bass.IndirectOffsetOnAxis(ap=posy_i[0:n, b // NSUB, k, s:s + 1], axis=0)
                    ).then_inc(s_gath[k][b // NSUB], 16)

        @block.scalar
        def _(act):
            for i in range(3):
                act.dma_start(pos[i * TOK:i * TOK + 1, :], cls_tok[0]).then_inc(s_pos, 16)
                act.dma_start(pos[i * TOK + 1:(i + 1) * TOK, :], tok_pos[0]).then_inc(s_pos, 16)
            act.dma_start(bu[:], b_u.rearrange("(a e) -> a e", a=1).broadcast_to([BM, EMB])).then_inc(s_bu, 16)
            act.wait_ge(s_dset, 1)
            for i in range(3):
                act.dma_start(pos2[i * TOK + 1:i * TOK + 2, :], tok_class[0]).then_inc(s_pos2, 16)
                act.dma_start(pos2[i * TOK + 2:(i + 1) * TOK, :],
                              tok_b.rearrange("(a e) -> a e", a=1).broadcast_to([TOK - 2, EMB])
                              ).then_inc(s_pos2, 16)
            act.wait_ge(s_wt, 32)
            act.activation(flat(Wth), raw[0][:, 0:CK * EMB], ACT.Copy).then_inc(s_wthi, 1)
            act.activation(flat(Wrh), flat(Wr), ACT.Copy).then_inc(s_wthi, 1)
            for n, (_, wh, _, src) in enumerate(WA):
                act.wait_ge(s_wa[n], 16)
                act.activation(flat(wh), src, ACT.Copy).then_inc(s_wahi, 1)
            act.sem_inc(s_mmact, PER["act"])
            act.sem_inc(s_yst, 1)
            act.sem_inc(s_hThi, 1)

            def take_hi(g, use, dst, src):
                tp_full(act, g, use)
                act.activation(dst, src, ACT.Copy).then_inc(s_tphi, 1)

            with act.Fori(0, GROUPS) as g:
                for c in range(CK):
                    tp_full(act, g, ("x", c))
                    act.activation(pT_view(pTh, c), x_view(c), ACT.Copy).then_inc(s_tphi, 1)
                for s in range(NSUB):
                    take_hi(g, ("xT", s), xTh[:, :, AT[s]:AT[s] + NS[s]], xT_view(("xT", s), s))
                act.wait_ge(s_sh, g + 1)
                act.activation(flat(ex), flat(sh), ACT.Exp).then_inc(s_rexp, 1)
                for w, dst in (("q", QT), ("k", KT)):
                    for m in range(0, HK, 2):
                        mm_full(act, g, (w, m))
                        act.activation(dst[:, m, :], mm_bank((w, m))[:, 0:GT], ACT.Copy).then_inc(s_mmact, 1)
                for n in range(0, 2 * NSUB, 2):
                    mm_full(act, g, ("v", n))
                    act.activation(v_dst(n), v_src(n), ACT.Copy).then_inc(s_mmact, 1)
                for kind, i in steps:
                    if kind == "S":
                        s, r = i // 4, i % 2
                        n = NS[s]
                        act.wait_ge(s_nm, g * NQ + i + 1)
                        if i >= 2:
                            tp_full(act, g, ("PT", i - 2))
                        for h in range(4):
                            ins = act.activation(Pr[0:n, r, h * n:(h + 1) * n],
                                                 mm_bank((kind, i))[0:n, h * n:(h + 1) * n], ACT.Exp,
                                                 bias=nmax[0:n, r, h:h + 1], scale=SCALE)
                        ins.then_inc(s_mmact, 1)
                    if kind == "OT":
                        s, half = i // 2, i % 2
                        n = NS[s]
                        if i >= 2:
                            mm_full(act, g, ("proj", s - 1))
                        take_hi(g, (kind, i), OTh[:, half * 4:half * 4 + 4, 0:n],
                                tp_bank((kind, i))[:, 0:4 * n].rearrange("p (m t) -> p m t", m=4))
                    if kind == "x2T":
                        take_hi(g, (kind, i), xTh[:, :, AT[i]:AT[i] + NS[i]], xT_view((kind, i), i))
            act.wait_ge(s_sh, GROUPS + 1)
            act.activation(flat(ex), flat(sh), ACT.Exp).then_inc(s_rexp, 1)

            def gate_hi(e, k):
                raw_there(act, e, k)
                act.activation(flat(Wgh[k]), raw[k][:, 0:1024], ACT.Copy).then_inc(s_whi_a, 1)

            gate_hi(0, 0)
            gate_hi(1, 1)
            act.wait_ge(s_tab, 1)
            act.wait_ge(s_ys0, 16)

            def rows_hi(n):
                act.wait_ge(s_bT, n + 2)
                act.activation(bTh[:], bank[2][:, 0:EMB], ACT.Copy).then_inc(s_bThi, 1)

            def store_y(n):
                act.wait_ge(s_ysb, n + 1)
                act.dma_start(Ys[bass.ds(n * P, P), :], ysb[:]).then_inc(s_yst, 16)

            def expert(e, k):
                first, end = bounds(act, e)
                with act.Fori(first, end) as j:
                    act.wait_ge(s_gs, j + 1)
                    act.activation(gact[:], gsum[:], ACT.Silu).then_inc(s_silu, 1)
                    rows_hi(j + 1)
                    act.wait_ge(s_hT, j + 1)
                    act.activation(hTh[:], bank[3][:], ACT.Copy).then_inc(s_hThi, 1)
                    store_y(j)

            rows_hi(0)
            with act.Fori(0, EXPERTS // 2 - 1) as ep:
                for k in range(2):
                    expert(ep * 2 + k, k)
                    gate_hi(ep * 2 + k + 2, k)
                    load_bias(act, ep * 2 + k + 2, k)
            for k in range(2):
                expert(EXPERTS - 2 + k, k)
            store_y(end_of_all(act))

        @block.tensor
        def _(pe):
            pe.sem_inc(s_bT, 1)
            pe.wait_ge(s_set, 15)
            pe.wait_ge(s_dset, NDSET)
            pe.wait_ge(s_wtlo, 2)

            def three(dst, a_hi, a_lo, b_hi, b_lo, first, last):
                pe.matmul(dst, a_hi, b_hi, start=first, stop=False)
                pe.matmul(dst, a_hi, b_lo, start=False, stop=False)
                return pe.matmul(dst, a_lo, b_hi, start=False, stop=last)

            def x_transposes(g, c):
                pe.wait_ge(s_xr, g * CK + c + 1)
                tp_free(pe, g, ("x", c))
                pe.sem_inc(s_carrier, 1)
                for w in range(GRID):
                    ins = pe.transpose(tp_bank(("x", c))[:, w * XP:(w + 1) * XP], Xr[:, c % 2, w, :],
                                       ident[0:XP, 0:XP])
                ins.then_inc(s_tp, 1)

            def embed(g, c):
                tp_done(pe, g, ("x", c))
                ph, pl = (t[:, c % 2].rearrange("p b t -> p (b t)") for t in (pTh, pTl))
                for s in range(NSUB):
                    if c == 0:
                        mm_free(pe, g, ("emb", s))
                    t = slice(AT[s], AT[s] + NS[s])
                    ins = three(mm_bank(("emb", s))[0:NS[s], 0:EMB], ph[:, t], pl[:, t],
                                Wth[:, c, :], Wtl[:, c, :], c == 0, c == CK - 1)
                    if c == CK - 1:
                        ins.then_inc(s_mm, 1)

            def transposes_of(g, use, src, n):
                tp_free(pe, g, use)
                for k in range(EK):
                    ins = pe.transpose(tp_bank(use)[:, k * n:(k + 1) * n], src[0:n, k * P:(k + 1) * P],
                                       ident[0:n, 0:n])
                ins.then_inc(s_tp, 1)

            def rank(g):
                use = ("rank", 0)
                dst = mm_bank(use)[0:BM, 0:NSUB * EXPERTS]
                pe.wait_ge(s_A, g + 1)
                pe.wait_ge(s_carry, g + 1)
                pe.matmul(dst, lower[0:BM, 0:BM], flat(A)[0:BM, :], start=True, stop=False)
                for s in range(NSUB):
                    pe.matmul(dst[:, s * EXPERTS:(s + 1) * EXPERTS], ones[0:BM, 0:BM], carry[0:BM, :],
                              start=False, stop=False)
                    for before_s in range(s):
                        last = pe.matmul(dst[:, s * EXPERTS:(s + 1) * EXPERTS], ones[0:BM, 0:BM],
                                         A[0:BM, before_s, :], start=False,
                                         stop=(s == NSUB - 1 and before_s == s - 1))
                return last

            def scores(g, i):
                use = ("S", i)
                s, half, par = i // 4, i % 4 // 2, i % 2
                n = NS[s]
                dst = mm_bank(use)
                mm_free(pe, g, use)
                m = mask if s < 2 else mask2
                pe.matmul(dst[0:n, 0:4 * n], identb[0:n, 0:n], m[0:n].rearrange("p h k -> p (h k)"),
                          start=True, stop=False)
                t = slice(AT[s], AT[s] + n)
                r = slice(par * HD, par * HD + HD)
                for h in range(4):
                    ins = pe.matmul(dst[0:n, h * n:(h + 1) * n], QT[r, half * 4 + h, t], KT[r, half * 4 + h, t],
                                    start=False, stop=(h == 3))
                ins.then_inc(s_mm, 1)

            def p_transposes(g, i):
                use = ("PT", i)
                s, r = i // 4, i % 2
                n = NS[s]
                mm_done(pe, g, ("S", i))
                tp_free(pe, g, use)
                for h in range(4):
                    ins = pe.transpose(tp_bank(use)[0:n, h * n:(h + 1) * n], Pr[0:n, r, h * n:(h + 1) * n],
                                       ident[0:n, 0:n])
                ins.then_inc(s_tp, 1)

            def values(g, i):
                use = ("AV", i)
                s, half, par, r = i // 4, i % 4 // 2, i % 2, i % 2
                n = NS[s]
                tp_done(pe, g, ("PT", i))
                mm_free(pe, g, use)
                for h in range(4):
                    ins = pe.matmul(mm_bank(use)[0:n, h * (HD + 1):(h + 1) * (HD + 1)],
                                    PT[0:n, r, h * n:(h + 1) * n], V[0:n, s, (half * 4 + h) * 2 + par, :],
                                    start=True, stop=True)
                ins.then_inc(s_mm, 1)

            def o_transposes(g, i):
                use = ("OT", i)
                s, half = i // 2, i % 2
                n = NS[s]
                mm_done(pe, g, ("AV", 2 * i + 1))
                tp_free(pe, g, use)
                for m in range(4):
                    ins = pe.transpose(tp_bank(use)[:, m * n:(m + 1) * n],
                                       O[0:n, half * 4 + m].rearrange("p a d -> p (a d)"), ident[0:n, 0:n])
                ins.then_inc(s_tp, 1)

            def project(g, s):
                use = ("proj", s)
                n = NS[s]
                tp_done(pe, g, ("OT", 2 * s + 1))
                mm_free(pe, g, use)
                for m in range(HK):
                    ins = three(mm_bank(use)[0:n, 0:EMB], OTh[:, m, 0:n], OTl[:, m, 0:n],
                                Wuh[:, m, :], Wul[:, m, :], m == 0, m == HK - 1)
                ins.then_inc(s_mm, 1)

            with pe.Fori(0, GROUPS) as g:
                x_transposes(g, 0)
                for c in range(CK):
                    if c + 1 < CK:
                        x_transposes(g, c + 1)
                    embed(g, c)
                for s in range(NSUB):
                    pe.wait_ge(s_xn, g * 6 + s + 1)
                    transposes_of(g, ("xT", s), xn[:, s], NS[s])
                tp_done(pe, g, ("xT", NSUB - 1))
                for n, (w, wh, wl) in enumerate((("q", Wqh, Wql), ("k", Wkh, Wkl))):
                    pe.wait_ge(s_walo, n + 1)
                    for m in range(HK):
                        mm_free(pe, g, (w, m))
                        for k in range(EK):
                            f = slice(m * P, (m + 1) * P)
                            ins = three(mm_bank((w, m))[:, 0:GT], wh[:, k, f], wl[:, k, f],
                                        xTh[:, k, :], xTl[:, k, :], k == 0, k == EK - 1)
                        ins.then_inc(s_mm, 1)
                pe.wait_ge(s_walo, 3)
                for n in range(2 * NSUB):
                    s, half = n // 2, n % 2
                    mm_free(pe, g, ("v", n))
                    for k in range(EK):
                        t, f = slice(AT[s], AT[s] + NS[s]), slice(half * 512, half * 512 + 512)
                        ins = three(mm_bank(("v", n))[0:NS[s], :], xTh[:, k, t], xTl[:, k, t],
                                    Wvh[:, k, f], Wvl[:, k, f], k == 0, k == EK - 1)
                    ins.then_inc(s_mm, 1)
                mm_free(pe, g, ("rank", 0))
                rank(g).then_inc(s_mm, 1)
                mm_done(pe, g, ("k", HK - 1))
                mm_done(pe, g, ("v", 2 * NSUB - 1))
                mm_done(pe, g, ("v", 2 * NSUB - 2))
                pe.wait_ge(s_walo, 4)
                for kind, i in steps:
                    if kind == "S":
                        scores(g, i)
                    if kind == "PT":
                        p_transposes(g, i)
                    if kind == "AV":
                        values(g, i)
                    if kind == "OT":
                        o_transposes(g, i)
                    if kind == "proj":
                        project(g, i)
                    if kind == "x2T":
                        pe.wait_ge(s_xn, g * 6 + NSUB + i + 1)
                        transposes_of(g, (kind, i), xn2[:, i], NS[i])
                    if kind == "route":
                        tp_done(pe, g, ("x2T", NSUB - 1))
                        mm_free(pe, g, (kind, i))
                        for s in range(NSUB):
                            for k in range(EK):
                                t = slice(AT[s], AT[s] + NS[s])
                                ins = three(mm_bank((kind, i))[0:NS[s], s * EXPERTS:(s + 1) * EXPERTS],
                                            xTh[:, k, t], xTl[:, k, t], Wrh[:, k, :], Wrl[:, k, :],
                                            k == 0, k == EK - 1)
                        ins.then_inc(s_mm, 1)
            rank(GROUPS).then_inc(s_mm, 1)
            pe.wait_ge(s_carry, GROUPS + 2)
            pe.matmul(bank[1][:, 0:EXPERTS], ones[0:BM, :], carry[0:BM, :], start=True, stop=True
                      ).then_inc(s_cnt, 1)

            def rows(n):
                pe.wait_ge(s_xs, n * 16 + 16)
                for k in range(EK):
                    ins = pe.transpose(bank[2][:, k * P:(k + 1) * P], xs[:, k * P:(k + 1) * P], ident[:])
                ins.then_inc(s_bT, 1)

            def outputs(n, e):
                pe.wait_ge(s_hThi, n + 1)
                pe.wait_ge(s_hTlo, n + 1)
                wh, wl = (w[:, bass.ds(e, 1), :].rearrange("p a (m n) -> p (a m) n", m=MK) for w in (Woh, Wol))
                for m in range(MK):
                    t = slice(m * P, (m + 1) * P)
                    ins = three(bank[4][:, 0:EMB], hTh[:, t], hTl[:, t], wh[:, m, :], wl[:, m, :],
                                m == 0, m == MK - 1)
                ins.then_inc(s_y, 1)

            def expert(e, k):
                first, end = bounds(pe, e)
                wait_first(pe, s_wlo, e * 3 + 3)
                with pe.Fori(first, end) as j:
                    pe.wait_ge(s_bThi, j + 1)
                    pe.wait_ge(s_bTlo, j + 1)
                    for b, (wh, wl), s in ((0, (Wgh, Wgl), s_g), (1, (Wph, Wpl), s_u)):
                        for c in range(EK):
                            t = slice(c * P, (c + 1) * P)
                            ins = three(bank[b][:, :], bTh[:, t], bTl[:, t], wh[k][:, c, :], wl[k][:, c, :],
                                        c == 0, c == EK - 1)
                        ins.then_inc(s, 1)
                    rows(j + 1)
                    outputs(j, expert_before(pe, e, first, j))
                    pe.wait_ge(s_hid, j + 1)
                    for m in range(MK):
                        t = slice(m * P, (m + 1) * P)
                        ins = pe.transpose(bank[3][:, t], hid[:, t], ident[:])
                    ins.then_inc(s_hT, 1)

            pe.wait_ge(s_tab, 1)
            rows(0)
            with pe.Fori(0, EXPERTS // 2) as ep:
                for k in range(2):
                    expert(ep * 2 + k, k)
            outputs(end_of_all(pe), EXPERTS - 1)

        @block.vector
        def _(dve):
            for n, (tile, value) in enumerate((
                    (pos2, 0.0), (zero, 0.0), (ones, 1.0), (carry, 0.0), (live, 0.0), (xn2, 0.0), (LG, 0.0),
                    (minus_half, -0.5), (mv, 0.0), (veps, 1.0), (steps128[:, 0:1], -1.0))):
                dve.memset(tile if n == 10 else tile[:], value).then_inc(s_dset, 1)
            for t in (pTh, pTl):
                dve.memset(t[:, :, :, 0:2].bitcast(F32), 0.0).then_inc(s_dset, 1)
            dve.memset(V[:, :, :, HD:HD + 1], 1.0).then_inc(s_dset, 1)
            for e in range(EXPERTS):
                dve.memset(iota[:, e:e + 1], float(e)).then_inc(s_dset, 1)
            for j in range(1, MAXNB):
                dve.memset(steps128[:, j:j + 1], float(P * j)).then_inc(s_dset, 1)
            dve.wait_ge(s_dset, NDSET - 2)
            dve.tensor_scalar(region[:], iota[:], float(REGION), None, ALU.mult).then_inc(s_dset, 1)
            dve.tensor_scalar(yshift[:], iota[:], float(-REGION), float(P), ALU.mult, ALU.add).then_inc(s_dset, 1)
            dve.sem_inc(s_tpfree, 2)
            dve.sem_inc(s_mmdve, PER["dve"])
            dve.wait_ge(s_wthi, 1)
            dve.tensor_tensor(flat(Wtl), raw[0][:, 0:CK * EMB], flat(Wth).bitcast(F32), ALU.subtract
                              ).then_inc(s_wtlo, 1)
            dve.wait_ge(s_wthi, 2)
            dve.tensor_tensor(flat(Wrl), flat(Wr), flat(Wrh).bitcast(F32), ALU.subtract).then_inc(s_wtlo, 1)
            for n, (_, wh, wl, src) in enumerate(WA):
                dve.wait_ge(s_wahi, n + 1)
                dve.tensor_tensor(flat(wl), src, flat(wh).bitcast(F32), ALU.subtract).then_inc(s_walo, 1)
            dve.wait_ge(s_pos, 96)
            dve.wait_ge(s_pos2, 96)
            dve.tensor_tensor(pos[:], pos[:], pos2[:], ALU.add).then_inc(s_posadd, 1)
            dve.wait_ge(s_posadd, 1)

            def take_lo(g, use, dst, src, hi):
                tp_full(dve, g, use)
                tp_hi(dve, g, use)
                dve.tensor_tensor(dst, src, hi.bitcast(F32), ALU.subtract).then_inc(s_tpfree, 1)

            def bc3(t, n=NSUB):
                return t.rearrange("p (s a) -> p s a", a=1).broadcast_to([P, n, EXPERTS])

            def be(t, n=NSUB):
                return t.rearrange("p (a e) -> p a e", a=1).broadcast_to([P, n, EXPERTS])

            def choose(turn):
                done = [turn * CHOOSE]

                def step(ins):
                    done[0] += 1
                    ins.then_inc(s_ro, 1)
                    wait_first(dve, s_ro, done[0])

                for s in range(NSUB):
                    step(dve.max(top[:, s, :], LG[:, s, :]))
                dve.tensor_tensor(sh[:], LG[:], bc3(top[:, :, 0]), ALU.subtract).then_inc(s_sh, 1)
                dve.wait_ge(s_rexp, turn + 1)
                step(dve.tensor_reduce(sm[:], ex[:], AX.X, ALU.add))
                step(dve.reciprocal(ri[:], sm[:]))
                step(dve.tensor_tensor(pr[:], ex[:], bc3(ri[:]), ALU.mult))
                for s in range(NSUB):
                    step(dve.max(tpr[:, s, :], pr[:, s, :]))
                    step(dve.max_index(tix[:, s, :], tpr[:, s, :], pr[:, s, :]))
                step(dve.tensor_copy(tif[:], tix[:, :, 0:2]))
                step(dve.tensor_tensor(lohi[:, 0, :], tif[:, :, 0], tif[:, :, 1], ALU.min))
                step(dve.tensor_tensor(lohi[:, 1, :], tif[:, :, 0], tif[:, :, 1], ALU.max))
                h = [hot[:, bass.ds(turn, 1), k].rearrange("p a s e -> p (a s) e") for k in range(2)]
                for k in range(2):
                    step(dve.tensor_tensor(h[k], be(iota[:]), bc3(lohi[:, k, :]), ALU.is_equal))
                step(dve.tensor_tensor(A[:], h[0], h[1], ALU.add))
                dve.sem_inc(s_A, 1)
                step(dve.tensor_tensor(sm[:], tpr[:, :, 0], tpr[:, :, 1], ALU.add))
                step(dve.tensor_scalar(sm[:], sm[:], 1e-8, None, ALU.add))
                step(dve.reciprocal(ri[:], sm[:]))
                step(dve.tensor_tensor(pw[:], pr[:], bc3(ri[:]), ALU.mult))
                for k in range(2):
                    step(dve.tensor_tensor(tmp8[:], h[k], pw[:], ALU.mult))
                    step(dve.tensor_reduce(wst[:, bass.ds(turn, 1), k].rearrange("p a s -> p (a s)"),
                                           tmp8[:], AX.X, ALU.add))

            def place(turn, src):
                done = [turn * PLACE]

                def step(ins):
                    done[0] += 1
                    ins.then_inc(s_tb, 1)
                    dve.wait_ge(s_tb, done[0])

                step(dve.tensor_tensor(rk[0:BM], src, be(region[:])[0:BM], ALU.add))
                for k in range(2):
                    h = hot[0:BM, bass.ds(turn, 1), k].rearrange("p a s e -> p (a s) e")
                    pf = posf[0:BM, bass.ds(turn, 1), k].rearrange("p a s -> p (a s)")
                    step(dve.tensor_tensor(tmp8[0:BM], h, rk[0:BM], ALU.mult))
                    step(dve.tensor_reduce(pf, tmp8[0:BM], AX.X, ALU.add))
                    wait_first(dve, s_sent, turn + 1)
                    dve.tensor_copy(pos_i[0:BM, k, :], pf).then_inc(s_pos_i, 1)
                for s in range(NSUB):
                    step(dve.scalar_tensor_tensor(out=carry[0:NS[s]], in0=A[0:NS[s], s, :],
                                                  scalar=live[0:NS[s], 0:1], in1=carry[0:NS[s]],
                                                  op0=ALU.mult, op1=ALU.add))
                dve.sem_inc(s_carry, 1)
                step(dve.memset(live[:], 1.0))

            dve.sem_inc(s_carry, 1)
            with dve.Fori(0, GROUPS) as g:
                dve.wait_ge(s_x, (g + 1) * (16 * GI))

                def reorder(c):
                    if c >= 2:
                        tp_full(dve, g, ("x", c - 2))
                    dve.tensor_copy(
                        Xr[:, c % 2].rearrange("p w (i j) -> p w i j", j=PATCH),
                        X[:, c // 2].rearrange("p (i w j) -> p w i j", w=GRID, j=PATCH)
                        [:, :, c % 2 * 8:c % 2 * 8 + 8, :]).then_inc(s_xr, 1)

                reorder(0)
                reorder(1)
                for c in range(CK):
                    if c + 2 < CK:
                        reorder(c + 2)
                    take_lo(g, ("x", c), pT_view(pTl, c), x_view(c), pT_view(pTh, c))
                for s in range(NSUB):
                    mm_full(dve, g, ("emb", s))
                    dve.tensor_tensor(H[0:NS[s], g * NSUB + s, :], mm_bank(("emb", s))[0:NS[s], 0:EMB],
                                      pos[0:NS[s], :], ALU.add).then_inc(s_mmdve, 1)
                for s in range(NSUB):
                    mm_done(dve, g, ("emb", s))
                    dve.sem_inc(s_carrier, 1)
                    dve.bn_stats(stats[0:NS[s], s, :], H[0:NS[s], g * NSUB + s, :]).then_inc(s_ln, 1)
                for s in range(NSUB):
                    wait_first(dve, s_ln, g * LN + s + 1)
                    dve.bn_aggr(mv[0:NS[s], s, :], stats[0:NS[s], s, :]).then_inc(s_ln, 1)
                dve.wait_ge(s_ln, g * LN + 6)
                dve.tensor_scalar(veps[:], mv[:, :, 1], EPS, None, ALU.add).then_inc(s_ve, 1)
                dve.wait_ge(s_rstd, g * 4 + 1)
                for s in range(NSUB):
                    dve.tensor_scalar(xn[0:NS[s], s, :], H[0:NS[s], g * NSUB + s, :], mv[0:NS[s], s, 0:1],
                                      rstd[0:NS[s], s:s + 1], ALU.subtract, ALU.mult).then_inc(s_xn, 1)
                for s in range(NSUB):
                    v = slice(AT[s], AT[s] + NS[s])
                    take_lo(g, ("xT", s), xTl[:, :, v], xT_view(("xT", s), s), xTh[:, :, v])
                choose(g)
                for w, dst in (("q", QT), ("k", KT)):
                    for m in range(1, HK, 2):
                        mm_full(dve, g, (w, m))
                        dve.tensor_copy(dst[:, m, :], mm_bank((w, m))[:, 0:GT]).then_inc(s_mmdve, 1)
                for n in range(1, 2 * NSUB, 2):
                    mm_full(dve, g, ("v", n))
                    dve.tensor_copy(v_dst(n), v_src(n)).then_inc(s_mmdve, 1)
                mm_full(dve, g, ("rank", 0))
                place(g, mm_bank(("rank", 0))[0:BM, 0:NSUB * EXPERTS].rearrange("p (s e) -> p s e", s=NSUB))
                dve.sem_inc(s_mmdve, 1)
                for kind, i in steps:
                    if kind == "S":
                        s, r = i // 4, i % 2
                        n = NS[s]
                        mm_full(dve, g, (kind, i))
                        if i >= 2:
                            mm_done(dve, g, ("S", i - 2))
                        dve.tensor_reduce(rowmax[0:n, r, :],
                                          mm_bank((kind, i))[0:n, 0:4 * n].rearrange("p (h k) -> p h k", h=4),
                                          AX.X, ALU.max).then_inc(s_rm, 1)
                        dve.wait_ge(s_rm, g * NQ + i + 1)
                        dve.tensor_scalar(nmax[0:n, r, :], rowmax[0:n, r, :], -SCALE, None, ALU.mult
                                          ).then_inc(s_nm, 1)
                    if kind == "PT":
                        s, r = i // 4, i % 2
                        n = NS[s]
                        tp_full(dve, g, (kind, i))
                        if i >= 2:
                            mm_full(dve, g, ("AV", i - 2))
                        dve.tensor_copy(PT[0:n, r, 0:4 * n], tp_bank((kind, i))[0:n, 0:4 * n]
                                        ).then_inc(s_tpfree, 1)
                    if kind == "AV":
                        s, half, par = i // 4, i % 4 // 2, i % 2
                        n = NS[s]
                        mm_full(dve, g, (kind, i))
                        ov = mm_bank((kind, i))[0:n, 0:4 * (HD + 1)].rearrange("p (h d) -> p h d", h=4)
                        if i >= 2:
                            mm_done(dve, g, ("AV", i - 2))
                        dve.reciprocal(rsum[0:n, i % 2, :], ov[:, :, HD]).then_inc(s_rs, 1)
                        dve.wait_ge(s_rs, g * NQ + i + 1)
                        if i >= 4:
                            tp_full(dve, g, ("OT", 2 * (s - 1) + half))
                        dve.tensor_tensor(O[0:n, half * 4:half * 4 + 4, par, :], ov[:, :, 0:HD],
                                          rsum[0:n, i % 2, :].rearrange("p (h a) -> p h a", a=1)
                                          .broadcast_to([n, 4, HD]), ALU.mult).then_inc(s_mmdve, 1)
                    if kind == "OT":
                        s, half = i // 2, i % 2
                        n = NS[s]
                        take_lo(g, (kind, i), OTl[:, half * 4:half * 4 + 4, 0:n],
                                tp_bank((kind, i))[:, 0:4 * n].rearrange("p (m t) -> p m t", m=4),
                                OTh[:, half * 4:half * 4 + 4, 0:n])
                    if kind == "proj":
                        n = NS[i]
                        Hb = H[0:n, g * NSUB + i, :]
                        mm_full(dve, g, (kind, i))
                        dve.wait_ge(s_hb, g * NSUB + i + 1)
                        dve.tensor_tensor(Hb, mm_bank((kind, i))[0:n, 0:EMB], Hb, ALU.add).then_inc(s_mmdve, 1)
                        mm_done(dve, g, (kind, i))
                        dve.sem_inc(s_carrier, 1)
                        dve.bn_stats(stats[0:n, i, :], Hb).then_inc(s_ln, 1)
                        wait_first(dve, s_ln, g * LN + 6 + 2 * i + 1)
                        dve.bn_aggr(mv[0:n, i, :], stats[0:n, i, :]).then_inc(s_ln, 1)
                        dve.wait_ge(s_ln, g * LN + 6 + 2 * i + 2)
                        dve.tensor_scalar(veps[:, i:i + 1], mv[:, i, 1:2], EPS, None, ALU.add).then_inc(s_ve, 1)
                        dve.wait_ge(s_rstd, g * 4 + i + 2)
                        dve.wait_ge(s_sent, g + 2)
                        dve.tensor_scalar(xn2[0:n, i, :], Hb, mv[0:n, i, 0:1], rstd[0:n, i:i + 1],
                                          ALU.subtract, ALU.mult).then_inc(s_xn, 1)
                    if kind == "x2T":
                        v = slice(AT[i], AT[i] + NS[i])
                        take_lo(g, (kind, i), xTl[:, :, v], xT_view((kind, i), i), xTh[:, :, v])
                    if kind == "route":
                        mm_full(dve, g, (kind, i))
                        for s in range(NSUB):
                            n = NS[s]
                            ins = dve.tensor_copy(LG[0:n, s, :],
                                                  mm_bank((kind, i))[0:n, s * EXPERTS:(s + 1) * EXPERTS])
                        ins.then_inc(s_mmdve, 1)
                        mm_done(dve, g, (kind, i))
            choose(GROUPS)
            dve.wait_ge(s_mm, GROUPS * MMS + 1)
            place(GROUPS, mm_bank(("rank", 0))[0:BM, 0:NSUB * EXPERTS].rearrange("p (s e) -> p s e", s=NSUB))

            done = [(GROUPS + 1) * PLACE]

            def step(ins):
                done[0] += 1
                ins.then_inc(s_tb, 1)
                dve.wait_ge(s_tb, done[0])

            dve.wait_ge(s_cnt, 1)
            step(dve.tensor_copy(cnt[:], bank[1][:, 0:EXPERTS]))
            step(dve.tensor_tensor(nbc[:], cnt[:].rearrange("p (e a) -> p e a", a=1)
                                   .broadcast_to([P, EXPERTS, MAXNB]),
                                   steps128[:].rearrange("p (a j) -> p a j", a=1)
                                   .broadcast_to([P, EXPERTS, MAXNB]), ALU.is_gt))
            step(dve.tensor_reduce(nb[:], nbc[:], AX.X, ALU.add))
            step(dve.tensor_tensor(st8[:], before[:], be(nb[:], EXPERTS), ALU.mult))
            step(dve.tensor_reduce(st[:], st8[:], AX.X, ALU.add))
            step(dve.tensor_copy(tab[:, 0, :], cnt[:]))
            step(dve.tensor_copy(tab[:, 1, :], st[:]))
            step(dve.tensor_tensor(nb[:], nb[:], st[:], ALU.add))
            dve.tensor_copy(tab[:, 2, :], nb[:]).then_inc(s_tab, 1)
            step(dve.scalar_tensor_tensor(out=sty[:], in0=st[:], scalar=float(P), in1=yshift[:],
                                          op0=ALU.mult, op1=ALU.add))
            for g in range(GROUPS):
                step(dve.tensor_tensor(ty[0:BM, g].rearrange("p k s e -> p (k s) e"),
                                       hot[0:BM, g + 1].rearrange("p k s e -> p (k s) e"),
                                       be(sty[:], 2 * NSUB)[0:BM], ALU.mult))
            step(dve.tensor_reduce(posy[0:BM].rearrange("p g k s -> p (g k s)"),
                                   ty[0:BM].rearrange("p g k s e -> p (g k s) e"), AX.X, ALU.add))
            step(dve.tensor_tensor(posy[0:BM].rearrange("p g k s -> p (g k s)"),
                                   posy[0:BM].rearrange("p g k s -> p (g k s)"),
                                   posf[0:BM, 1:].rearrange("p g k s -> p (g k s)"), ALU.add))
            dve.tensor_copy(posy_i[0:BM].rearrange("p g k s -> p (g k s)"),
                            posy[0:BM].rearrange("p g k s -> p (g k s)")).then_inc(s_posy, 1)

            def weights_hi(e, k):
                raw_there(dve, e, k)
                dve.tensor_copy(flat(Wph[k]), raw[k][:, 1024:2048]).then_inc(s_whi_d, 1)
                dve.tensor_copy(Woh[:, bass.ds(e, 1), :].rearrange("p a n -> p (a n)"),
                                raw[k][:, 2048:3072]).then_inc(s_whi_d, 1)

            def rows_lo(n):
                dve.wait_ge(s_bThi, n + 1)
                dve.tensor_tensor(bTl[:], bank[2][:, 0:EMB], bTh[:].bitcast(F32), ALU.subtract
                                  ).then_inc(s_bTlo, 1)

            def add_bo(n, e):
                dve.wait_ge(s_y, n + 1)
                dve.wait_ge(s_yst, n * 16 + 1)
                dve.tensor_tensor(ysb[:], bank[4][:, 0:EMB],
                                  bo[:, bass.ds(e, 1), :].rearrange("p a n -> p (a n)"), ALU.add
                                  ).then_inc(s_ysb, 1)

            def expert(e, k):
                first, end = bounds(dve, e)
                wait_first(dve, s_bias[k], (e + 2 - k) * 16)
                with dve.Fori(first, end) as j:
                    dve.wait_ge(s_g, j + 1)
                    dve.tensor_tensor(gsum[:], bank[0][:], bgu[k][:, 0, :], ALU.add).then_inc(s_gs, 1)
                    dve.wait_ge(s_u, j + 1)
                    dve.tensor_tensor(usum[:], bank[1][:], bgu[k][:, 1, :], ALU.add).then_inc(s_us, 1)
                    dve.wait_ge(s_us, j + 1)
                    dve.wait_ge(s_silu, j + 1)
                    dve.tensor_tensor(hid[:], gact[:], usum[:], ALU.mult).then_inc(s_hid, 1)
                    rows_lo(j + 1)
                    add_bo(j, expert_before(dve, e, first, j))
                    dve.wait_ge(s_hThi, j + 2)
                    dve.tensor_tensor(hTl[:], bank[3][:], hTh[:].bitcast(F32), ALU.subtract
                                      ).then_inc(s_hTlo, 1)

            dve.memset(hTh[:].bitcast(F32), 0.0)
            dve.memset(hTl[:].bitcast(F32), 0.0).then_inc(s_hTlo, 1)
            weights_hi(0, 0)
            weights_hi(1, 1)
            rows_lo(0)
            dve.wait_ge(s_bo, 16)
            with dve.Fori(0, EXPERTS // 2 - 1) as ep:
                for k in range(2):
                    expert(ep * 2 + k, k)
                    weights_hi(ep * 2 + k + 2, k)
            for k in range(2):
                expert(EXPERTS - 2 + k, k)
            add_bo(end_of_all(dve), EXPERTS - 1)
            for k in range(2):
                for b in range(BLOCKS):
                    n, g, s = NS[b % NSUB], b // NSUB, b % NSUB
                    dve.wait_ge(s_gath[k][g], 16 * NSUB)
                    if k:
                        dve.wait_ge(s_add, b + 1)
                    dve.scalar_tensor_tensor(out=H[0:n, b, :], in0=gath[k][0:n, b, :],
                                             scalar=wst[0:n, g + 1, k, s:s + 1], in1=H[0:n, b, :],
                                             op0=ALU.mult, op1=ALU.add).then_inc(s_add, 1)


_INS = ['x', 'cls_tok', 'L0_tok_W', 'L0_tok_b', 'L0_tok_class_token', 'L0_tok_pos_emb', 'L0_attn_w_q',
        'L0_attn_w_k', 'L0_attn_w_v', 'L0_attn_w_u', 'L0_attn_b_u', 'L0_ffn_W_router', 'L0_ffn_W_gate',
        'L0_ffn_b_gate', 'L0_ffn_W_up', 'L0_ffn_b_up', 'L0_ffn_W_out', 'L0_ffn_b_out']
_OUTS = [((IMAGES, TOK, EMB), 'float32')]


def kernel(**inputs):
    import numpy as _np
    import concourse.bacc as _bacc
    from concourse import mybir as _mybir
    from concourse.bass_utils import run_bass_kernel_spmd as _run

    nc = _bacc.Bacc("TRN2", target_bir_lowering=False, num_devices=1)
    arrays, args = {}, []
    for name in _INS:
        a = _np.ascontiguousarray(inputs[name])
        arrays[f"in_{name}_dram"] = a
        args.append(nc.dram_tensor(f"in_{name}_dram", a.shape, _mybir.dt.from_np(a.dtype), kind="ExternalInput").ap())
    for i, (shape, dtype) in enumerate(_OUTS):
        dt = _mybir.dt.from_np(_np.dtype(dtype))
        args.append(nc.dram_tensor(f"out_{i}_dram", shape, dt, kind="ExternalOutput").ap())
    vit_tower(nc, *args)
    r = _run(nc, [arrays], core_ids=[0])
    got = tuple(r.results[0][f"out_{i}_dram"] for i in range(len(_OUTS)))
    return got[0]
```

```python
from contextlib import ExitStack

import concourse.bass as bass
from concourse import mybir

F32 = mybir.dt.float32
F32R = mybir.dt.float32r
BF16 = mybir.dt.bfloat16
U32 = mybir.dt.uint32
I32 = mybir.dt.int32
ALU = mybir.AluOpType
ACT = mybir.ActivationFunctionType
AX = mybir.AxisListType

P = 128
IMAGES, CHANNELS, SIDE = 32, 3, 96
PATCH = 16
GRID = SIDE // PATCH
EMB = 256
TOK = GRID * GRID + 2
HEADS, HD = 16, 64
EXPERTS, MID = 8, 512
EPS = 1e-5

GROUPS = 4
GI = IMAGES // GROUPS
GT = GI * TOK
SUBS = (3, 3, 2)
NSUB = len(SUBS)
NS = [n * TOK for n in SUBS]
AT = [0, NS[0], NS[0] + NS[1]]
BLOCKS = GROUPS * NSUB
BM = NS[0]
EK = EMB // P
CK = CHANNELS * PATCH * PATCH // P
HK = HEADS * HD // P
MK = MID // P
NQ = NSUB * 4
XP = GI * GRID
SCALE = 1.0 / HD
NEG = -1.0e30

NDSET = 20 + (IMAGES * TOK + P - 1) // P - 1
CHOOSE, PLACE = 26, 9
TOKENS = IMAGES * TOK
REGION = (TOKENS + P - 1) // P * P + P
MAXNB = (TOKENS + P - 1) // P
MAXBLOCKS = (2 * TOKENS + EXPERTS * P) // P


def vit_tower(nc, x, cls_tok, tok_W, tok_b, tok_class, tok_pos, w_q, w_k, w_v, w_u, b_u,
              W_router, W_gate, b_gate, W_up, b_up, W_out, b_out, out):
    ctx = ExitStack()
    only_a = ExitStack()
    Xs = nc.dram_tensor("Xs", (EXPERTS * REGION, EMB), F32, kind="Internal").ap()
    Ys = nc.dram_tensor("Ys", ((MAXBLOCKS + 1) * P, EMB), F32, kind="Internal").ap()
    with ctx:
        def sb(name, shape, dt=F32, where=ctx):
            return where.enter_context(nc.sbuf_tensor(name, shape, dt))

        def sem(name):
            return ctx.enter_context(nc.semaphore(name))

        pre = ExitStack()
        pTh, pTl = (sb(n, [P, CK, GI, TOK], F32R, pre) for n in ("pTh", "pTl"))
        Xr = sb("Xr", [P, 2, GRID, P], F32, pre)
        pre.close()
        raws = sb("raws", [P, 2 * 3072])
        raw = [raws[:, i * 3072:(i + 1) * 3072] for i in range(2)]
        H = sb("H", [P, BLOCKS, EMB])
        zero = sb("zero", [P, EMB])
        ident = sb("ident", [P, P])
        lower = sb("lower", [P, P])
        ones = sb("ones", [P, P])
        iota = sb("iota", [P, EXPERTS])
        region = sb("region", [P, EXPERTS])
        yshift = sb("yshift", [P, EXPERTS])
        before = sb("before", [P, EXPERTS, EXPERTS])
        steps128 = sb("steps128", [P, MAXNB])
        carry = sb("carry", [P, EXPERTS])
        live = sb("live", [P, 1])
        xn2 = sb("xn2", [P, NSUB, EMB])
        LG = sb("LG", [P, NSUB, EXPERTS])
        sh = sb("sh", [P, NSUB, EXPERTS])
        ex = sb("ex", [P, NSUB, EXPERTS])
        pr = sb("pr", [P, NSUB, EXPERTS])
        pw = sb("pw", [P, NSUB, EXPERTS])
        tmp8 = sb("tmp8", [P, NSUB, EXPERTS])
        sm = sb("sm", [P, NSUB])
        ri = sb("ri", [P, NSUB])
        top = sb("top", [P, NSUB, 8])
        tpr = sb("tpr", [P, NSUB, 8])
        tix = sb("tix", [P, NSUB, 8], U32)
        tif = sb("tif", [P, NSUB, 2])
        lohi = sb("lohi", [P, 2, NSUB])
        A = sb("A", [P, NSUB, EXPERTS])
        rk = sb("rk", [P, NSUB, EXPERTS])
        pos_i = sb("pos_i", [P, 2, NSUB], U32)
        hot = sb("hot", [P, GROUPS + 1, 2, NSUB, EXPERTS])
        posf = sb("posf", [P, GROUPS + 1, 2, NSUB])
        wst = sb("wst", [P, GROUPS + 1, 2, NSUB])
        posy = sb("posy", [P, GROUPS, 2, NSUB])
        posy_i = sb("posy_i", [P, GROUPS, 2, NSUB], U32)
        cnt = sb("cnt", [P, EXPERTS])
        nb = sb("nb", [P, EXPERTS])
        st = sb("st", [P, EXPERTS])
        sty = sb("sty", [P, EXPERTS])
        tab = sb("tab", [P, 3, EXPERTS], I32)
        def a(name, shape, dt=F32):
            return sb(name, shape, dt, only_a)
        Wth, Wtl = (a(n, [P, CK, EMB], F32R) for n in ("Wth", "Wtl"))
        Wqh, Wql = (a(n, [P, EK, HEADS * HD], F32R) for n in ("Wqh", "Wql"))
        Wkh, Wkl = (a(n, [P, EK, HEADS * HD], F32R) for n in ("Wkh", "Wkl"))
        Wvh, Wvl = (a(n, [P, EK, HEADS * HD], F32R) for n in ("Wvh", "Wvl"))
        Wuh, Wul = (a(n, [P, HK, EMB], F32R) for n in ("Wuh", "Wul"))
        Wr = a("Wr", [P, EK, EXPERTS])
        Wrh, Wrl = (a(n, [P, EK, EXPERTS], F32R) for n in ("Wrh", "Wrl"))
        X = a("X", [XP, CHANNELS, PATCH * SIDE])
        pos = a("pos", [BM, EMB])
        bu = a("bu", [BM, EMB])
        xn = a("xn", [BM, NSUB, EMB])
        xTh, xTl = (a(n, [P, EK, GT], F32R) for n in ("xTh", "xTl"))
        stats1, stats2 = (a(n, [BM, NSUB, 6]) for n in ("stats1", "stats2"))
        mv1, mv2 = (a(n, [BM, NSUB, 2]) for n in ("mv1", "mv2"))
        veps1, veps2 = (a(n, [BM, NSUB]) for n in ("veps1", "veps2"))
        rstd1, rstd2 = (a(n, [BM, NSUB]) for n in ("rstd1", "rstd2"))
        minus_half = a("minus_half", [BM, NSUB])
        QT = a("QT", [P, HK, GT])
        KT = a("KT", [P, HK, GT])
        V = a("V", [P, NSUB, HEADS, HD + 1])
        mask = a("mask", [BM, 4, BM], BF16)
        mask2 = a("mask2", [BM, 4, NS[2]], BF16)
        identb = a("identb", [BM, BM], BF16)
        rowmax = a("rowmax", [BM, 3, 4])
        nmax = a("nmax", [BM, 3, 4])
        PP = a("PP", [P, 2, 3, 4 * BM])
        Pr = PP[:, 0]
        PT = PP[:, 1]
        rsum = a("rsum", [BM, 2, 4])
        O = a("O", [BM, HK, 2, HD])
        pos2 = O[:, 0:2].rearrange("p m a d -> p (m a d)")
        OTh, OTl = (a(n, [P, HK, BM], F32R) for n in ("OTh", "OTl"))
        x2Th, x2Tl = (a(n, [P, EK * BM], F32R) for n in ("x2Th", "x2Tl"))
        only_a.close()
        Wgh, Wgl, Wph, Wpl = ([sb(f"{n}{i}", [P, EK, MID], F32R) for i in range(2)]
                              for n in ("Wgh", "Wgl", "Wph", "Wpl"))
        bgu = [sb(f"bgu{i}", [P, 2, MID]) for i in range(2)]
        bo = sb("bo", [P, EXPERTS, EMB])
        Woh, Wol = (sb(n, [P, EXPERTS, MK * EMB], F32R) for n in ("Woh", "Wol"))
        xs = sb("xs", [P, EMB])
        bTh, bTl = (sb(n, [P, EK * P], F32R) for n in ("bTh", "bTl"))
        gsum = sb("gsum", [P, MID])
        usum = sb("usum", [P, MID])
        gact = sb("gact", [P, MID])
        hid = sb("hid", [P, MID])
        hTh, hTl = (sb(n, [P, MK * P], F32R) for n in ("hTh", "hTl"))
        ysb = sb("ysb", [P, EMB])
        ty = sb("ty", [P, GROUPS, 2, NSUB, EXPERTS])
        st8 = sb("st8", [P, EXPERTS, EXPERTS])
        nbc = sb("nbc", [P, EXPERTS, MAXNB])
        gath = [r.rearrange("p (b e) -> p b e", e=EMB) for r in raw]

        bank = [ctx.enter_context(nc.psum_tensor(f"bank{i}", [P, 512], F32)) for i in range(8)]
        mmb, tpb = bank[0:5], bank[5:8]

        s_carrier = sem("s_carrier")
        s_x = sem("s_x")
        s_xr = sem("s_xr")
        s_wt = sem("s_wt")
        s_wr = sem("s_wr")
        s_wa = [sem(f"s_wa{i}") for i in range(4)]
        s_pos = sem("s_pos")
        s_pos2 = sem("s_pos2")
        s_bu = sem("s_bu")
        s_ys0 = sem("s_ys0")
        s_raw = [sem(f"s_raw{i}") for i in range(2)]
        s_raw2 = [sem(f"s_raw2_{i}") for i in range(2)]
        s_bias = [sem(f"s_bias{i}") for i in range(2)]
        s_bo = sem("s_bo")
        s_scat = sem("s_scat")
        s_sent = sem("s_sent")
        s_tail = sem("s_tail")
        s_xs = sem("s_xs")
        s_yst = sem("s_yst")
        s_gath = [[sem(f"s_gath{k}_{g}") for g in range(GROUPS)] for k in range(2)]
        s_out = sem("s_out")
        s_set = sem("s_set")
        s_dset = sem("s_dset")
        s_wahi = sem("s_wahi")
        s_walo = sem("s_walo")
        s_wthi = sem("s_wthi")
        s_wtlo = sem("s_wtlo")
        s_ptl = sem("s_ptl")
        s_posadd = sem("s_posadd")
        s_tp = sem("s_tp")
        s_tphi = sem("s_tphi")
        s_tpact = sem("s_tpact")
        s_tpdve = sem("s_tpdve")
        s_mm = sem("s_mm")
        s_mmact = sem("s_mmact")
        s_mmdve = sem("s_mmdve")
        s_ln1 = sem("s_ln1")
        s_ve1 = sem("s_ve1")
        s_rstd1 = sem("s_rstd1")
        s_xn = sem("s_xn")
        s_hb = sem("s_hb")
        s_ln2 = sem("s_ln2")
        s_ve2 = sem("s_ve2")
        s_rstd2 = sem("s_rstd2")
        s_xn2 = sem("s_xn2")
        s_rm = sem("s_rm")
        s_nm = sem("s_nm")
        s_rs = sem("s_rs")
        s_lg = sem("s_lg")
        s_sh = sem("s_sh")
        s_rexp = sem("s_rexp")
        s_ro = sem("s_ro")
        s_A = sem("s_A")
        s_pos_i = sem("s_pos_i")
        s_carry = sem("s_carry")
        s_cnt = sem("s_cnt")
        s_tab = sem("s_tab")
        s_tb = sem("s_tb")
        s_posy = sem("s_posy")
        s_whi_a = sem("s_whi_a")
        s_whi_d = sem("s_whi_d")
        s_wlo = sem("s_wlo")
        s_bT = sem("s_bT")
        s_bThi = sem("s_bThi")
        s_bTlo = sem("s_bTlo")
        s_g = sem("s_g")
        s_u = sem("s_u")
        s_gs = sem("s_gs")
        s_us = sem("s_us")
        s_silu = sem("s_silu")
        s_hid = sem("s_hid")
        s_hT = sem("s_hT")
        s_hThi = sem("s_hThi")
        s_hTlo = sem("s_hTlo")
        s_y = sem("s_y")
        s_ysb = sem("s_ysb")
        s_add = sem("s_add")

        def turn_steps(attention, following):
            steps = []

            def add(kind, *numbers):
                part = attention if kind not in ("reorder", "x", "emb", "ln1", "xT", "qa", "ka") else following
                if part:
                    steps.extend((kind, n) for n in numbers)

            add("v", 0, 1)
            add("reorder", 0)
            for t in range(NQ + 8):
                if t < NQ:
                    add("S", t)
                if t < 2:
                    for m in (0, 1):
                        add("qb", HK // 2 + 2 * t + m)
                        add("kb", HK // 2 + 2 * t + m)
                if t in (3, 5, 6, 7):
                    add("v", {3: 2, 5: 3, 6: 4, 7: 5}[t])
                if t < 4:
                    add("choose", t)
                if t == 5:
                    add("place", 0)
                if 1 <= t < 1 + CK:
                    add("x", t - 1)
                if t % 4 == 1 and 9 <= t < NQ + 9:
                    add("ln2", (t - 9) // 4)
                if 9 <= t < 9 + NSUB:
                    add("ln1", t - 9)
                if 2 <= t < NQ + 2:
                    add("PT", t - 2)
                if 3 <= t < NQ + 3:
                    add("AV", t - 3)
                if t % 2 == 1 and 5 <= t < NQ + 5:
                    add("OT", (t - 5) // 2)
                if t % 4 == 3 and 11 <= t < NQ + 11:
                    add("route", (t - 11) // 4)
                if 10 <= t < 10 + NSUB:
                    add("xT", t - 10)
                if t % 4 == 2 and 10 <= t < NQ + 10:
                    add("x2T", (t - 10) // 4)
                if 8 <= t < 8 + NSUB:
                    add("emb", t - 8)
                if t % 4 == 0 and 8 <= t < NQ + 8:
                    add("proj", (t - 8) // 4)
                if t == 4:
                    add("rank", 0)
                if t in (6, 7):
                    add("choose", t - 2)
                if t == 7:
                    add("sent", 0)
                for use in {13: (("qa", 0),), 14: (("ka", 0), ("qa", 1)), 15: (("ka", 1),), 16: (("qa", 2),),
                            17: (("ka", 2), ("qa", 3)), 18: (("ka", 3),)}.get(t, ()):
                    add(*use)
            return steps

        def taker(use):
            return "act" if use[0] in ("S", "qa", "ka", "qb", "kb", "v", "PT") else "dve"

        class Turn:
            def __init__(self, steps, before, loops):
                self.steps, self.loops = steps, loops
                self.mm = [u for u in steps if u[0] in ("emb", "qa", "ka", "qb", "kb", "v", "rank", "S", "AV",
                                                        "proj", "route")]
                self.tp = [u for u in steps if u[0] in ("x", "xT", "PT", "OT", "x2T")]
                self.his = [u for u in self.tp if u[0] != "PT"]
                self.per = dict(mm=len(self.mm), tp=len(self.tp), hi=len(self.his))
                for e in ("act", "dve"):
                    self.per[e] = sum(taker(u) == e for u in self.mm)
                    self.per["tp" + e] = sum(taker(u) == e for u in self.tp)
                self.start = {k: before.get(k, 0) for k in self.per}

            def before(self, g, key):
                return self.start[key] + (g * self.per[key] if self.loops else 0)

            def end(self, turns=1):
                return {k: self.start[k] + turns * self.per[k] for k in self.per}

            def bank_of(self, use):
                return mmb[self.mm.index(use) % len(mmb)] if use in self.mm else tpb[self.tp.index(use) % len(tpb)]

            def taken(self, n):
                e = taker(self.mm[n])
                return e, sum(taker(u) == e for u in self.mm[:n + 1])

            def tp_taken(self, n):
                e = taker(self.tp[n])
                return "tp" + e, sum(taker(u) == e for u in self.tp[:n + 1])

        FIRST = Turn(turn_steps(False, True), {}, False)
        LOOP = Turn(turn_steps(True, True), FIRST.end(), True)
        LAST = Turn(turn_steps(True, False), LOOP.end(GROUPS - 1), False)
        END = LAST.end()
        s_taken = {"act": s_mmact, "dve": s_mmdve, "tpact": s_tpact, "tpdve": s_tpdve}

        def mm_free(pe, T, g, use):
            n = T.mm.index(use) - len(mmb)
            if n >= 0:
                e, k = T.taken(n)
                pe.wait_ge(s_taken[e], T.before(g, e) + k)
            elif n == -len(mmb) and T is not FIRST:
                for e in ("act", "dve"):
                    pe.wait_ge(s_taken[e], T.before(g, e))

        def mm_full(eng, T, g, use):
            eng.wait_ge(s_mm, T.before(g, "mm") + T.mm.index(use) + 1)

        def mm_done(eng, T, g, use):
            e, k = T.taken(T.mm.index(use))
            eng.wait_ge(s_taken[e], T.before(g, e) + k)

        def tp_free(pe, T, g, use):
            n = T.tp.index(use) - len(tpb)
            if n >= 0:
                e, k = T.tp_taken(n)
                pe.wait_ge(s_taken[e], T.before(g, e) + k)
            elif n == -len(tpb) and T is not FIRST:
                for e in ("tpact", "tpdve"):
                    if T.start[e]:
                        pe.wait_ge(s_taken[e], T.before(g, e))

        def tp_full(eng, T, g, use):
            eng.wait_ge(s_tp, T.before(g, "tp") + T.tp.index(use) + 1)

        def tp_done(eng, T, g, use):
            e, k = T.tp_taken(T.tp.index(use))
            eng.wait_ge(s_taken[e], T.before(g, e) + k)

        def tp_hi(eng, T, g, use):
            eng.wait_ge(s_tphi, T.before(g, "hi") + T.his.index(use) + 1)

        WA = [(w_q, Wqh, Wql, QT[:].rearrange("p m t -> p (m t)")[:, 0:2048]),
              (w_k, Wkh, Wkl, KT[:].rearrange("p m t -> p (m t)")[:, 0:2048]),
              (w_v, Wvh, Wvl, V[:].rearrange("p s h d -> p (s h d)")[:, 0:2048]),
              (w_u, Wuh, Wul, PP[:].rearrange("p a r t -> p (a r t)")[:, 0:2048])]
        tok_W_raw = raws[:, CK * GT:CK * GT + CK * EMB]
        XD = x.rearrange("(g b) c (h i) w -> g b h c (i w)", g=GROUPS, i=PATCH)
        outd = out.rearrange("b t e -> (b t) e")

        def wait_first(eng, s, value):
            eng.wait_ge(s, value)
            eng.sem_inc(s_carrier, 1)

        def flat(t):
            return t[:].rearrange("p k n -> p (k n)")

        def load_expert(eng, e, k, done):
            for j, (w, kk) in enumerate(((W_gate, EK), (W_up, EK), (W_out, MK))):
                eng.dma_start(raw[k][:, j * 1024:(j + 1) * 1024].rearrange("p (k n) -> p k n", k=kk),
                              w[bass.ds(e, 1)].rearrange("a (k p) n -> p (a k) n", p=P)).then_inc(done[k], 16)

        def raw_there(eng, e, k):
            if isinstance(e, int) and e < 2:
                eng.wait_ge(s_raw[k], 48)
            else:
                eng.wait_ge(s_raw2[k], (e - k) * 24)

        def load_bias(eng, e, k):
            for j, b in enumerate((b_gate, b_up)):
                eng.dma_start(bgu[k][:, j, :], b[bass.ds(e, 1)].broadcast_to([P, MID])).then_inc(s_bias[k], 16)

        def bounds(eng, e):
            first = eng.value_load(tab[0:1, 1, bass.ds(e, 1)], min_val=0, max_val=MAXBLOCKS)
            end = eng.value_load(tab[0:1, 2, bass.ds(e, 1)], min_val=1, max_val=MAXBLOCKS)
            return first, end

        def expert_before(eng, e, first, j):
            return ((e - 1 + (j > first)) * (j > 0)).with_bounds(min_val=0, max_val=EXPERTS - 1)

        def end_of_all(eng):
            return eng.value_load(tab[0:1, 2, EXPERTS - 1:EXPERTS], min_val=1, max_val=MAXBLOCKS)

        def x_view(T, c):
            return T.bank_of(("x", c))[:, 0:GRID * XP].rearrange("p (w b h) -> p b h w", w=GRID, b=GI)

        def pT_view(t, c):
            return t[:, c, :, 2:TOK].rearrange("p b (h w) -> p b h w", w=GRID)

        def xT_view(T, use):
            return T.bank_of(use)[:, 0:EK * NS[use[1]]].rearrange("p (k t) -> p k t", k=EK)

        def x2T_view(t, s):
            return t[:, 0:EK * NS[s]].rearrange("p (k t) -> p k t", k=EK)

        def v_dst(n):
            s, half = n // 2, n % 2
            return V[0:NS[s], s, half * 8:half * 8 + 8, 0:HD]

        def v_src(T, n):
            return T.bank_of(("v", n))[0:NS[n // 2], :].rearrange("p (h d) -> p h d", d=HD)

        block = ctx.enter_context(nc.Block())

        @block.sync
        def _(sp):
            def load_x(g):
                for b in range(GI):
                    sp.dma_start(X[b * GRID:(b + 1) * GRID],
                                 XD[bass.ds(g, 1), b].rearrange("a h c n -> (a h) c n")).then_inc(s_x, 16)

            load_x(0)
            sp.dma_start(tok_W_raw.rearrange("p (c e) -> p c e", c=CK),
                         tok_W.rearrange("(c p) e -> p c e", p=P)).then_inc(s_wt, 16)
            for n, (w, _, _, src) in enumerate(WA):
                sp.dma_start(src.rearrange("p (k n) -> p k n", k=w.shape[0] // P),
                             w.rearrange("(k p) n -> p k n", p=P)).then_inc(s_wa[n], 16)
            sp.wait_ge(s_dset, 2)
            sp.dma_start(Ys.rearrange("(b p) e -> p b e", p=P),
                          zero[:].rearrange("p (b e) -> p b e", b=1).broadcast_to([P, MAXBLOCKS + 1, EMB])
                          ).then_inc(s_ys0, 16)
            with sp.Fori(0, GROUPS - 1) as g:
                sp.wait_ge(s_xr, g * CK + CK)
                load_x(g + 1)
            sp.wait_ge(s_mm, LOOP.before(GROUPS - 2, "mm") + LOOP.mm.index(("emb", NSUB - 1)) + 1)
            load_expert(sp, 0, 0, s_raw)
            load_expert(sp, 1, 1, s_raw)
            sp.wait_ge(s_mm, LAST.start["mm"] + LAST.mm.index(("v", 2 * NSUB - 1)) + 1)
            for e in range(2):
                load_bias(sp, e, e)
            sp.dma_start(bo[:], b_out.rearrange("(a e) n -> a e n", a=1).broadcast_to([P, EXPERTS, EMB])
                         ).then_inc(s_bo, 16)
            sp.wait_ge(s_tab, 1)
            sp.wait_ge(s_scat, 96 * (GROUPS + 1))
            for e in range(EXPERTS):
                count = sp.value_load(tab[0:1, 0, e:e + 1], min_val=0, max_val=TOKENS)
                sp.dma_start(Xs[bass.ds(count + e * REGION, P), :], zero[:]).then_inc(s_tail, 16)
            sp.wait_ge(s_tail, 16 * EXPERTS)
            with sp.Fori(0, EXPERTS) as e:
                first, end = bounds(sp, e)
                with sp.Fori(first, end) as j:
                    row = (e * REGION + (j - first) * P).with_bounds(min_val=0, max_val=EXPERTS * REGION - P)
                    sp.wait_ge(s_bT, j + 1)
                    sp.dma_start(xs[:], Xs[bass.ds(row, P), :]).then_inc(s_xs, 16)
            sp.wait_ge(s_bT, end_of_all(sp) + 1)
            sp.dma_start(xs[:], W_out[0, 0:P, :]).then_inc(s_xs, 16)
            for b in range(BLOCKS):
                sp.wait_ge(s_add, BLOCKS + b + 1)
                n = NS[b % NSUB]
                t0 = b // NSUB * GT + AT[b % NSUB]
                sp.dma_start(outd[t0:t0 + n, :], H[0:n, b, :]).then_inc(s_out, 16)
            sp.wait_ge(s_out, 16 * BLOCKS)

        @block.gpsimd
        def _(pool):
            pool.memset(ident[:], 0.0).then_inc(s_set, 1)
            pool.memset(identb[:], 0.0).then_inc(s_set, 1)
            pool.memset(mask[:], 0.0).then_inc(s_set, 1)
            pool.memset(lower[:], 1.0).then_inc(s_set, 1)
            pool.memset(before[:], 1.0).then_inc(s_set, 1)
            pool.wait_ge(s_set, 5)
            pool.affine_select(out=ident[:], in_=ident[:], compare_op=ALU.not_equal, fill=1.0, base=0,
                               pattern=[[-1, P]], channel_multiplier=1).then_inc(s_set, 1)
            pool.affine_select(out=identb[:], in_=identb[:], compare_op=ALU.not_equal, fill=1.0, base=0,
                               pattern=[[-1, BM]], channel_multiplier=1).then_inc(s_set, 1)
            pool.affine_select(out=lower[:], in_=lower[:], compare_op=ALU.is_gt, fill=0.0, base=0,
                               pattern=[[1, P]], channel_multiplier=-1).then_inc(s_set, 1)
            pool.affine_select(out=before[:], in_=before[:], compare_op=ALU.is_gt, fill=0.0, base=0,
                               pattern=[[1, EXPERTS], [-1, EXPERTS]], channel_multiplier=0).then_inc(s_set, 1)
            m = mask[:]
            pool.affine_select(out=m, in_=m, compare_op=ALU.is_ge, fill=NEG, base=0,
                               pattern=[[0, 4], [-1, BM]], channel_multiplier=1).then_inc(s_set, 1)
            for h in range(4):
                pool.wait_ge(s_set, 10 + h)
                mh = mask[:, h, :].rearrange("p (j k) -> p j k", k=TOK)
                pool.affine_select(out=mh, in_=mh, compare_op=ALU.is_ge, fill=NEG, base=TOK - 1,
                                   pattern=[[TOK, 3], [0, TOK]], channel_multiplier=-1).then_inc(s_set, 1)
            pool.wait_ge(s_set, 14)
            pool.tensor_copy(mask2[:], mask[:, :, 0:NS[2]]).then_inc(s_set, 1)
            pool.wait_ge(s_dset, NDSET)
            pool.wait_ge(s_bu, 16)
            pool.sem_inc(s_sent, 1)

            def scatter(turn):
                wait_first(pool, s_pos_i, 2 * turn + 2)
                for k in range(2):
                    for s in range(NSUB):
                        pool.indirect_dma_start(
                            out=Xs, out_offset=bass.IndirectOffsetOnAxis(ap=pos_i[0:NS[s], k, s:s + 1], axis=0),
                            in_=xn2[0:NS[s], s, :], in_offset=None).then_inc(s_scat, 16)

            def sent(turn):
                pool.wait_ge(s_scat, 96 * turn + 96)
                pool.sem_inc(s_sent, 1)

            def turn(T, g):
                for kind, i in T.steps:
                    if kind == "emb":
                        pool.wait_ge(s_ve1, (g + 1) * NSUB + i + 1)
                        pool.tensor_tensor(rstd1[0:NS[i], i:i + 1], veps1[0:NS[i], i:i + 1], minus_half[0:NS[i], i:i + 1],
                                           ALU.pow).then_inc(s_rstd1, 1)
                    if kind == "ln1":
                        pool.wait_ge(s_xn, (g + 1) * NSUB + i + 1)
                        hb = H[0:NS[i], (g + 1) * NSUB + i, :]
                        pool.tensor_tensor(hb, hb, bu[0:NS[i], :], ALU.add).then_inc(s_hb, 1)
                    if kind == "place":
                        scatter(g)
                    if kind == "sent":
                        sent(g)
                    if kind == "proj":
                        pool.wait_ge(s_ve2, g * NSUB + i + 1)
                        pool.tensor_tensor(rstd2[0:NS[i], i:i + 1], veps2[0:NS[i], i:i + 1], minus_half[0:NS[i], i:i + 1],
                                           ALU.pow).then_inc(s_rstd2, 1)

            turn(FIRST, -1)
            with pool.Fori(0, GROUPS - 1) as g:
                turn(LOOP, g)
            turn(LAST, GROUPS - 1)
            scatter(GROUPS)

            def split_lo(e, k):
                for j, (hi, lo) in enumerate((
                        (flat(Wgh[k]), flat(Wgl[k])), (flat(Wph[k]), flat(Wpl[k])),
                        (Woh[:, bass.ds(e, 1), :].rearrange("p a n -> p (a n)"),
                         Wol[:, bass.ds(e, 1), :].rearrange("p a n -> p (a n)")))):
                    if j == 0:
                        pool.wait_ge(s_whi_a, e + 1)
                    if j == 1:
                        pool.wait_ge(s_whi_d, e * 2 + 1)
                    if j == 2:
                        pool.wait_ge(s_whi_d, e * 2 + 2)
                    pool.tensor_tensor(lo, raw[k][:, j * 1024:(j + 1) * 1024], hi.bitcast(F32),
                                       ALU.subtract).then_inc(s_wlo, 1)

            with pool.Fori(0, EXPERTS // 2 - 1) as ep:
                for k in range(2):
                    split_lo(ep * 2 + k, k)
                    pool.wait_ge(s_wlo, (ep * 2 + k) * 3 + 3)
                    load_expert(pool, ep * 2 + k + 2, k, s_raw2)
            for k in range(2):
                split_lo(EXPERTS - 2 + k, k)
            pool.wait_ge(s_wlo, EXPERTS * 3)
            pool.wait_ge(s_posy, 1)
            last = pool.value_load(tab[0:1, 1, EXPERTS - 1:EXPERTS], min_val=1, max_val=MAXBLOCKS)
            end = end_of_all(pool)
            for k, done in ((0, last), (1, end)):
                wait_first(pool, s_yst, done * 16 + 17)
                for b in range(BLOCKS):
                    n, s = NS[b % NSUB], b % NSUB
                    pool.indirect_dma_start(
                        out=gath[k][0:n, b, :], out_offset=None, in_=Ys,
                        in_offset=bass.IndirectOffsetOnAxis(ap=posy_i[0:n, b // NSUB, k, s:s + 1], axis=0)
                    ).then_inc(s_gath[k][b // NSUB], 16)

        @block.scalar
        def _(act):
            for i in range(3):
                act.dma_start(pos[i * TOK:i * TOK + 1, :], cls_tok[0]).then_inc(s_pos, 16)
                act.dma_start(pos[i * TOK + 1:(i + 1) * TOK, :], tok_pos[0]).then_inc(s_pos, 16)
            act.dma_start(bu[:], b_u.rearrange("(a e) -> a e", a=1).broadcast_to([BM, EMB])).then_inc(s_bu, 16)
            act.wait_ge(s_dset, 1)
            for i in range(3):
                act.dma_start(pos2[i * TOK + 1:i * TOK + 2, :], tok_class[0]).then_inc(s_pos2, 16)
                act.dma_start(pos2[i * TOK + 2:(i + 1) * TOK, :],
                              tok_b.rearrange("(a e) -> a e", a=1).broadcast_to([TOK - 2, EMB])
                              ).then_inc(s_pos2, 16)
            def weights_hi(n):
                _, wh, _, src = WA[n]
                act.wait_ge(s_wa[n], 16)
                act.activation(flat(wh), src, ACT.Copy).then_inc(s_wahi, 1)

            act.dma_start(Wr[:], W_router.rearrange("(k p) e -> p k e", p=P)).then_inc(s_wr, 16)
            act.wait_ge(s_wt, 16)
            act.activation(flat(Wth), tok_W_raw, ACT.Copy).then_inc(s_wthi, 1)

            def reorder(c):
                act.activation(
                    Xr[0:XP, c % 2, :, :].rearrange("p w (i j) -> p w i j", j=PATCH),
                    X[:, c // 2].rearrange("p (i w j) -> p w i j", w=GRID, j=PATCH)
                    [:, :, c % 2 * 8:c % 2 * 8 + 8, :], ACT.Copy).then_inc(s_xr, 1)

            def take_hi(T, g, use, dst, src):
                tp_full(act, T, g, use)
                act.activation(dst, src, ACT.Copy).then_inc(s_tphi, 1)

            def turn(T, g):
                for kind, i in T.steps:
                    use = (kind, i)
                    if kind == "reorder":
                        act.wait_ge(s_x, (g + 2) * (16 * GI))
                        reorder(0)
                        reorder(1)
                    if kind == "x":
                        take_hi(T, g, use, pT_view(pTh, i), x_view(T, i))
                        if i + 2 < CK:
                            reorder(i + 2)
                    if T is FIRST and kind == "x" and i == CK - 1:
                        weights_hi(0)
                        weights_hi(1)
                    if kind == "xT":
                        take_hi(T, g, use, xTh[:, :, AT[i]:AT[i] + NS[i]], xT_view(T, use))
                    if kind in ("qa", "qb", "ka", "kb"):
                        mm_full(act, T, g, use)
                        act.activation((QT if kind[0] == "q" else KT)[:, i, :], T.bank_of(use)[:, 0:GT], ACT.Copy
                                       ).then_inc(s_mmact, 1)
                    if kind == "v":
                        mm_full(act, T, g, use)
                        act.activation(v_dst(i), v_src(T, i), ACT.Copy).then_inc(s_mmact, 1)
                    if kind == "choose" and i == 1:
                        act.wait_ge(s_sh, g + 1)
                        act.activation(flat(ex), flat(sh), ACT.Exp).then_inc(s_rexp, 1)
                    if kind == "S":
                        s, r = i // 4, i % 3
                        n = NS[s]
                        act.wait_ge(s_nm, g * NQ + i + 1)
                        if i >= 3:
                            tp_full(act, T, g, ("PT", i - 3))
                        for h in range(4):
                            ins = act.activation(Pr[0:n, r, h * n:(h + 1) * n],
                                                 T.bank_of(use)[0:n, h * n:(h + 1) * n], ACT.Exp,
                                                 bias=nmax[0:n, r, h:h + 1], scale=SCALE)
                        ins.then_inc(s_mmact, 1)
                    if kind == "PT":
                        s, r = i // 4, i % 3
                        n = NS[s]
                        tp_full(act, T, g, use)
                        if i >= 3:
                            mm_full(act, T, g, ("AV", i - 3))
                        act.activation(PT[0:n, r, 0:4 * n], T.bank_of(use)[0:n, 0:4 * n], ACT.Copy
                                       ).then_inc(s_tpact, 1)
                    if kind == "OT":
                        s, half = i // 2, i % 2
                        n = NS[s]
                        if i >= 2:
                            mm_full(act, T, g, ("proj", s - 1))
                        take_hi(T, g, use, OTh[:, half * 4:half * 4 + 4, 0:n],
                                T.bank_of(use)[:, 0:4 * n].rearrange("p (m t) -> p m t", m=4))
                    if kind == "x2T":
                        if i >= 1:
                            mm_full(act, T, g, ("route", i - 1))
                        take_hi(T, g, use, x2T_view(x2Th, i), xT_view(T, use))

            turn(FIRST, -1)
            weights_hi(2)
            weights_hi(3)
            act.wait_ge(s_wr, 16)
            act.activation(flat(Wrh), flat(Wr), ACT.Copy).then_inc(s_wthi, 1)
            act.wait_ge(s_walo, 4)
            with act.Fori(0, GROUPS - 1) as g:
                turn(LOOP, g)
            turn(LAST, GROUPS - 1)
            act.wait_ge(s_sh, GROUPS + 1)
            act.activation(flat(ex), flat(sh), ACT.Exp).then_inc(s_rexp, 1)
            act.sem_inc(s_yst, 1)
            act.sem_inc(s_hThi, 1)

            def gate_hi(e, k):
                raw_there(act, e, k)
                act.activation(flat(Wgh[k]), raw[k][:, 0:1024], ACT.Copy).then_inc(s_whi_a, 1)

            gate_hi(0, 0)
            gate_hi(1, 1)
            act.wait_ge(s_tab, 1)
            act.wait_ge(s_ys0, 16)

            def rows_hi(n):
                act.wait_ge(s_bT, n + 2)
                act.activation(bTh[:], bank[2][:, 0:EMB], ACT.Copy).then_inc(s_bThi, 1)

            def store_y(n):
                act.wait_ge(s_ysb, n + 1)
                act.dma_start(Ys[bass.ds(n * P, P), :], ysb[:]).then_inc(s_yst, 16)

            def expert(e, k):
                first, end = bounds(act, e)
                with act.Fori(first, end) as j:
                    act.wait_ge(s_gs, j + 1)
                    act.activation(gact[:], gsum[:], ACT.Silu).then_inc(s_silu, 1)
                    rows_hi(j + 1)
                    act.wait_ge(s_hT, j + 1)
                    act.activation(hTh[:], bank[3][:], ACT.Copy).then_inc(s_hThi, 1)
                    store_y(j)

            rows_hi(0)
            with act.Fori(0, EXPERTS // 2 - 1) as ep:
                for k in range(2):
                    expert(ep * 2 + k, k)
                    gate_hi(ep * 2 + k + 2, k)
                    load_bias(act, ep * 2 + k + 2, k)
            for k in range(2):
                expert(EXPERTS - 2 + k, k)
            store_y(end_of_all(act))

        @block.tensor
        def _(pe):
            pe.sem_inc(s_bT, 1)
            pe.wait_ge(s_set, 15)
            pe.wait_ge(s_dset, NDSET)

            def three(dst, a_hi, a_lo, b_hi, b_lo, first, last):
                pe.matmul(dst, a_hi, b_hi, start=first, stop=False)
                pe.matmul(dst, a_hi, b_lo, start=False, stop=False)
                return pe.matmul(dst, a_lo, b_hi, start=False, stop=last)

            def x_transposes(T, g, c):
                pe.wait_ge(s_xr, (g + 1) * CK + c + 1)
                tp_free(pe, T, g, ("x", c))
                pe.sem_inc(s_carrier, 1)
                for w in range(GRID):
                    ins = pe.transpose(T.bank_of(("x", c))[:, w * XP:(w + 1) * XP], Xr[0:XP, c % 2, w, :],
                                       ident[0:XP, 0:XP])
                ins.then_inc(s_tp, 1)

            def embed(T, g, s):
                use = ("emb", s)
                tp_done(pe, T, g, ("x", CK - 1))
                if T is FIRST and s == 0:
                    pe.wait_ge(s_wtlo, 1)
                mm_free(pe, T, g, use)
                for c in range(CK):
                    t = slice(AT[s], AT[s] + NS[s])
                    ph, pl = (t_[:, c].rearrange("p b t -> p (b t)") for t_ in (pTh, pTl))
                    ins = three(T.bank_of(use)[0:NS[s], 0:EMB], ph[:, t], pl[:, t],
                                Wth[:, c, :], Wtl[:, c, :], c == 0, c == CK - 1)
                ins.then_inc(s_mm, 1)

            def transposes_of(T, g, use, src, n):
                tp_free(pe, T, g, use)
                for k in range(EK):
                    ins = pe.transpose(T.bank_of(use)[:, k * n:(k + 1) * n], src[0:n, k * P:(k + 1) * P],
                                       ident[0:n, 0:n])
                ins.then_inc(s_tp, 1)

            def rank(g, bank_):
                dst = bank_[0:BM, 0:NSUB * EXPERTS]
                pe.wait_ge(s_A, g + 1)
                pe.wait_ge(s_carry, g + 1)
                pe.matmul(dst, lower[0:BM, 0:BM], flat(A)[0:BM, :], start=True, stop=False)
                pe.matmul(dst.rearrange("p (s e) -> p s e", e=EXPERTS), ones[0:BM, 0:BM],
                          carry[0:BM].rearrange("p (a e) -> p a e", a=1).broadcast_to([BM, NSUB, EXPERTS]),
                          start=False, stop=False)
                for back in range(1, NSUB):
                    last = pe.matmul(dst[:, back * EXPERTS:], ones[0:BM, 0:BM],
                                     flat(A)[0:BM, 0:(NSUB - back) * EXPERTS], start=False,
                                     stop=(back == NSUB - 1))
                return last

            def q_or_k(T, g, use):
                kind, m = use
                wh, wl = (Wqh, Wql) if kind[0] == "q" else (Wkh, Wkl)
                mm_free(pe, T, g, use)
                for k in range(EK):
                    f = slice(m * P, (m + 1) * P)
                    ins = three(T.bank_of(use)[:, 0:GT], wh[:, k, f], wl[:, k, f],
                                xTh[:, k, :], xTl[:, k, :], k == 0, k == EK - 1)
                ins.then_inc(s_mm, 1)

            def token_values(T, g, n):
                use = ("v", n)
                s, half = n // 2, n % 2
                mm_free(pe, T, g, use)
                for k in range(EK):
                    t, f = slice(AT[s], AT[s] + NS[s]), slice(half * 512, half * 512 + 512)
                    ins = three(T.bank_of(use)[0:NS[s], :], xTh[:, k, t], xTl[:, k, t],
                                Wvh[:, k, f], Wvl[:, k, f], k == 0, k == EK - 1)
                ins.then_inc(s_mm, 1)

            def scores(T, g, i):
                use = ("S", i)
                s, half, par = i // 4, i % 4 // 2, i % 2
                n = NS[s]
                dst = T.bank_of(use)
                if i == 0:
                    mm_done(pe, T, g, T.mm[1])
                if i == 2:
                    mm_done(pe, T, g, ("kb", HK - 1))
                mm_free(pe, T, g, use)
                m = mask if s < 2 else mask2
                pe.matmul(dst[0:n, 0:4 * n], identb[0:n, 0:n], m[0:n].rearrange("p h k -> p (h k)"),
                          start=True, stop=False)
                t = slice(AT[s], AT[s] + n)
                r = slice(par * HD, par * HD + HD)
                for h in range(4):
                    ins = pe.matmul(dst[0:n, h * n:(h + 1) * n], QT[r, half * 4 + h, t], KT[r, half * 4 + h, t],
                                    start=False, stop=(h == 3))
                ins.then_inc(s_mm, 1)

            def p_transposes(T, g, i):
                use = ("PT", i)
                s, r = i // 4, i % 3
                n = NS[s]
                mm_done(pe, T, g, ("S", i))
                tp_free(pe, T, g, use)
                for h in range(4):
                    ins = pe.transpose(T.bank_of(use)[0:n, h * n:(h + 1) * n], Pr[0:n, r, h * n:(h + 1) * n],
                                       ident[0:n, 0:n])
                ins.then_inc(s_tp, 1)

            def values(T, g, i):
                use = ("AV", i)
                s, half, par, r = i // 4, i % 4 // 2, i % 2, i % 3
                n = NS[s]
                if i % 4 == 0:
                    mm_done(pe, T, g, ("v", 2 * s + 1))
                tp_done(pe, T, g, ("PT", i))
                mm_free(pe, T, g, use)
                for h in range(4):
                    ins = pe.matmul(T.bank_of(use)[0:n, h * (HD + 1):(h + 1) * (HD + 1)],
                                    PT[0:n, r, h * n:(h + 1) * n], V[0:n, s, (half * 4 + h) * 2 + par, :],
                                    start=True, stop=True)
                ins.then_inc(s_mm, 1)

            def o_transposes(T, g, i):
                use = ("OT", i)
                s, half = i // 2, i % 2
                n = NS[s]
                mm_done(pe, T, g, ("AV", 2 * i + 1))
                tp_free(pe, T, g, use)
                for m in range(4):
                    ins = pe.transpose(T.bank_of(use)[:, m * n:(m + 1) * n],
                                       O[0:n, half * 4 + m].rearrange("p a d -> p (a d)"), ident[0:n, 0:n])
                ins.then_inc(s_tp, 1)

            def project(T, g, s):
                use = ("proj", s)
                n = NS[s]
                tp_done(pe, T, g, ("OT", 2 * s + 1))
                mm_free(pe, T, g, use)
                for m in range(HK):
                    ins = three(T.bank_of(use)[0:n, 0:EMB], OTh[:, m, 0:n], OTl[:, m, 0:n],
                                Wuh[:, m, :], Wul[:, m, :], m == 0, m == HK - 1)
                ins.then_inc(s_mm, 1)

            def turn(T, g):
                for kind, i in T.steps:
                    use = (kind, i)
                    if kind == "x":
                        x_transposes(T, g, i)
                    if kind == "emb":
                        embed(T, g, i)
                    if kind == "xT":
                        pe.wait_ge(s_xn, (g + 1) * NSUB + i + 1)
                        transposes_of(T, g, use, xn[:, i], NS[i])
                    if kind in ("qa", "ka", "qb", "kb"):
                        if kind == "qa" and i == 0:
                            tp_done(pe, T, g, ("xT", NSUB - 1))
                        if T is FIRST and kind in ("qa", "ka") and i == 0:
                            pe.wait_ge(s_walo, 1 if kind == "qa" else 2)
                        q_or_k(T, g, use)
                    if kind == "v":
                        token_values(T, g, i)
                    if kind == "rank":
                        mm_free(pe, T, g, use)
                        rank(g, T.bank_of(use)).then_inc(s_mm, 1)
                    if kind == "S":
                        scores(T, g, i)
                    if kind == "PT":
                        p_transposes(T, g, i)
                    if kind == "AV":
                        values(T, g, i)
                    if kind == "OT":
                        o_transposes(T, g, i)
                    if kind == "proj":
                        project(T, g, i)
                    if kind == "x2T":
                        pe.wait_ge(s_xn2, g * NSUB + i + 1)
                        transposes_of(T, g, use, xn2[:, i], NS[i])
                    if kind == "route":
                        tp_done(pe, T, g, ("x2T", i))
                        mm_free(pe, T, g, use)
                        n = NS[i]
                        for k in range(EK):
                            t = slice(k * n, (k + 1) * n)
                            ins = three(T.bank_of(use)[0:n, 0:EXPERTS], x2Th[:, t], x2Tl[:, t],
                                        Wrh[:, k, :], Wrl[:, k, :], k == 0, k == EK - 1)
                        ins.then_inc(s_mm, 1)

            turn(FIRST, -1)
            pe.wait_ge(s_walo, 4)
            pe.wait_ge(s_wtlo, 2)
            with pe.Fori(0, GROUPS - 1) as g:
                turn(LOOP, g)
            turn(LAST, GROUPS - 1)
            pe.wait_ge(s_mmdve, END["dve"])
            rank(GROUPS, bank[0]).then_inc(s_mm, 1)
            pe.wait_ge(s_carry, GROUPS + 2)
            pe.matmul(bank[1][:, 0:EXPERTS], ones[0:BM, :], carry[0:BM, :], start=True, stop=True
                      ).then_inc(s_cnt, 1)

            def rows(n):
                pe.wait_ge(s_xs, n * 16 + 16)
                for k in range(EK):
                    ins = pe.transpose(bank[2][:, k * P:(k + 1) * P], xs[:, k * P:(k + 1) * P], ident[:])
                ins.then_inc(s_bT, 1)

            def outputs(n, e):
                pe.wait_ge(s_hThi, n + 1)
                pe.wait_ge(s_hTlo, n + 1)
                wh, wl = (w[:, bass.ds(e, 1), :].rearrange("p a (m n) -> p (a m) n", m=MK) for w in (Woh, Wol))
                for m in range(MK):
                    t = slice(m * P, (m + 1) * P)
                    ins = three(bank[4][:, 0:EMB], hTh[:, t], hTl[:, t], wh[:, m, :], wl[:, m, :],
                                m == 0, m == MK - 1)
                ins.then_inc(s_y, 1)

            def expert(e, k):
                first, end = bounds(pe, e)
                wait_first(pe, s_wlo, e * 3 + 3)
                with pe.Fori(first, end) as j:
                    pe.wait_ge(s_bThi, j + 1)
                    pe.wait_ge(s_bTlo, j + 1)
                    for b, (wh, wl), s in ((0, (Wgh, Wgl), s_g), (1, (Wph, Wpl), s_u)):
                        for c in range(EK):
                            t = slice(c * P, (c + 1) * P)
                            ins = three(bank[b][:, :], bTh[:, t], bTl[:, t], wh[k][:, c, :], wl[k][:, c, :],
                                        c == 0, c == EK - 1)
                        ins.then_inc(s, 1)
                    rows(j + 1)
                    outputs(j, expert_before(pe, e, first, j))
                    pe.wait_ge(s_hid, j + 1)
                    for m in range(MK):
                        t = slice(m * P, (m + 1) * P)
                        ins = pe.transpose(bank[3][:, t], hid[:, t], ident[:])
                    ins.then_inc(s_hT, 1)

            pe.wait_ge(s_tab, 1)
            rows(0)
            with pe.Fori(0, EXPERTS // 2) as ep:
                for k in range(2):
                    expert(ep * 2 + k, k)
            outputs(end_of_all(pe), EXPERTS - 1)

        @block.vector
        def _(dve):
            for n, (tile, value) in enumerate((
                    (pos2, 0.0), (zero, 0.0), (ones, 1.0), (carry, 0.0), (live, 0.0), (xn2, 0.0), (LG, 0.0),
                    (minus_half, -0.5), (steps128[:, 0:1], -1.0))):
                dve.memset(tile if n in (0, 8) else tile[:], value).then_inc(s_dset, 1)
            dve.memset(pTh[:, :, :, 0:2].bitcast(F32), 0.0).then_inc(s_dset, 1)
            for e in range(EXPERTS):
                dve.memset(iota[:, e:e + 1], float(e)).then_inc(s_dset, 1)
            for j in range(1, MAXNB):
                dve.memset(steps128[:, j:j + 1], float(P * j)).then_inc(s_dset, 1)
            dve.wait_ge(s_dset, NDSET - 2)
            dve.tensor_scalar(region[:], iota[:], float(REGION), None, ALU.mult).then_inc(s_dset, 1)
            dve.tensor_scalar(yshift[:], iota[:], float(-REGION), float(P), ALU.mult, ALU.add).then_inc(s_dset, 1)
            dve.wait_ge(s_wthi, 1)
            dve.tensor_tensor(flat(Wtl), tok_W_raw, flat(Wth).bitcast(F32), ALU.subtract).then_inc(s_wtlo, 1)
            dve.wait_ge(s_wtlo, 1)
            dve.memset(pTl[:, :, :, 0:2].bitcast(F32), 0.0).then_inc(s_ptl, 1)
            dve.wait_ge(s_pos, 96)
            dve.wait_ge(s_pos2, 96)
            dve.tensor_tensor(pos[:], pos[:], pos2, ALU.add).then_inc(s_posadd, 1)
            dve.wait_ge(s_posadd, 1)

            def weights_lo(n):
                _, wh, wl, src = WA[n]
                dve.wait_ge(s_wahi, n + 1)
                dve.tensor_tensor(flat(wl), src, flat(wh).bitcast(F32), ALU.subtract).then_inc(s_walo, 1)

            def take_lo(T, g, use, dst, src, hi):
                tp_full(dve, T, g, use)
                tp_hi(dve, T, g, use)
                dve.tensor_tensor(dst, src, hi.bitcast(F32), ALU.subtract).then_inc(s_tpdve, 1)

            def bc3(t, n=NSUB):
                return t.rearrange("p (s a) -> p s a", a=1).broadcast_to([P, n, EXPERTS])

            def be(t, n=NSUB):
                return t.rearrange("p (a e) -> p a e", a=1).broadcast_to([P, n, EXPERTS])

            CHOSEN = (0, 3, 6, 12, 18, 22, CHOOSE)

            def choose(turn, part):
                done = [turn * CHOOSE + CHOSEN[part]]

                def step(ins, wait=True):
                    done[0] += 1
                    ins.then_inc(s_ro, 1)
                    if wait:
                        wait_first(dve, s_ro, done[0])

                h = [hot[:, bass.ds(turn, 1), k].rearrange("p a s e -> p (a s) e") for k in range(2)]
                if part == 0:
                    for s in range(NSUB):
                        step(dve.max(top[:, s, :], LG[:, s, :]), s == NSUB - 1)
                    dve.tensor_tensor(sh[:], LG[:], bc3(top[:, :, 0]), ALU.subtract).then_inc(s_sh, 1)
                if part == 1:
                    dve.wait_ge(s_rexp, turn + 1)
                    step(dve.tensor_reduce(sm[:], ex[:], AX.X, ALU.add))
                    step(dve.reciprocal(ri[:], sm[:]))
                    step(dve.tensor_tensor(pr[:], ex[:], bc3(ri[:]), ALU.mult))
                if part == 2:
                    for s in range(NSUB):
                        step(dve.max(tpr[:, s, :], pr[:, s, :]), s == NSUB - 1)
                    for s in range(NSUB):
                        step(dve.max_index(tix[:, s, :], tpr[:, s, :], pr[:, s, :]), s == NSUB - 1)
                if part == 3:
                    step(dve.tensor_copy(tif[:], tix[:, :, 0:2]))
                    step(dve.tensor_tensor(lohi[:, 0, :], tif[:, :, 0], tif[:, :, 1], ALU.min), False)
                    step(dve.tensor_tensor(lohi[:, 1, :], tif[:, :, 0], tif[:, :, 1], ALU.max))
                    for k in range(2):
                        step(dve.tensor_tensor(h[k], be(iota[:]), bc3(lohi[:, k, :]), ALU.is_equal), k == 1)
                    step(dve.tensor_tensor(A[:], h[0], h[1], ALU.add))
                    dve.sem_inc(s_A, 1)
                if part == 4:
                    step(dve.tensor_tensor(sm[:], tpr[:, :, 0], tpr[:, :, 1], ALU.add))
                    step(dve.tensor_scalar(sm[:], sm[:], 1e-8, None, ALU.add))
                    step(dve.reciprocal(ri[:], sm[:]))
                    step(dve.tensor_tensor(pw[:], pr[:], bc3(ri[:]), ALU.mult))
                if part == 5:
                    for k in range(2):
                        step(dve.tensor_tensor(tmp8[:], h[k], pw[:], ALU.mult))
                        step(dve.tensor_reduce(wst[:, bass.ds(turn, 1), k].rearrange("p a s -> p (a s)"),
                                               tmp8[:], AX.X, ALU.add))
                assert done[0] == turn * CHOOSE + CHOSEN[part + 1] if isinstance(turn, int) else True

            def place(turn, src):
                done = [turn * PLACE]

                def step(ins):
                    done[0] += 1
                    ins.then_inc(s_tb, 1)
                    dve.wait_ge(s_tb, done[0])

                step(dve.tensor_tensor(rk[0:BM], src, be(region[:])[0:BM], ALU.add))
                for k in range(2):
                    h = hot[0:BM, bass.ds(turn, 1), k].rearrange("p a s e -> p (a s) e")
                    pf = posf[0:BM, bass.ds(turn, 1), k].rearrange("p a s -> p (a s)")
                    step(dve.tensor_tensor(tmp8[0:BM], h, rk[0:BM], ALU.mult))
                    step(dve.tensor_reduce(pf, tmp8[0:BM], AX.X, ALU.add))
                    wait_first(dve, s_sent, turn + 1)
                    dve.tensor_copy(pos_i[0:BM, k, :], pf).then_inc(s_pos_i, 1)
                for s in range(NSUB):
                    step(dve.scalar_tensor_tensor(out=carry[0:NS[s]], in0=A[0:NS[s], s, :],
                                                  scalar=live[0:NS[s], 0:1], in1=carry[0:NS[s]],
                                                  op0=ALU.mult, op1=ALU.add))
                dve.sem_inc(s_carry, 1)
                step(dve.memset(live[:], 1.0))

            def layer_norm(Hb, s, n, stats, mv, veps, s_ln, s_ve, count):
                dve.bn_stats(stats[0:n, s, :], Hb).then_inc(s_ln, 1)
                wait_first(dve, s_ln, count * 2 + 1)
                dve.bn_aggr(mv[0:n, s, :], stats[0:n, s, :]).then_inc(s_ln, 1)
                dve.wait_ge(s_ln, count * 2 + 2)
                dve.tensor_scalar(veps[0:n, s:s + 1], mv[0:n, s, 1:2], EPS, None, ALU.add).then_inc(s_ve, 1)

            def turn(T, g):
                for kind, i in T.steps:
                    use = (kind, i)
                    if kind == "choose":
                        choose(g, i)
                    if kind == "place":
                        mm_full(dve, T, g, ("rank", 0))
                        place(g, T.bank_of(("rank", 0))[0:BM, 0:NSUB * EXPERTS].rearrange("p (s e) -> p s e", s=NSUB))
                        dve.sem_inc(s_mmdve, 1)
                    if kind == "x":
                        take_lo(T, g, use, pT_view(pTl, i), x_view(T, i), pT_view(pTh, i))
                    if T is FIRST and kind == "x" and i == CK - 1:
                        weights_lo(0)
                    if kind == "emb":
                        n = NS[i]
                        Hb = H[0:n, (g + 1) * NSUB + i, :]
                        mm_full(dve, T, g, use)
                        dve.tensor_tensor(Hb, T.bank_of(use)[0:n, 0:EMB], pos[0:n, :], ALU.add).then_inc(s_mmdve, 1)
                        mm_done(dve, T, g, use)
                        dve.sem_inc(s_carrier, 1)
                        layer_norm(Hb, i, n, stats1, mv1, veps1, s_ln1, s_ve1, (g + 1) * NSUB + i)
                    if kind == "ln1":
                        n = NS[i]
                        dve.wait_ge(s_rstd1, (g + 1) * NSUB + i + 1)
                        dve.tensor_scalar(xn[0:n, i, :], H[0:n, (g + 1) * NSUB + i, :], mv1[0:n, i, 0:1],
                                          rstd1[0:n, i:i + 1], ALU.subtract, ALU.mult).then_inc(s_xn, 1)
                    if kind == "xT":
                        v = slice(AT[i], AT[i] + NS[i])
                        take_lo(T, g, use, xTl[:, :, v], xT_view(T, use), xTh[:, :, v])
                    if T is FIRST and kind == "xT" and i == NSUB - 1:
                        weights_lo(1)
                    if kind == "S":
                        s, r = i // 4, i % 3
                        n = NS[s]
                        mm_full(dve, T, g, use)
                        if i >= 3:
                            mm_done(dve, T, g, ("S", i - 3))
                        dve.tensor_reduce(rowmax[0:n, r, :],
                                          T.bank_of(use)[0:n, 0:4 * n].rearrange("p (h k) -> p h k", h=4),
                                          AX.X, ALU.max).then_inc(s_rm, 1)
                        dve.wait_ge(s_rm, g * NQ + i + 1)
                        dve.tensor_scalar(nmax[0:n, r, :], rowmax[0:n, r, :], -SCALE, None, ALU.mult
                                          ).then_inc(s_nm, 1)
                    if kind == "AV":
                        s, half, par = i // 4, i % 4 // 2, i % 2
                        n = NS[s]
                        mm_full(dve, T, g, use)
                        ov = T.bank_of(use)[0:n, 0:4 * (HD + 1)].rearrange("p (h d) -> p h d", h=4)
                        if i >= 2:
                            mm_done(dve, T, g, ("AV", i - 2))
                        dve.reciprocal(rsum[0:n, i % 2, :], ov[:, :, HD]).then_inc(s_rs, 1)
                        dve.wait_ge(s_rs, g * NQ + i + 1)
                        if i >= 4:
                            tp_full(dve, T, g, ("OT", 2 * (s - 1) + half))
                        dve.tensor_tensor(O[0:n, half * 4:half * 4 + 4, par, :], ov[:, :, 0:HD],
                                          rsum[0:n, i % 2, :].rearrange("p (h a) -> p h a", a=1)
                                          .broadcast_to([n, 4, HD]), ALU.mult).then_inc(s_mmdve, 1)
                    if kind == "OT":
                        s, half = i // 2, i % 2
                        n = NS[s]
                        take_lo(T, g, use, OTl[:, half * 4:half * 4 + 4, 0:n],
                                T.bank_of(use)[:, 0:4 * n].rearrange("p (m t) -> p m t", m=4),
                                OTh[:, half * 4:half * 4 + 4, 0:n])
                    if kind == "proj":
                        n = NS[i]
                        Hb = H[0:n, g * NSUB + i, :]
                        mm_full(dve, T, g, use)
                        dve.wait_ge(s_hb, g * NSUB + i + 1)
                        dve.tensor_tensor(Hb, T.bank_of(use)[0:n, 0:EMB], Hb, ALU.add).then_inc(s_mmdve, 1)
                        mm_done(dve, T, g, use)
                        dve.sem_inc(s_carrier, 1)
                        layer_norm(Hb, i, n, stats2, mv2, veps2, s_ln2, s_ve2, g * NSUB + i)
                    if kind == "ln2":
                        n = NS[i]
                        dve.wait_ge(s_rstd2, g * NSUB + i + 1)
                        dve.wait_ge(s_sent, g + 2)
                        dve.tensor_scalar(xn2[0:n, i, :], H[0:n, g * NSUB + i, :], mv2[0:n, i, 0:1],
                                          rstd2[0:n, i:i + 1], ALU.subtract, ALU.mult).then_inc(s_xn2, 1)
                    if kind == "x2T":
                        take_lo(T, g, use, x2T_view(x2Tl, i), xT_view(T, use), x2T_view(x2Th, i))
                    if kind == "route":
                        n = NS[i]
                        mm_full(dve, T, g, use)
                        dve.tensor_copy(LG[0:n, i, :], T.bank_of(use)[0:n, 0:EXPERTS]).then_inc(s_mmdve, 1)
                        mm_done(dve, T, g, use)

            dve.wait_ge(s_ptl, 1)
            turn(FIRST, -1)
            weights_lo(2)
            weights_lo(3)
            dve.wait_ge(s_wthi, 2)
            dve.tensor_tensor(flat(Wrl), flat(Wr), flat(Wrh).bitcast(F32), ALU.subtract).then_inc(s_wtlo, 1)
            dve.wait_ge(s_walo, 4)
            dve.memset(V[:, :, :, HD:HD + 1], 1.0).then_inc(s_ptl, 1)
            dve.sem_inc(s_carry, 1)
            with dve.Fori(0, GROUPS - 1) as g:
                turn(LOOP, g)
            turn(LAST, GROUPS - 1)
            for part in range(len(CHOSEN) - 1):
                choose(GROUPS, part)
            dve.wait_ge(s_mm, END["mm"] + 1)
            place(GROUPS, bank[0][0:BM, 0:NSUB * EXPERTS].rearrange("p (s e) -> p s e", s=NSUB))

            done = [(GROUPS + 1) * PLACE]

            def step(ins):
                done[0] += 1
                ins.then_inc(s_tb, 1)
                dve.wait_ge(s_tb, done[0])

            dve.wait_ge(s_cnt, 1)
            step(dve.tensor_copy(cnt[:], bank[1][:, 0:EXPERTS]))
            step(dve.tensor_tensor(nbc[:], cnt[:].rearrange("p (e a) -> p e a", a=1)
                                   .broadcast_to([P, EXPERTS, MAXNB]),
                                   steps128[:].rearrange("p (a j) -> p a j", a=1)
                                   .broadcast_to([P, EXPERTS, MAXNB]), ALU.is_gt))
            step(dve.tensor_reduce(nb[:], nbc[:], AX.X, ALU.add))
            step(dve.tensor_tensor(st8[:], before[:], be(nb[:], EXPERTS), ALU.mult))
            step(dve.tensor_reduce(st[:], st8[:], AX.X, ALU.add))
            step(dve.tensor_copy(tab[:, 0, :], cnt[:]))
            step(dve.tensor_copy(tab[:, 1, :], st[:]))
            step(dve.tensor_tensor(nb[:], nb[:], st[:], ALU.add))
            dve.tensor_copy(tab[:, 2, :], nb[:]).then_inc(s_tab, 1)
            step(dve.scalar_tensor_tensor(out=sty[:], in0=st[:], scalar=float(P), in1=yshift[:],
                                          op0=ALU.mult, op1=ALU.add))
            for g in range(GROUPS):
                step(dve.tensor_tensor(ty[0:BM, g].rearrange("p k s e -> p (k s) e"),
                                       hot[0:BM, g + 1].rearrange("p k s e -> p (k s) e"),
                                       be(sty[:], 2 * NSUB)[0:BM], ALU.mult))
            step(dve.tensor_reduce(posy[0:BM].rearrange("p g k s -> p (g k s)"),
                                   ty[0:BM].rearrange("p g k s e -> p (g k s) e"), AX.X, ALU.add))
            step(dve.tensor_tensor(posy[0:BM].rearrange("p g k s -> p (g k s)"),
                                   posy[0:BM].rearrange("p g k s -> p (g k s)"),
                                   posf[0:BM, 1:].rearrange("p g k s -> p (g k s)"), ALU.add))
            dve.tensor_copy(posy_i[0:BM].rearrange("p g k s -> p (g k s)"),
                            posy[0:BM].rearrange("p g k s -> p (g k s)")).then_inc(s_posy, 1)

            def weights_hi(e, k):
                raw_there(dve, e, k)
                dve.tensor_copy(flat(Wph[k]), raw[k][:, 1024:2048]).then_inc(s_whi_d, 1)
                dve.tensor_copy(Woh[:, bass.ds(e, 1), :].rearrange("p a n -> p (a n)"),
                                raw[k][:, 2048:3072]).then_inc(s_whi_d, 1)

            def rows_lo(n):
                dve.wait_ge(s_bThi, n + 1)
                dve.tensor_tensor(bTl[:], bank[2][:, 0:EMB], bTh[:].bitcast(F32), ALU.subtract
                                  ).then_inc(s_bTlo, 1)

            def add_bo(n, e):
                dve.wait_ge(s_y, n + 1)
                dve.wait_ge(s_yst, n * 16 + 1)
                dve.tensor_tensor(ysb[:], bank[4][:, 0:EMB],
                                  bo[:, bass.ds(e, 1), :].rearrange("p a n -> p (a n)"), ALU.add
                                  ).then_inc(s_ysb, 1)

            def expert(e, k):
                first, end = bounds(dve, e)
                wait_first(dve, s_bias[k], (e + 2 - k) * 16)
                with dve.Fori(first, end) as j:
                    dve.wait_ge(s_g, j + 1)
                    dve.tensor_tensor(gsum[:], bank[0][:], bgu[k][:, 0, :], ALU.add).then_inc(s_gs, 1)
                    dve.wait_ge(s_u, j + 1)
                    dve.tensor_tensor(usum[:], bank[1][:], bgu[k][:, 1, :], ALU.add).then_inc(s_us, 1)
                    dve.wait_ge(s_us, j + 1)
                    dve.wait_ge(s_silu, j + 1)
                    dve.tensor_tensor(hid[:], gact[:], usum[:], ALU.mult).then_inc(s_hid, 1)
                    rows_lo(j + 1)
                    add_bo(j, expert_before(dve, e, first, j))
                    dve.wait_ge(s_hThi, j + 2)
                    dve.tensor_tensor(hTl[:], bank[3][:], hTh[:].bitcast(F32), ALU.subtract
                                      ).then_inc(s_hTlo, 1)

            dve.memset(hTh[:].bitcast(F32), 0.0)
            dve.memset(hTl[:].bitcast(F32), 0.0).then_inc(s_hTlo, 1)
            weights_hi(0, 0)
            weights_hi(1, 1)
            rows_lo(0)
            dve.wait_ge(s_bo, 16)
            with dve.Fori(0, EXPERTS // 2 - 1) as ep:
                for k in range(2):
                    expert(ep * 2 + k, k)
                    weights_hi(ep * 2 + k + 2, k)
            for k in range(2):
                expert(EXPERTS - 2 + k, k)
            add_bo(end_of_all(dve), EXPERTS - 1)
            for k in range(2):
                for b in range(BLOCKS):
                    n, g, s = NS[b % NSUB], b // NSUB, b % NSUB
                    dve.wait_ge(s_gath[k][g], 16 * NSUB)
                    if k:
                        dve.wait_ge(s_add, b + 1)
                    dve.scalar_tensor_tensor(out=H[0:n, b, :], in0=gath[k][0:n, b, :],
                                             scalar=wst[0:n, g + 1, k, s:s + 1], in1=H[0:n, b, :],
                                             op0=ALU.mult, op1=ALU.add).then_inc(s_add, 1)


_INS = ['x', 'cls_tok', 'L0_tok_W', 'L0_tok_b', 'L0_tok_class_token', 'L0_tok_pos_emb', 'L0_attn_w_q',
        'L0_attn_w_k', 'L0_attn_w_v', 'L0_attn_w_u', 'L0_attn_b_u', 'L0_ffn_W_router', 'L0_ffn_W_gate',
        'L0_ffn_b_gate', 'L0_ffn_W_up', 'L0_ffn_b_up', 'L0_ffn_W_out', 'L0_ffn_b_out']
_OUTS = [((IMAGES, TOK, EMB), 'float32')]


def kernel(**inputs):
    import numpy as _np
    import concourse.bacc as _bacc
    from concourse import mybir as _mybir
    from concourse.bass_utils import run_bass_kernel_spmd as _run

    nc = _bacc.Bacc("TRN2", target_bir_lowering=False, num_devices=1)
    arrays, args = {}, []
    for name in _INS:
        a = _np.ascontiguousarray(inputs[name])
        arrays[f"in_{name}_dram"] = a
        args.append(nc.dram_tensor(f"in_{name}_dram", a.shape, _mybir.dt.from_np(a.dtype), kind="ExternalInput").ap())
    for i, (shape, dtype) in enumerate(_OUTS):
        dt = _mybir.dt.from_np(_np.dtype(dtype))
        args.append(nc.dram_tensor(f"out_{i}_dram", shape, dt, kind="ExternalOutput").ap())
    vit_tower(nc, *args)
    r = _run(nc, [arrays], core_ids=[0])
    got = tuple(r.results[0][f"out_{i}_dram"] for i in range(len(_OUTS)))
    return got[0]
```

```python
from contextlib import ExitStack

import concourse.bass as bass
from concourse import mybir

F32 = mybir.dt.float32
F32R = mybir.dt.float32r
BF16 = mybir.dt.bfloat16
U32 = mybir.dt.uint32
I32 = mybir.dt.int32
ALU = mybir.AluOpType
ACT = mybir.ActivationFunctionType
AX = mybir.AxisListType

P = 128
IMAGES, CHANNELS, SIDE = 32, 3, 96
PATCH = 16
GRID = SIDE // PATCH
EMB = 256
TOK = GRID * GRID + 2
HEADS, HD = 16, 64
EXPERTS, MID = 8, 512
EPS = 1e-5

GROUPS = 4
GI = IMAGES // GROUPS
GT = GI * TOK
SUBS = (3, 3, 2)
NSUB = len(SUBS)
NS = [n * TOK for n in SUBS]
AT = [0, NS[0], NS[0] + NS[1]]
BLOCKS = GROUPS * NSUB
BM = NS[0]
EK = EMB // P
CK = CHANNELS * PATCH * PATCH // P
HK = HEADS * HD // P
MK = MID // P
NQ = NSUB * 4
XP = GI * GRID
SCALE = 1.0 / HD
NEG = -1.0e30

NDSET = 19 + (IMAGES * TOK + P - 1) // P - 1
CHOOSE, PLACE = 26, 9
TOKENS = IMAGES * TOK
REGION = (TOKENS + P - 1) // P * P + P
MAXNB = (TOKENS + P - 1) // P
MAXBLOCKS = (2 * TOKENS + EXPERTS * P) // P


def vit_tower(nc, x, cls_tok, tok_W, tok_b, tok_class, tok_pos, w_q, w_k, w_v, w_u, b_u,
              W_router, W_gate, b_gate, W_up, b_up, W_out, b_out, out):
    ctx = ExitStack()
    only_a = ExitStack()
    Xs = nc.dram_tensor("Xs", (EXPERTS * REGION, EMB), F32, kind="Internal").ap()
    Ys = nc.dram_tensor("Ys", ((MAXBLOCKS + 1) * P, EMB), F32, kind="Internal").ap()
    with ctx:
        def sb(name, shape, dt=F32, where=ctx):
            return where.enter_context(nc.sbuf_tensor(name, shape, dt))

        def sem(name):
            return ctx.enter_context(nc.semaphore(name))

        pre = ExitStack()
        pTh, pTl = (sb(n, [P, CK, GI, TOK], F32R, pre) for n in ("pTh", "pTl"))
        Xr = sb("Xr", [P, 2, GRID, P], F32, pre)
        pre.close()
        raws = sb("raws", [P, 2 * 3072])
        raw = [raws[:, i * 3072:(i + 1) * 3072] for i in range(2)]
        H = sb("H", [P, BLOCKS, EMB])
        zero = sb("zero", [P, EMB])
        ident = sb("ident", [P, P])
        lower = sb("lower", [P, P], F32R)
        ones = sb("ones", [P, P], F32R)
        iota = sb("iota", [P, EXPERTS])
        region = sb("region", [P, EXPERTS])
        yshift = sb("yshift", [P, EXPERTS])
        before = sb("before", [P, EXPERTS, EXPERTS])
        steps128 = sb("steps128", [P, MAXNB])
        carry = sb("carry", [P, EXPERTS], F32R)
        live = sb("live", [P, 1])
        xn2 = sb("xn2", [P, NSUB, EMB])
        LG = sb("LG", [P, NSUB, EXPERTS])
        sh = sb("sh", [P, NSUB, EXPERTS])
        ex = sb("ex", [P, NSUB, EXPERTS])
        pr = sb("pr", [P, NSUB, EXPERTS])
        pw = sb("pw", [P, NSUB, EXPERTS])
        tmp8 = sb("tmp8", [P, NSUB, EXPERTS])
        sm = sb("sm", [P, NSUB])
        ri = sb("ri", [P, NSUB])
        top = sb("top", [P, NSUB, 8])
        tpr = sb("tpr", [P, NSUB, 8])
        tix = sb("tix", [P, NSUB, 8], U32)
        tif = sb("tif", [P, NSUB, 2])
        lohi = sb("lohi", [P, 2, NSUB])
        A = sb("A", [P, NSUB, EXPERTS], F32R)
        rk = sb("rk", [P, NSUB, EXPERTS])
        pos_i = sb("pos_i", [P, 2, NSUB], U32)
        hot = sb("hot", [P, GROUPS + 1, 2, NSUB, EXPERTS])
        posf = sb("posf", [P, GROUPS + 1, 2, NSUB])
        wst = sb("wst", [P, GROUPS + 1, 2, NSUB])
        posy = sb("posy", [P, GROUPS, 2, NSUB])
        posy_i = sb("posy_i", [P, GROUPS, 2, NSUB], U32)
        cnt = sb("cnt", [P, EXPERTS])
        nb = sb("nb", [P, EXPERTS])
        st = sb("st", [P, EXPERTS])
        sty = sb("sty", [P, EXPERTS])
        tab = sb("tab", [P, 3, EXPERTS], I32)
        def a(name, shape, dt=F32):
            return sb(name, shape, dt, only_a)
        Wth, Wtl = (a(n, [P, CK, EMB], F32R) for n in ("Wth", "Wtl"))
        X = a("X", [P, CHANNELS, PATCH * SIDE])
        pos = a("pos", [BM, EMB])
        xTh, xTl = (a(n, [P, EK, GT], F32R) for n in ("xTh", "xTl"))
        Wqh, Wql = (a(n, [P, EK, HEADS * HD], F32R) for n in ("Wqh", "Wql"))
        Wkh, Wkl = (a(n, [P, EK, HEADS * HD], F32R) for n in ("Wkh", "Wkl"))
        Wvh, Wvl = (a(n, [P, EK, HEADS * HD], F32R) for n in ("Wvh", "Wvl"))
        Wuh, Wul = (a(n, [P, HK, EMB], F32R) for n in ("Wuh", "Wul"))
        Wr = a("Wr", [P, EK, EXPERTS])
        Wrh, Wrl = (a(n, [P, EK, EXPERTS], F32R) for n in ("Wrh", "Wrl"))
        bu = a("bu", [BM, EMB])
        xn = a("xn", [BM, NSUB, EMB])
        stats1, stats2 = (a(n, [BM, NSUB, 6]) for n in ("stats1", "stats2"))
        mv1, mv2 = (a(n, [BM, NSUB, 2]) for n in ("mv1", "mv2"))
        veps1, veps2 = (a(n, [BM, NSUB]) for n in ("veps1", "veps2"))
        rstd1, rstd2 = (a(n, [BM, NSUB]) for n in ("rstd1", "rstd2"))
        minus_half = a("minus_half", [BM, NSUB])
        QT = a("QT", [P, HK, GT])
        KT = a("KT", [P, HK, GT])
        V = a("V", [P, NSUB, HEADS, HD + 1])
        mask = a("mask", [BM, 4, BM], BF16)
        mask2 = a("mask2", [BM, 4, NS[2]], BF16)
        identb = a("identb", [BM, BM], BF16)
        rowmax = a("rowmax", [BM, 3, 4])
        nmax = a("nmax", [BM, 3, 4])
        PP = a("PP", [P, 2, 3, 4 * BM])
        Pr = PP[:, 0]
        PT = PP[:, 1]
        rsum = a("rsum", [BM, 2, 4])
        O = a("O", [BM, HK, 2, HD])
        pos2 = O[:, 0:2].rearrange("p m a d -> p (m a d)")
        OTh, OTl = (a(n, [P, HK, BM], F32R) for n in ("OTh", "OTl"))
        x2Th, x2Tl = (a(n, [P, EK * BM], F32R) for n in ("x2Th", "x2Tl"))
        only_a.close()
        Wgh, Wgl, Wph, Wpl = ([sb(f"{n}{i}", [P, EK, MID], F32R) for i in range(2)]
                              for n in ("Wgh", "Wgl", "Wph", "Wpl"))
        bgu = [sb(f"bgu{i}", [P, 2, MID]) for i in range(2)]
        Woh, Wol = (sb(n, [P, EXPERTS, MK * EMB], F32R) for n in ("Woh", "Wol"))
        bo = sb("bo", [P, EXPERTS, EMB])
        xs = sb("xs", [P, EMB])
        bTh, bTl = (sb(n, [P, EK * P], F32R) for n in ("bTh", "bTl"))
        gsum = sb("gsum", [P, MID])
        usum = sb("usum", [P, MID])
        gact = sb("gact", [P, MID])
        hid = sb("hid", [P, MID])
        hTh, hTl = (sb(n, [P, MK * P], F32R) for n in ("hTh", "hTl"))
        ysb = sb("ysb", [P, EMB])
        ty = sb("ty", [P, GROUPS, 2, NSUB, EXPERTS])
        st8 = sb("st8", [P, EXPERTS, EXPERTS])
        nbc = sb("nbc", [P, EXPERTS, MAXNB])
        gath = [r.rearrange("p (b e) -> p b e", e=EMB) for r in raw]

        bank = [ctx.enter_context(nc.psum_tensor(f"bank{i}", [P, 512], F32)) for i in range(8)]
        mmb, tpb = bank[0:5], bank[5:8]

        s_carrier = sem("s_carrier")
        s_x = sem("s_x")
        s_xr = sem("s_xr")
        s_wt = sem("s_wt")
        s_wr = sem("s_wr")
        s_wa = [sem(f"s_wa{i}") for i in range(4)]
        s_pos = sem("s_pos")
        s_pos2 = sem("s_pos2")
        s_bu = sem("s_bu")
        s_ys0 = sem("s_ys0")
        s_raw = [sem(f"s_raw{i}") for i in range(2)]
        s_raw2 = [sem(f"s_raw2_{i}") for i in range(2)]
        s_bias = [sem(f"s_bias{i}") for i in range(2)]
        s_bo = sem("s_bo")
        s_scat = [sem(f"s_scat{k}") for k in range(2)]
        s_sent = sem("s_sent")
        s_tail0 = sem("s_tail0")
        s_tail = sem("s_tail")
        s_xs = sem("s_xs")
        s_yst = sem("s_yst")
        s_gath = [[sem(f"s_gath{k}_{i}") for i in range(n)] for k, n in enumerate((GROUPS, BLOCKS))]
        s_out = sem("s_out")
        s_set = sem("s_set")
        s_dset = sem("s_dset")
        s_wahi = sem("s_wahi")
        s_walo = sem("s_walo")
        s_walo2 = sem("s_walo2")
        s_wthi = sem("s_wthi")
        s_wtlo = sem("s_wtlo")
        s_ptl = sem("s_ptl")
        s_posadd = sem("s_posadd")
        s_tp = sem("s_tp")
        s_tphi = sem("s_tphi")
        s_tpact = sem("s_tpact")
        s_tpdve = sem("s_tpdve")
        s_mm = sem("s_mm")
        s_mmact = sem("s_mmact")
        s_exp = sem("s_exp")
        s_mmdve = sem("s_mmdve")
        s_ln1 = sem("s_ln1")
        s_ve1 = sem("s_ve1")
        s_rstd1 = sem("s_rstd1")
        s_xn = sem("s_xn")
        s_hb = sem("s_hb")
        s_ln2 = sem("s_ln2")
        s_ve2 = sem("s_ve2")
        s_rstd2 = sem("s_rstd2")
        s_xn2 = sem("s_xn2")
        s_rm = sem("s_rm")
        s_nm = sem("s_nm")
        s_rs = sem("s_rs")
        s_lg = sem("s_lg")
        s_sh = sem("s_sh")
        s_rexp = sem("s_rexp")
        s_ro = sem("s_ro")
        s_A = sem("s_A")
        s_pos_i = sem("s_pos_i")
        s_carry = sem("s_carry")
        s_cnt = sem("s_cnt")
        s_tab = sem("s_tab")
        s_tb = sem("s_tb")
        s_posy = sem("s_posy")
        s_whi01 = sem("s_whi01")
        s_whi_a = sem("s_whi_a")
        s_whi_d = sem("s_whi_d")
        s_wlo = sem("s_wlo")
        s_bT = sem("s_bT")
        s_bThi = sem("s_bThi")
        s_bTlo = sem("s_bTlo")
        s_g = sem("s_g")
        s_u = sem("s_u")
        s_gs = sem("s_gs")
        s_us = sem("s_us")
        s_silu = sem("s_silu")
        s_hid = sem("s_hid")
        s_hT = sem("s_hT")
        s_hThi = sem("s_hThi")
        s_hTlo = sem("s_hTlo")
        s_y = sem("s_y")
        s_ysb = sem("s_ysb")
        s_add = sem("s_add")

        NEXT = ("reorder", "x", "emb", "embedded", "ln1", "xT", "qa", "ka")

        def turn_steps(attention, following):
            steps = []

            def add(kind, *numbers):
                if kind in ("split", "proj_half") and following:
                    return
                if following if kind in NEXT else attention:
                    steps.extend((kind, n) for n in numbers)

            values_at = {3: 2, 5: 3, 7: 4, 9: 5}
            embed_at, xT_at = range(8, 8 + NSUB), range(10, 10 + NSUB)
            project_at = [8, 12, 16]
            split_at = range(8, 14)
            between = {10: (("x2T", 0),),
                       13: (("qa", 0),),
                       14: (("ka", 0), ("x2T", 1), ("qa", 1)),
                       15: (("ka", 1),),
                       16: (("qa", 2),),
                       17: (("ka", 2), ("qa", 3)),
                       18: (("x2T", 2), ("ka", 3))}
            add("v", 0, 1)
            add("reorder", 0)
            for t in range(NQ + 7):
                if t < NQ:
                    add("S", t)
                if t - 1 in embed_at:
                    add("embedded", embed_at.index(t - 1))
                if t - 1 in project_at:
                    add("projected", project_at.index(t - 1))
                if t < 2:
                    m = HK // 2 + 2 * t
                    add("qb", m)
                    add("kb", m)
                    add("exp", t)
                    add("qb", m + 1)
                    add("kb", m + 1)
                if t in values_at:
                    add("v", values_at[t])
                if t < 4:
                    add("choose", t)
                if t == 5:
                    add("place", 0)
                if 1 <= t < 1 + CK:
                    add("x", t - 1)
                if 2 <= t < NQ + 2:
                    add("PT", t - 2)
                if t % 2 == 1 and 5 <= t < NQ + 5:
                    add("OT", (t - 5) // 2)
                if 3 <= t < NQ + 3:
                    add("AV", t - 3)
                if 2 <= t < NQ:
                    add("exp", t)
                if t - 1 in project_at:
                    add("ln2", project_at.index(t - 1))
                if t - 1 in embed_at:
                    add("ln1", embed_at.index(t - 1))
                if t - 3 in project_at:
                    add("route", project_at.index(t - 3))
                if t in embed_at:
                    add("emb", embed_at.index(t))
                if t == 14:
                    add("proj_half", 2)
                if t in project_at:
                    add("proj", project_at.index(t))
                if t in xT_at:
                    add("xT", xT_at.index(t))
                if t == 4:
                    add("rank", 0)
                if t in (6, 7):
                    add("choose", t - 2)
                if t == 7:
                    add("sent", 0)
                for kind, n in between.get(t, ()):
                    add(kind, n)
                if t in split_at:
                    add("split", split_at.index(t))
            add("route", 2)
            return steps

        def taker(use):
            if use[0] == "S":
                return "exp"
            return "act" if use[0] in ("qa", "ka", "qb", "kb", "v", "PT") else "dve"

        class Turn:
            def __init__(self, steps, before, loops):
                self.steps, self.loops = steps, loops
                self.mm = [u for u in steps if u[0] in ("emb", "qa", "ka", "qb", "kb", "v", "rank", "S", "AV",
                                                        "proj", "route")]
                self.tp = [u for u in steps if u[0] in ("x", "xT", "PT", "OT", "x2T")]
                self.his = [u for u in self.tp if u[0] != "PT"]
                self.per = dict(mm=len(self.mm), tp=len(self.tp), hi=len(self.his))
                for e in ("act", "dve", "exp"):
                    self.per[e] = sum(taker(u) == e for u in self.mm)
                    self.per["tp" + e] = sum(taker(u) == e for u in self.tp)
                self.start = {k: before.get(k, 0) for k in self.per}

            def before(self, g, key):
                return self.start[key] + (g * self.per[key] if self.loops else 0)

            def end(self, turns=1):
                return {k: self.start[k] + turns * self.per[k] for k in self.per}

            def bank_of(self, use):
                return mmb[self.mm.index(use) % len(mmb)] if use in self.mm else tpb[self.tp.index(use) % len(tpb)]

            def taken(self, n):
                e = taker(self.mm[n])
                return e, sum(taker(u) == e for u in self.mm[:n + 1])

            def tp_taken(self, n):
                e = taker(self.tp[n])
                return "tp" + e, sum(taker(u) == e for u in self.tp[:n + 1])

        FIRST = Turn(turn_steps(False, True), {}, False)
        LOOP = Turn(turn_steps(True, True), FIRST.end(), True)
        LAST = Turn(turn_steps(True, False), LOOP.end(GROUPS - 1), False)
        END = LAST.end()
        s_taken = {"act": s_mmact, "dve": s_mmdve, "exp": s_exp, "tpact": s_tpact, "tpdve": s_tpdve}

        def mm_free(pe, T, g, use):
            n = T.mm.index(use) - len(mmb)
            if n >= 0:
                e, k = T.taken(n)
                pe.wait_ge(s_taken[e], T.before(g, e) + k)
            elif n == -len(mmb) and T is not FIRST:
                for e in ("act", "dve"):
                    pe.wait_ge(s_taken[e], T.before(g, e))

        def mm_full(eng, T, g, use):
            eng.wait_ge(s_mm, T.before(g, "mm") + T.mm.index(use) + 1)

        def mm_done(eng, T, g, use):
            e, k = T.taken(T.mm.index(use))
            eng.wait_ge(s_taken[e], T.before(g, e) + k)

        def tp_free(pe, T, g, use):
            n = T.tp.index(use) - len(tpb)
            if n >= 0:
                e, k = T.tp_taken(n)
                pe.wait_ge(s_taken[e], T.before(g, e) + k)
            elif n == -len(tpb) and T is not FIRST:
                for e in ("tpact", "tpdve"):
                    if T.start[e]:
                        pe.wait_ge(s_taken[e], T.before(g, e))

        def tp_full(eng, T, g, use):
            eng.wait_ge(s_tp, T.before(g, "tp") + T.tp.index(use) + 1)

        def tp_done(eng, T, g, use):
            e, k = T.tp_taken(T.tp.index(use))
            eng.wait_ge(s_taken[e], T.before(g, e) + k)

        def tp_hi(eng, T, g, use):
            eng.wait_ge(s_tphi, T.before(g, "hi") + T.his.index(use) + 1)

        WA = [(w_q, Wqh, Wql, QT[:].rearrange("p m t -> p (m t)")[:, 0:2048]),
              (w_k, Wkh, Wkl, KT[:].rearrange("p m t -> p (m t)")[:, 0:2048]),
              (w_v, Wvh, Wvl, V[:].rearrange("p s h d -> p (s h d)")[:, 0:2048]),
              (w_u, Wuh, Wul, PP[:].rearrange("p a r t -> p (a r t)")[:, 0:2048])]
        tok_W_raw = raws[:, CK * GT:CK * GT + CK * EMB]
        XD = x.rearrange("(g b) c (h i) w -> g b h c (i w)", g=GROUPS, i=PATCH)
        outd = out.rearrange("b t e -> (b t) e")

        def wait_first(eng, s, value):
            eng.wait_ge(s, value)
            if not isinstance(value, int):
                eng.sem_inc(s_carrier, 1)

        def flat(t):
            return t[:].rearrange("p k n -> p (k n)")

        def load_expert(eng, e, k, done):
            for j, (w, kk) in enumerate(((W_gate, EK), (W_up, EK), (W_out, MK))):
                eng.dma_start(raw[k][:, j * 1024:(j + 1) * 1024].rearrange("p (k n) -> p k n", k=kk),
                              w[bass.ds(e, 1)].rearrange("a (k p) n -> p (a k) n", p=P)).then_inc(done[k], 16)

        def raw_there(eng, e, k):
            if isinstance(e, int) and e < 2:
                eng.wait_ge(s_raw[k], 48)
            else:
                eng.wait_ge(s_raw2[k], (e - k) * 24)

        def load_bias(eng, e, k):
            for j, b in enumerate((b_gate, b_up)):
                eng.dma_start(bgu[k][:, j, :], b[bass.ds(e, 1)].broadcast_to([P, MID])).then_inc(s_bias[k], 16)

        def bounds(eng, e):
            first = eng.value_load(tab[0:1, 1, bass.ds(e, 1)], min_val=0, max_val=MAXBLOCKS)
            ends = [eng.value_load(tab[0:1, 2, bass.ds(e + k, 1)], min_val=1, max_val=MAXBLOCKS) for k in range(2)]
            return (first, ends[0]), (ends[0], ends[1])

        def clear_tails(eng, experts, done):
            eng.wait_ge(s_tab, 1)
            eng.wait_ge(s_sent, GROUPS + 1)
            for e in experts:
                count = eng.value_load(tab[0:1, 0, e:e + 1], min_val=0, max_val=TOKENS)
                eng.dma_start(Xs[bass.ds(count + e * REGION, P), :], zero[:]).then_inc(done, 16)

        def expert_before(eng, e, first, j):
            return ((e - 1 + (j > first)) * (j > 0)).with_bounds(min_val=0, max_val=EXPERTS - 1)

        def end_of_all(eng):
            return eng.value_load(tab[0:1, 2, EXPERTS - 1:EXPERTS], min_val=1, max_val=MAXBLOCKS)

        def x_view(T, c):
            return T.bank_of(("x", c))[:, 0:GRID * XP].rearrange("p (w b h) -> p b h w", w=GRID, b=GI)

        def pT_view(t, c):
            return t[:, c, :, 2:TOK].rearrange("p b (h w) -> p b h w", w=GRID)

        def xT_view(T, use):
            return T.bank_of(use)[:, 0:EK * NS[use[1]]].rearrange("p (k t) -> p k t", k=EK)

        def x2T_view(t, s):
            return t[:, 0:EK * NS[s]].rearrange("p (k t) -> p k t", k=EK)

        def v_dst(n):
            s, half = n // 2, n % 2
            return V[0:NS[s], s, half * 8:half * 8 + 8, 0:HD]

        def v_src(T, n):
            return T.bank_of(("v", n))[0:NS[n // 2], :].rearrange("p (h d) -> p h d", d=HD)

        block = ctx.enter_context(nc.Block())

        @block.sync
        def _(sp):
            def load_x(g):
                for b in range(GI):
                    sp.dma_start(X[b * GRID:(b + 1) * GRID],
                                 XD[bass.ds(g, 1), b].rearrange("a h c n -> (a h) c n")).then_inc(s_x, 16)

            load_x(0)
            sp.dma_start(tok_W_raw.rearrange("p (c e) -> p c e", c=CK),
                         tok_W.rearrange("(c p) e -> p c e", p=P)).then_inc(s_wt, 16)

            def load_w(n):
                w, _, _, src = WA[n]
                sp.dma_start(src.rearrange("p (k n) -> p k n", k=w.shape[0] // P),
                             w.rearrange("(k p) n -> p k n", p=P)).then_inc(s_wa[n], 16)

            load_w(0)
            for i in range(3):
                sp.dma_start(pos[i * TOK:i * TOK + 1, :], cls_tok[0]).then_inc(s_pos, 16)
                sp.dma_start(pos[i * TOK + 1:(i + 1) * TOK, :], tok_pos[0]).then_inc(s_pos, 16)
            sp.wait_ge(s_dset, 2)
            for i in range(3):
                sp.dma_start(pos2[i * TOK + 1:i * TOK + 2, :], tok_class[0]).then_inc(s_pos2, 16)
                sp.dma_start(pos2[i * TOK + 2:(i + 1) * TOK, :],
                             tok_b.rearrange("(a e) -> a e", a=1).broadcast_to([TOK - 2, EMB])
                             ).then_inc(s_pos2, 16)
            load_w(1)
            sp.dma_start(bu[:], b_u.rearrange("(a e) -> a e", a=1).broadcast_to([BM, EMB])).then_inc(s_bu, 16)
            load_w(2)
            load_w(3)
            sp.dma_start(Wr[:], W_router.rearrange("(k p) e -> p k e", p=P)).then_inc(s_wr, 16)
            sp.wait_ge(s_xr, CK)
            load_x(1)
            sp.dma_start(Ys.rearrange("(b p) e -> p b e", p=P),
                          zero[:].rearrange("p (b e) -> p b e", b=1).broadcast_to([P, MAXBLOCKS + 1, EMB])
                          ).then_inc(s_ys0, 16)
            with sp.Fori(1, GROUPS - 1) as g:
                sp.wait_ge(s_xr, g * CK + CK)
                load_x(g + 1)
            sp.wait_ge(s_mm, LOOP.before(GROUPS - 2, "mm") + LOOP.mm.index(("emb", NSUB - 1)) + 1)
            load_expert(sp, 0, 0, s_raw)
            load_expert(sp, 1, 1, s_raw)
            sp.wait_ge(s_mm, LAST.start["mm"] + LAST.mm.index(("v", 2 * NSUB - 1)) + 1)
            for e in range(2):
                load_bias(sp, e, e)
            sp.wait_ge(s_mmdve, END["dve"])
            sp.dma_start(bo[:], b_out.rearrange("(a e) n -> a e n", a=1).broadcast_to([P, EXPERTS, EMB])
                         ).then_inc(s_bo, 16)
            clear_tails(sp, [0], s_tail0)
            with sp.Fori(0, EXPERTS // 2) as ep:
                for k, (first, end) in enumerate(bounds(sp, ep * 2)):
                    if k == 0:
                        sp.wait_ge(s_scat[0], 48 * (GROUPS + 1))
                        sp.wait_ge(s_tail0, 16)
                    else:
                        sp.wait_ge(s_scat[1], 48 * (GROUPS + 1))
                        sp.wait_ge(s_tail, 16 * (EXPERTS - 1))
                    with sp.Fori(first, end) as j:
                        row = ((ep * 2 + k) * REGION + (j - first) * P
                               ).with_bounds(min_val=0, max_val=EXPERTS * REGION - P)
                        sp.wait_ge(s_bT, j + 1)
                        sp.dma_start(xs[:], Xs[bass.ds(row, P), :]).then_inc(s_xs, 16)
            sp.wait_ge(s_bT, end_of_all(sp) + 1)
            sp.dma_start(xs[:], W_out[0, 0:P, :]).then_inc(s_xs, 16)
            for b in range(BLOCKS):
                sp.wait_ge(s_add, BLOCKS + b + 1)
                n = NS[b % NSUB]
                t0 = b // NSUB * GT + AT[b % NSUB]
                sp.dma_start(outd[t0:t0 + n, :], H[0:n, b, :]).then_inc(s_out, 16)
            sp.wait_ge(s_out, 16 * BLOCKS)

        @block.gpsimd
        def _(pool):
            pool.memset(ident[:], 0.0).then_inc(s_set, 1)
            pool.memset(identb[:], 0.0).then_inc(s_set, 1)
            pool.memset(mask[:], 0.0).then_inc(s_set, 1)
            pool.memset(H[:, 0, 0:P], 1.0).then_inc(s_set, 1)
            pool.memset(before[:], 1.0).then_inc(s_set, 1)
            pool.wait_ge(s_set, 5)
            pool.affine_select(out=ident[:], in_=ident[:], compare_op=ALU.not_equal, fill=1.0, base=0,
                               pattern=[[-1, P]], channel_multiplier=1).then_inc(s_set, 1)
            pool.affine_select(out=identb[:], in_=identb[:], compare_op=ALU.not_equal, fill=1.0, base=0,
                               pattern=[[-1, BM]], channel_multiplier=1).then_inc(s_set, 1)
            pool.affine_select(out=H[:, 0, 0:P], in_=H[:, 0, 0:P], compare_op=ALU.is_gt, fill=0.0, base=0,
                               pattern=[[1, P]], channel_multiplier=-1).then_inc(s_set, 1)
            pool.affine_select(out=before[:], in_=before[:], compare_op=ALU.is_gt, fill=0.0, base=0,
                               pattern=[[1, EXPERTS], [-1, EXPERTS]], channel_multiplier=0).then_inc(s_set, 1)
            m = mask[:]
            pool.affine_select(out=m, in_=m, compare_op=ALU.is_ge, fill=NEG, base=0,
                               pattern=[[0, 4], [-1, BM]], channel_multiplier=1).then_inc(s_set, 1)
            for h in range(4):
                pool.wait_ge(s_set, 10 + h)
                mh = mask[:, h, :].rearrange("p (j k) -> p j k", k=TOK)
                pool.affine_select(out=mh, in_=mh, compare_op=ALU.is_ge, fill=NEG, base=TOK - 1,
                                   pattern=[[TOK, 3], [0, TOK]], channel_multiplier=-1).then_inc(s_set, 1)
            pool.wait_ge(s_set, 14)
            pool.tensor_copy(mask2[:], mask[:, :, 0:NS[2]]).then_inc(s_set, 1)
            pool.wait_ge(s_dset, NDSET)
            pool.wait_ge(s_bu, 16)
            pool.sem_inc(s_sent, 1)

            def scatter(turn):
                for k in range(2):
                    wait_first(pool, s_pos_i, 2 * turn + k + 1)
                    for s in range(NSUB):
                        pool.indirect_dma_start(
                            out=Xs, out_offset=bass.IndirectOffsetOnAxis(ap=pos_i[0:NS[s], k, s:s + 1], axis=0),
                            in_=xn2[0:NS[s], s, :], in_offset=None).then_inc(s_scat[k], 16)

            def sent(turn):
                for k in range(2):
                    pool.wait_ge(s_scat[k], 48 * turn + 48)
                pool.sem_inc(s_sent, 1)

            def expert_parts(e, k):
                return ((Wgh[k], Wgl[k]), (Wph[k], Wpl[k]),
                        (Woh[:, bass.ds(e, 1), :], Wol[:, bass.ds(e, 1), :]))

            def split_lo(e, k, j):
                hi, lo = (t[:].rearrange("p k n -> p (k n)") for t in expert_parts(e, k)[j])
                pool.tensor_tensor(lo, raw[k][:, j * 1024:(j + 1) * 1024], hi.bitcast(F32),
                                   ALU.subtract).then_inc(s_wlo, 1)

            def turn(T, g):
                for kind, i in T.steps:
                    if kind == "split":
                        pool.wait_ge(s_whi01, i + 1)
                        split_lo(i // 3, i // 3, i % 3)
                    if kind == "embedded":
                        pool.wait_ge(s_ve1, (g + 1) * NSUB + i + 1)
                        pool.tensor_tensor(rstd1[0:NS[i], i:i + 1], veps1[0:NS[i], i:i + 1], minus_half[0:NS[i], i:i + 1],
                                           ALU.pow).then_inc(s_rstd1, 1)
                    if kind == "ln1":
                        pool.wait_ge(s_xn, (g + 1) * NSUB + i + 1)
                        hb = H[0:NS[i], (g + 1) * NSUB + i, :]
                        pool.tensor_tensor(hb, hb, bu[0:NS[i], :], ALU.add).then_inc(s_hb, 1)
                    if kind == "place":
                        scatter(g)
                    if kind == "sent":
                        sent(g)
                    if kind == "projected":
                        pool.wait_ge(s_ve2, g * NSUB + i + 1)
                        pool.tensor_tensor(rstd2[0:NS[i], i:i + 1], veps2[0:NS[i], i:i + 1], minus_half[0:NS[i], i:i + 1],
                                           ALU.pow).then_inc(s_rstd2, 1)

            def weights_lo(n):
                _, wh, wl, src = WA[n]
                pool.wait_ge(s_wahi, n + 1)
                pool.tensor_tensor(flat(wl), src, flat(wh).bitcast(F32), ALU.subtract).then_inc(s_walo2, 1)

            turn(FIRST, -1)
            weights_lo(2)
            weights_lo(3)
            with pool.Fori(0, GROUPS - 1) as g:
                turn(LOOP, g)
            turn(LAST, GROUPS - 1)
            scatter(GROUPS)

            pool.wait_ge(s_xs, 16)
            for k in range(2):
                load_expert(pool, 2 + k, k, s_raw2)
            with pool.Fori(0, EXPERTS // 2 - 2) as ep:
                for k in range(2):
                    for j in range(3):
                        if j == 0:
                            pool.wait_ge(s_whi_a, ep * 2 + k + 1)
                        else:
                            pool.wait_ge(s_whi_d, (ep * 2 + k) * 2 + j)
                        split_lo(ep * 2 + k + 2, k, j)
                    pool.wait_ge(s_wlo, (ep * 2 + k + 2) * 3 + 3)
                    load_expert(pool, ep * 2 + k + 4, k, s_raw2)
            for k in range(2):
                for j in range(3):
                    if j == 0:
                        pool.wait_ge(s_whi_a, EXPERTS - 4 + k + 1)
                    else:
                        pool.wait_ge(s_whi_d, (EXPERTS - 4 + k) * 2 + j)
                    split_lo(EXPERTS - 2 + k, k, j)
            pool.wait_ge(s_wlo, EXPERTS * 3)
            pool.wait_ge(s_posy, 1)
            last = pool.value_load(tab[0:1, 1, EXPERTS - 1:EXPERTS], min_val=1, max_val=MAXBLOCKS)
            end = end_of_all(pool)
            for k, done in ((0, last), (1, end)):
                wait_first(pool, s_yst, done * 16 + 17)
                for b in range(BLOCKS):
                    n, s = NS[b % NSUB], b % NSUB
                    pool.indirect_dma_start(
                        out=gath[k][0:n, b, :], out_offset=None, in_=Ys,
                        in_offset=bass.IndirectOffsetOnAxis(ap=posy_i[0:n, b // NSUB, k, s:s + 1], axis=0)
                    ).then_inc(s_gath[k][b if k else b // NSUB], 16)

        @block.scalar
        def _(act):
            def weights_hi(n):
                _, wh, _, src = WA[n]
                act.wait_ge(s_wa[n], 16)
                act.activation(flat(wh), src, ACT.Copy).then_inc(s_wahi, 1)

            act.wait_ge(s_wt, 16)
            act.activation(flat(Wth), tok_W_raw, ACT.Copy).then_inc(s_wthi, 1)

            def reorder(c):
                act.activation(
                    Xr[0:XP, c % 2, :, :].rearrange("p w (i j) -> p w i j", j=PATCH),
                    X[0:XP, c // 2].rearrange("p (i w j) -> p w i j", w=GRID, j=PATCH)
                    [:, :, c % 2 * 8:c % 2 * 8 + 8, :], ACT.Copy).then_inc(s_xr, 1)

            def take_hi(T, g, use, dst, src):
                tp_full(act, T, g, use)
                act.activation(dst, src, ACT.Copy).then_inc(s_tphi, 1)

            def turn(T, g):
                for kind, i in T.steps:
                    use = (kind, i)
                    if kind == "split":
                        e, j = i // 3, i % 3
                        act.wait_ge(s_raw[e], 48)
                        act.activation(flat((Wgh[e], Wph[e], Woh[:, e:e + 1, :])[j]),
                                       raw[e][:, j * 1024:(j + 1) * 1024], ACT.Copy).then_inc(s_whi01, 1)
                    if kind == "reorder" and T is not FIRST:
                        act.wait_ge(s_x, (g + 2) * (16 * GI))
                        reorder(0)
                        reorder(1)
                    if kind == "x":
                        take_hi(T, g, use, pT_view(pTh, i), x_view(T, i))
                        if i + 2 < CK and T is not FIRST:
                            reorder(i + 2)
                    if T is FIRST and kind == "x" and i == CK - 1:
                        for n in range(len(WA)):
                            weights_hi(n)
                    if kind == "xT":
                        take_hi(T, g, use, xTh[:, :, AT[i]:AT[i] + NS[i]], xT_view(T, use))
                    if kind in ("qa", "qb", "ka", "kb"):
                        mm_full(act, T, g, use)
                        act.activation((QT if kind[0] == "q" else KT)[:, i, :], T.bank_of(use)[:, 0:GT], ACT.Copy
                                       ).then_inc(s_mmact, 1)
                    if kind == "v":
                        mm_full(act, T, g, use)
                        act.activation(v_dst(i), v_src(T, i), ACT.Copy).then_inc(s_mmact, 1)
                    if kind == "choose" and i == 1:
                        act.wait_ge(s_sh, g + 1)
                        act.activation(flat(ex), flat(sh), ACT.Exp).then_inc(s_rexp, 1)
                    if kind == "exp":
                        s, r = i // 4, i % 3
                        n = NS[s]
                        act.wait_ge(s_walo2, 2)
                        act.wait_ge(s_nm, g * NQ + i + 1)
                        if i >= 3:
                            tp_full(act, T, g, ("PT", i - 3))
                        for h in range(4):
                            ins = act.activation(Pr[0:n, r, h * n:(h + 1) * n],
                                                 T.bank_of(("S", i))[0:n, h * n:(h + 1) * n], ACT.Exp,
                                                 bias=nmax[0:n, r, h:h + 1], scale=SCALE)
                        ins.then_inc(s_exp, 1)
                    if kind == "PT":
                        s, r = i // 4, i % 3
                        n = NS[s]
                        tp_full(act, T, g, use)
                        if i >= 3:
                            mm_full(act, T, g, ("AV", i - 3))
                        act.activation(PT[0:n, r, 0:4 * n], T.bank_of(use)[0:n, 0:4 * n], ACT.Copy
                                       ).then_inc(s_tpact, 1)
                    if kind == "OT":
                        s, half = i // 2, i % 2
                        n = NS[s]
                        if i >= 2:
                            mm_full(act, T, g, ("proj", s - 1))
                        take_hi(T, g, use, OTh[:, half * 4:half * 4 + 4, 0:n],
                                T.bank_of(use)[:, 0:4 * n].rearrange("p (m t) -> p m t", m=4))
                    if kind == "x2T":
                        if i >= 1:
                            mm_full(act, T, g, ("route", i - 1))
                        take_hi(T, g, use, x2T_view(x2Th, i), xT_view(T, use))

            turn(FIRST, -1)
            act.wait_ge(s_wr, 16)
            act.activation(flat(Wrh), flat(Wr), ACT.Copy).then_inc(s_wthi, 1)
            with act.Fori(0, GROUPS - 1) as g:
                turn(LOOP, g)
            turn(LAST, GROUPS - 1)
            act.wait_ge(s_sh, GROUPS + 1)
            act.activation(flat(ex), flat(sh), ACT.Exp).then_inc(s_rexp, 1)
            act.sem_inc(s_yst, 1)
            act.sem_inc(s_hThi, 1)

            def gate_hi(e, k):
                raw_there(act, e, k)
                act.activation(flat(Wgh[k]), raw[k][:, 0:1024], ACT.Copy).then_inc(s_whi_a, 1)

            clear_tails(act, range(1, EXPERTS), s_tail)
            act.wait_ge(s_ys0, 16)

            def rows_hi(n):
                act.wait_ge(s_bT, n + 2)
                act.activation(bTh[:], bank[2][:, 0:EMB], ACT.Copy).then_inc(s_bThi, 1)

            def store_y(n):
                act.wait_ge(s_ysb, n + 1)
                act.dma_start(Ys[bass.ds(n * P, P), :], ysb[:]).then_inc(s_yst, 16)

            def expert(e, k, first, end):
                with act.Fori(first, end) as j:
                    act.wait_ge(s_gs, j + 1)
                    act.activation(gact[:], gsum[:], ACT.Silu).then_inc(s_silu, 1)
                    rows_hi(j + 1)
                    act.wait_ge(s_hT, j + 1)
                    act.activation(hTh[:], bank[3][:], ACT.Copy).then_inc(s_hThi, 1)
                    store_y(j)

            rows_hi(0)
            with act.Fori(0, EXPERTS // 2 - 1) as ep:
                for k, blocks in enumerate(bounds(act, ep * 2)):
                    expert(ep * 2 + k, k, *blocks)
                    gate_hi(ep * 2 + k + 2, k)
                    load_bias(act, ep * 2 + k + 2, k)
            for k, blocks in enumerate(bounds(act, EXPERTS - 2)):
                expert(EXPERTS - 2 + k, k, *blocks)
            store_y(end_of_all(act))

        @block.tensor
        def _(pe):
            pe.sem_inc(s_bT, 1)
            pe.wait_ge(s_set, 15)
            pe.wait_ge(s_dset, NDSET)

            def three(dst, a_hi, a_lo, b_hi, b_lo, first, last):
                pe.matmul(dst, a_hi, b_hi, start=first, stop=False)
                pe.matmul(dst, a_hi, b_lo, start=False, stop=False)
                return pe.matmul(dst, a_lo, b_hi, start=False, stop=last)

            def x_transposes(T, g, c):
                pe.wait_ge(s_xr, (g + 1) * CK + c + 1)
                tp_free(pe, T, g, ("x", c))
                pe.sem_inc(s_carrier, 1)
                for w in range(GRID):
                    ins = pe.transpose(T.bank_of(("x", c))[:, w * XP:(w + 1) * XP], Xr[0:XP, c % 2, w, :],
                                       ident[0:XP, 0:XP])
                ins.then_inc(s_tp, 1)

            def embed(T, g, s):
                use = ("emb", s)
                tp_done(pe, T, g, ("x", CK - 1))
                if T is FIRST and s == 0:
                    pe.wait_ge(s_wtlo, 1)
                mm_free(pe, T, g, use)
                for c in range(CK):
                    t = slice(AT[s], AT[s] + NS[s])
                    ph, pl = (t_[:, c].rearrange("p b t -> p (b t)") for t_ in (pTh, pTl))
                    ins = three(T.bank_of(use)[0:NS[s], 0:EMB], ph[:, t], pl[:, t],
                                Wth[:, c, :], Wtl[:, c, :], c == 0, c == CK - 1)
                ins.then_inc(s_mm, 1)

            def transposes_of(T, g, use, src, n):
                tp_free(pe, T, g, use)
                for k in range(EK):
                    ins = pe.transpose(T.bank_of(use)[:, k * n:(k + 1) * n], src[0:n, k * P:(k + 1) * P],
                                       ident[0:n, 0:n])
                ins.then_inc(s_tp, 1)

            def rank(g, bank_):
                dst = bank_[0:BM, 0:NSUB * EXPERTS]
                pe.wait_ge(s_A, g + 1)
                pe.wait_ge(s_carry, g + 1)
                pe.matmul(dst, lower[0:BM, 0:BM], flat(A)[0:BM, :], start=True, stop=False)
                pe.matmul(dst.rearrange("p (s e) -> p s e", e=EXPERTS), ones[0:BM, 0:BM],
                          carry[0:BM].rearrange("p (a e) -> p a e", a=1).broadcast_to([BM, NSUB, EXPERTS]),
                          start=False, stop=False)
                for back in range(1, NSUB):
                    last = pe.matmul(dst[:, back * EXPERTS:], ones[0:BM, 0:BM],
                                     flat(A)[0:BM, 0:(NSUB - back) * EXPERTS], start=False,
                                     stop=(back == NSUB - 1))
                return last

            def q_or_k(T, g, use):
                kind, m = use
                wh, wl = (Wqh, Wql) if kind[0] == "q" else (Wkh, Wkl)
                mm_free(pe, T, g, use)
                for k in range(EK):
                    f = slice(m * P, (m + 1) * P)
                    ins = three(T.bank_of(use)[:, 0:GT], wh[:, k, f], wl[:, k, f],
                                xTh[:, k, :], xTl[:, k, :], k == 0, k == EK - 1)
                ins.then_inc(s_mm, 1)

            def token_values(T, g, n):
                use = ("v", n)
                s, half = n // 2, n % 2
                mm_free(pe, T, g, use)
                for k in range(EK):
                    t, f = slice(AT[s], AT[s] + NS[s]), slice(half * 512, half * 512 + 512)
                    ins = three(T.bank_of(use)[0:NS[s], :], xTh[:, k, t], xTl[:, k, t],
                                Wvh[:, k, f], Wvl[:, k, f], k == 0, k == EK - 1)
                ins.then_inc(s_mm, 1)

            def scores(T, g, i):
                use = ("S", i)
                s, half, par = i // 4, i % 4 // 2, i % 2
                n = NS[s]
                dst = T.bank_of(use)
                if i == 2:
                    mm_done(pe, T, g, ("kb", HK - 1))
                mm_free(pe, T, g, use)
                m = mask if s < 2 else mask2
                pe.matmul(dst[0:n, 0:4 * n], identb[0:n, 0:n], m[0:n].rearrange("p h k -> p (h k)"),
                          start=True, stop=False)
                t = slice(AT[s], AT[s] + n)
                r = slice(par * HD, par * HD + HD)
                for h in range(4):
                    ins = pe.matmul(dst[0:n, h * n:(h + 1) * n], QT[r, half * 4 + h, t], KT[r, half * 4 + h, t],
                                    start=False, stop=(h == 3))
                ins.then_inc(s_mm, 1)

            def p_transposes(T, g, i):
                use = ("PT", i)
                s, r = i // 4, i % 3
                n = NS[s]
                mm_done(pe, T, g, ("S", i))
                tp_free(pe, T, g, use)
                for h in range(4):
                    ins = pe.transpose(T.bank_of(use)[0:n, h * n:(h + 1) * n], Pr[0:n, r, h * n:(h + 1) * n],
                                       ident[0:n, 0:n])
                ins.then_inc(s_tp, 1)

            def values(T, g, i):
                use = ("AV", i)
                s, half, par, r = i // 4, i % 4 // 2, i % 2, i % 3
                n = NS[s]
                if i % 4 == 0:
                    mm_done(pe, T, g, ("v", 2 * s + 1))
                tp_done(pe, T, g, ("PT", i))
                mm_free(pe, T, g, use)
                for h in range(4):
                    ins = pe.matmul(T.bank_of(use)[0:n, h * (HD + 1):(h + 1) * (HD + 1)],
                                    PT[0:n, r, h * n:(h + 1) * n], V[0:n, s, (half * 4 + h) * 2 + par, :],
                                    start=True, stop=True)
                ins.then_inc(s_mm, 1)

            def o_transposes(T, g, i):
                use = ("OT", i)
                s, half = i // 2, i % 2
                n = NS[s]
                mm_done(pe, T, g, ("AV", 2 * i + 1))
                tp_free(pe, T, g, use)
                for m in range(4):
                    ins = pe.transpose(T.bank_of(use)[:, m * n:(m + 1) * n],
                                       O[0:n, half * 4 + m].rearrange("p a d -> p (a d)"), ident[0:n, 0:n])
                ins.then_inc(s_tp, 1)

            def project(T, g, s):
                use = ("proj", s)
                n = NS[s]
                pe.wait_ge(s_walo2, 2)
                half_done = T is LAST and s == NSUB - 1
                if not half_done:
                    mm_free(pe, T, g, use)
                tp_done(pe, T, g, ("OT", 2 * s + 1))
                for m in range(HK // 2 if half_done else 0, HK):
                    ins = three(T.bank_of(use)[0:n, 0:EMB], OTh[:, m, 0:n], OTl[:, m, 0:n],
                                Wuh[:, m, :], Wul[:, m, :], m == 0, m == HK - 1)
                ins.then_inc(s_mm, 1)

            def project_half(T, g, s):
                use = ("proj", s)
                tp_done(pe, T, g, ("OT", 2 * s))
                mm_free(pe, T, g, use)
                for m in range(HK // 2):
                    three(T.bank_of(use)[0:NS[s], 0:EMB], OTh[:, m, 0:NS[s]], OTl[:, m, 0:NS[s]],
                          Wuh[:, m, :], Wul[:, m, :], m == 0, False)

            def turn(T, g):
                for kind, i in T.steps:
                    use = (kind, i)
                    if kind == "x":
                        x_transposes(T, g, i)
                    if kind == "emb":
                        embed(T, g, i)
                    if kind == "xT":
                        pe.wait_ge(s_xn, (g + 1) * NSUB + i + 1)
                        transposes_of(T, g, use, xn[:, i], NS[i])
                    if kind in ("qa", "ka", "qb", "kb"):
                        if kind == "qa" and i == 0:
                            tp_done(pe, T, g, ("xT", NSUB - 1))
                        if T is FIRST and kind in ("qa", "ka") and i == 0:
                            pe.wait_ge(s_walo, 1 if kind == "qa" else 2)
                        q_or_k(T, g, use)
                    if kind == "v":
                        token_values(T, g, i)
                    if kind == "rank":
                        mm_free(pe, T, g, use)
                        rank(g, T.bank_of(use)).then_inc(s_mm, 1)
                    if kind == "S":
                        scores(T, g, i)
                    if kind == "PT":
                        p_transposes(T, g, i)
                    if kind == "AV":
                        values(T, g, i)
                    if kind == "OT":
                        o_transposes(T, g, i)
                    if kind == "proj_half":
                        project_half(T, g, i)
                    if kind == "proj":
                        project(T, g, i)
                    if kind == "x2T":
                        pe.wait_ge(s_xn2, g * NSUB + i + 1)
                        transposes_of(T, g, use, xn2[:, i], NS[i])
                    if kind == "route":
                        tp_done(pe, T, g, ("x2T", i))
                        mm_free(pe, T, g, use)
                        n = NS[i]
                        for k in range(EK):
                            t = slice(k * n, (k + 1) * n)
                            ins = three(T.bank_of(use)[0:n, 0:EXPERTS], x2Th[:, t], x2Tl[:, t],
                                        Wrh[:, k, :], Wrl[:, k, :], k == 0, k == EK - 1)
                        ins.then_inc(s_mm, 1)

            turn(FIRST, -1)
            pe.wait_ge(s_walo2, 1)
            pe.wait_ge(s_wtlo, 2)
            with pe.Fori(0, GROUPS - 1) as g:
                turn(LOOP, g)
            turn(LAST, GROUPS - 1)
            pe.wait_ge(s_mmdve, END["dve"])
            rank(GROUPS, bank[0]).then_inc(s_mm, 1)
            pe.matmul(bank[1][:, 0:EXPERTS], ones[0:BM, :], carry[0:BM, :], start=True, stop=False)
            for s in range(NSUB):
                last = pe.matmul(bank[1][:, 0:EXPERTS], ones[0:NS[s], :], A[0:NS[s], s, :], start=False,
                                 stop=(s == NSUB - 1))
            last.then_inc(s_cnt, 1)

            def rows(n):
                pe.wait_ge(s_xs, n * 16 + 16)
                for k in range(EK):
                    ins = pe.transpose(bank[2][:, k * P:(k + 1) * P], xs[:, k * P:(k + 1) * P], ident[:])
                ins.then_inc(s_bT, 1)

            def outputs(n, e):
                pe.wait_ge(s_hThi, n + 1)
                pe.wait_ge(s_hTlo, n + 1)
                wh, wl = (w[:, bass.ds(e, 1), :].rearrange("p a (m n) -> p (a m) n", m=MK) for w in (Woh, Wol))
                for m in range(MK):
                    t = slice(m * P, (m + 1) * P)
                    ins = three(bank[4][:, 0:EMB], hTh[:, t], hTl[:, t], wh[:, m, :], wl[:, m, :],
                                m == 0, m == MK - 1)
                ins.then_inc(s_y, 1)

            def expert(e, k, first, end):
                wait_first(pe, s_wlo, e * 3 + 3)
                with pe.Fori(first, end) as j:
                    pe.wait_ge(s_bThi, j + 1)
                    pe.wait_ge(s_bTlo, j + 1)
                    for b, (wh, wl), s in ((0, (Wgh, Wgl), s_g), (1, (Wph, Wpl), s_u)):
                        for c in range(EK):
                            t = slice(c * P, (c + 1) * P)
                            ins = three(bank[b][:, :], bTh[:, t], bTl[:, t], wh[k][:, c, :], wl[k][:, c, :],
                                        c == 0, c == EK - 1)
                        ins.then_inc(s, 1)
                    rows(j + 1)
                    outputs(j, expert_before(pe, e, first, j))
                    pe.wait_ge(s_hid, j + 1)
                    for m in range(MK):
                        t = slice(m * P, (m + 1) * P)
                        ins = pe.transpose(bank[3][:, t], hid[:, t], ident[:])
                    ins.then_inc(s_hT, 1)

            pe.wait_ge(s_tab, 1)
            rows(0)
            with pe.Fori(0, EXPERTS // 2) as ep:
                for k, blocks in enumerate(bounds(pe, ep * 2)):
                    expert(ep * 2 + k, k, *blocks)
            outputs(end_of_all(pe), EXPERTS - 1)

        @block.vector
        def _(dve):
            for n, (tile, value) in enumerate((
                    (pos2, 0.0), (zero, 0.0), (carry[:].bitcast(F32), 0.0), (live, 0.0), (xn2, 0.0), (LG, 0.0),
                    (minus_half, -0.5), (steps128[:, 0:1], -1.0))):
                dve.memset(tile if n in (0, 2, 7) else tile[:], value).then_inc(s_dset, 1)
            dve.memset(pTh[:, :, :, 0:2].bitcast(F32), 0.0).then_inc(s_dset, 1)
            for e in range(EXPERTS):
                dve.memset(iota[:, e:e + 1], float(e)).then_inc(s_dset, 1)
            for j in range(1, MAXNB):
                dve.memset(steps128[:, j:j + 1], float(P * j)).then_inc(s_dset, 1)
            dve.wait_ge(s_dset, NDSET - 2)
            dve.tensor_scalar(region[:], iota[:], float(REGION), None, ALU.mult).then_inc(s_dset, 1)
            dve.tensor_scalar(yshift[:], iota[:], float(-REGION), float(P), ALU.mult, ALU.add).then_inc(s_dset, 1)
            dve.wait_ge(s_dset, NDSET)

            def weights_lo(n):
                _, wh, wl, src = WA[n]
                dve.wait_ge(s_wahi, n + 1)
                dve.tensor_tensor(flat(wl), src, flat(wh).bitcast(F32), ALU.subtract).then_inc(s_walo, 1)

            def take_lo(T, g, use, dst, src, hi):
                tp_full(dve, T, g, use)
                tp_hi(dve, T, g, use)
                dve.tensor_tensor(dst, src, hi.bitcast(F32), ALU.subtract).then_inc(s_tpdve, 1)

            def bc3(t, n=NSUB):
                return t.rearrange("p (s a) -> p s a", a=1).broadcast_to([P, n, EXPERTS])

            def be(t, n=NSUB):
                return t.rearrange("p (a e) -> p a e", a=1).broadcast_to([P, n, EXPERTS])

            CHOSEN = (0, 3, 6, 12, 18, 22, CHOOSE)

            def choose(turn, part):
                done = [turn * CHOOSE + CHOSEN[part]]

                def step(ins, wait=True):
                    done[0] += 1
                    ins.then_inc(s_ro, 1)
                    if wait:
                        wait_first(dve, s_ro, done[0])

                h = [hot[:, bass.ds(turn, 1), k].rearrange("p a s e -> p (a s) e") for k in range(2)]
                if part == 0:
                    for s in range(NSUB):
                        step(dve.max(top[:, s, :], LG[:, s, :]), s == NSUB - 1)
                    dve.tensor_tensor(sh[:], LG[:], bc3(top[:, :, 0]), ALU.subtract).then_inc(s_sh, 1)
                if part == 1:
                    dve.wait_ge(s_rexp, turn + 1)
                    step(dve.tensor_reduce(sm[:], ex[:], AX.X, ALU.add))
                    step(dve.reciprocal(ri[:], sm[:]))
                    step(dve.tensor_tensor(pr[:], ex[:], bc3(ri[:]), ALU.mult))
                if part == 2:
                    for s in range(NSUB):
                        step(dve.max(tpr[:, s, :], pr[:, s, :]), s == NSUB - 1)
                    for s in range(NSUB):
                        step(dve.max_index(tix[:, s, :], tpr[:, s, :], pr[:, s, :]), s == NSUB - 1)
                if part == 3:
                    step(dve.tensor_copy(tif[:], tix[:, :, 0:2]))
                    step(dve.tensor_tensor(lohi[:, 0, :], tif[:, :, 0], tif[:, :, 1], ALU.min), False)
                    step(dve.tensor_tensor(lohi[:, 1, :], tif[:, :, 0], tif[:, :, 1], ALU.max))
                    for k in range(2):
                        step(dve.tensor_tensor(h[k], be(iota[:]), bc3(lohi[:, k, :]), ALU.is_equal), k == 1)
                    step(dve.tensor_tensor(A[:], h[0], h[1], ALU.add))
                    dve.sem_inc(s_A, 1)
                if part == 4:
                    step(dve.tensor_tensor(sm[:], tpr[:, :, 0], tpr[:, :, 1], ALU.add))
                    step(dve.tensor_scalar(sm[:], sm[:], 1e-8, None, ALU.add))
                    step(dve.reciprocal(ri[:], sm[:]))
                    step(dve.tensor_tensor(pw[:], pr[:], bc3(ri[:]), ALU.mult))
                if part == 5:
                    for k in range(2):
                        step(dve.tensor_tensor(tmp8[:], h[k], pw[:], ALU.mult))
                        step(dve.tensor_reduce(wst[:, bass.ds(turn, 1), k].rearrange("p a s -> p (a s)"),
                                               tmp8[:], AX.X, ALU.add))

            def place(turn, src, final=False):
                done = [turn * PLACE]

                def step(ins):
                    done[0] += 1
                    ins.then_inc(s_tb, 1)
                    dve.wait_ge(s_tb, done[0])

                step(dve.tensor_tensor(rk[0:BM], src, be(region[:])[0:BM], ALU.add))
                for k in range(2):
                    h = hot[0:BM, bass.ds(turn, 1), k].rearrange("p a s e -> p (a s) e")
                    pf = posf[0:BM, bass.ds(turn, 1), k].rearrange("p a s -> p (a s)")
                    step(dve.tensor_tensor(tmp8[0:BM], h, rk[0:BM], ALU.mult))
                    step(dve.tensor_reduce(pf, tmp8[0:BM], AX.X, ALU.add))
                    wait_first(dve, s_sent, turn + 1)
                    dve.tensor_copy(pos_i[0:BM, k, :], pf).then_inc(s_pos_i, 1)
                if final:
                    return
                for s in range(NSUB):
                    step(dve.scalar_tensor_tensor(out=carry[0:NS[s]], in0=A[0:NS[s], s, :].bitcast(F32),
                                                  scalar=live[0:NS[s], 0:1], in1=carry[0:NS[s]].bitcast(F32),
                                                  op0=ALU.mult, op1=ALU.add))
                dve.sem_inc(s_carry, 1)
                step(dve.memset(live[:], 1.0))

            def reorder(c):
                dve.tensor_copy(
                    Xr[0:XP, c % 2, :, :].rearrange("p w (i j) -> p w i j", j=PATCH),
                    X[0:XP, c // 2].rearrange("p (i w j) -> p w i j", w=GRID, j=PATCH)
                    [:, :, c % 2 * 8:c % 2 * 8 + 8, :]).then_inc(s_xr, 1)

            def layer_norm(Hb, s, n, stats, mv, veps, s_ln, s_ve, count):
                dve.bn_stats(stats[0:n, s, :], Hb).then_inc(s_ln, 1)
                wait_first(dve, s_ln, count * 2 + 1)
                dve.bn_aggr(mv[0:n, s, :], stats[0:n, s, :]).then_inc(s_ln, 1)
                dve.wait_ge(s_ln, count * 2 + 2)
                dve.tensor_scalar(veps[0:n, s:s + 1], mv[0:n, s, 1:2], EPS, None, ALU.add).then_inc(s_ve, 1)

            def turn(T, g):
                for kind, i in T.steps:
                    use = (kind, i)
                    if kind == "choose":
                        choose(g, i)
                    if kind == "place":
                        mm_full(dve, T, g, ("rank", 0))
                        place(g, T.bank_of(("rank", 0))[0:BM, 0:NSUB * EXPERTS].rearrange("p (s e) -> p s e", s=NSUB))
                        dve.sem_inc(s_mmdve, 1)
                    if T is FIRST and kind == "reorder":
                        dve.wait_ge(s_x, 16 * GI)
                        reorder(0)
                        reorder(1)
                        dve.wait_ge(s_wthi, 1)
                        dve.tensor_tensor(flat(Wtl), tok_W_raw, flat(Wth).bitcast(F32), ALU.subtract
                                          ).then_inc(s_wtlo, 1)
                        dve.wait_ge(s_wtlo, 1)
                        dve.memset(pTl[:, :, :, 0:2].bitcast(F32), 0.0).then_inc(s_ptl, 1)
                        dve.wait_ge(s_ptl, 1)
                    if T is FIRST and kind == "x" and i + 2 < CK:
                        tp_full(dve, T, g, use)
                        reorder(i + 2)
                    if T is FIRST and kind == "emb" and i == 0:
                        dve.wait_ge(s_set, 15)
                        dve.tensor_copy(lower[:], H[:, 0, 0:P]).then_inc(s_posadd, 1)
                        dve.tensor_scalar(ones[:], H[:, 0, 0:P], 0.0, 1.0, ALU.mult, ALU.add).then_inc(s_posadd, 1)
                        dve.wait_ge(s_pos, 96)
                        dve.wait_ge(s_pos2, 96)
                        dve.tensor_tensor(pos[:], pos[:], pos2, ALU.add).then_inc(s_posadd, 1)
                        dve.wait_ge(s_posadd, 3)
                    if kind == "x":
                        take_lo(T, g, use, pT_view(pTl, i), x_view(T, i), pT_view(pTh, i))
                    if T is FIRST and kind == "x" and i == CK - 1:
                        weights_lo(0)
                    if kind == "embedded":
                        use = ("emb", i)
                        n = NS[i]
                        Hb = H[0:n, (g + 1) * NSUB + i, :]
                        mm_full(dve, T, g, use)
                        dve.tensor_tensor(Hb, T.bank_of(use)[0:n, 0:EMB], pos[0:n, :], ALU.add).then_inc(s_mmdve, 1)
                        mm_done(dve, T, g, use)
                        dve.sem_inc(s_carrier, 1)
                        layer_norm(Hb, i, n, stats1, mv1, veps1, s_ln1, s_ve1, (g + 1) * NSUB + i)
                    if kind == "ln1":
                        n = NS[i]
                        dve.wait_ge(s_rstd1, (g + 1) * NSUB + i + 1)
                        dve.tensor_scalar(xn[0:n, i, :], H[0:n, (g + 1) * NSUB + i, :], mv1[0:n, i, 0:1],
                                          rstd1[0:n, i:i + 1], ALU.subtract, ALU.mult).then_inc(s_xn, 1)
                    if kind == "xT":
                        v = slice(AT[i], AT[i] + NS[i])
                        take_lo(T, g, use, xTl[:, :, v], xT_view(T, use), xTh[:, :, v])
                    if T is FIRST and kind == "xT" and i == NSUB - 1:
                        weights_lo(1)
                    if kind == "S":
                        s, r = i // 4, i % 3
                        n = NS[s]
                        mm_full(dve, T, g, use)
                        if i >= 3:
                            mm_done(dve, T, g, ("S", i - 3))
                        dve.tensor_reduce(rowmax[0:n, r, :],
                                          T.bank_of(use)[0:n, 0:4 * n].rearrange("p (h k) -> p h k", h=4),
                                          AX.X, ALU.max).then_inc(s_rm, 1)
                        dve.wait_ge(s_rm, g * NQ + i + 1)
                        dve.tensor_scalar(nmax[0:n, r, :], rowmax[0:n, r, :], -SCALE, None, ALU.mult
                                          ).then_inc(s_nm, 1)
                    if kind == "AV":
                        s, half, par = i // 4, i % 4 // 2, i % 2
                        n = NS[s]
                        mm_full(dve, T, g, use)
                        ov = T.bank_of(use)[0:n, 0:4 * (HD + 1)].rearrange("p (h d) -> p h d", h=4)
                        if i >= 2:
                            mm_done(dve, T, g, ("AV", i - 2))
                        dve.reciprocal(rsum[0:n, i % 2, :], ov[:, :, HD]).then_inc(s_rs, 1)
                        dve.wait_ge(s_rs, g * NQ + i + 1)
                        if i >= 4:
                            tp_full(dve, T, g, ("OT", 2 * (s - 1) + half))
                        dve.tensor_tensor(O[0:n, half * 4:half * 4 + 4, par, :], ov[:, :, 0:HD],
                                          rsum[0:n, i % 2, :].rearrange("p (h a) -> p h a", a=1)
                                          .broadcast_to([n, 4, HD]), ALU.mult).then_inc(s_mmdve, 1)
                    if kind == "OT":
                        s, half = i // 2, i % 2
                        n = NS[s]
                        take_lo(T, g, use, OTl[:, half * 4:half * 4 + 4, 0:n],
                                T.bank_of(use)[:, 0:4 * n].rearrange("p (m t) -> p m t", m=4),
                                OTh[:, half * 4:half * 4 + 4, 0:n])
                    if kind == "projected":
                        use = ("proj", i)
                        n = NS[i]
                        Hb = H[0:n, g * NSUB + i, :]
                        mm_full(dve, T, g, use)
                        dve.wait_ge(s_hb, g * NSUB + i + 1)
                        dve.tensor_tensor(Hb, T.bank_of(use)[0:n, 0:EMB], Hb, ALU.add).then_inc(s_mmdve, 1)
                        mm_done(dve, T, g, use)
                        dve.sem_inc(s_carrier, 1)
                        layer_norm(Hb, i, n, stats2, mv2, veps2, s_ln2, s_ve2, g * NSUB + i)
                    if kind == "ln2":
                        n = NS[i]
                        dve.wait_ge(s_rstd2, g * NSUB + i + 1)
                        dve.wait_ge(s_sent, g + 2)
                        dve.tensor_scalar(xn2[0:n, i, :], H[0:n, g * NSUB + i, :], mv2[0:n, i, 0:1],
                                          rstd2[0:n, i:i + 1], ALU.subtract, ALU.mult).then_inc(s_xn2, 1)
                    if kind == "x2T":
                        take_lo(T, g, use, x2T_view(x2Tl, i), xT_view(T, use), x2T_view(x2Th, i))
                    if kind == "route":
                        n = NS[i]
                        mm_full(dve, T, g, use)
                        dve.tensor_copy(LG[0:n, i, :], T.bank_of(use)[0:n, 0:EXPERTS]).then_inc(s_mmdve, 1)
                        mm_done(dve, T, g, use)

            turn(FIRST, -1)
            dve.wait_ge(s_wthi, 2)
            dve.tensor_tensor(flat(Wrl), flat(Wr), flat(Wrh).bitcast(F32), ALU.subtract).then_inc(s_wtlo, 1)
            dve.wait_ge(s_walo2, 1)
            dve.memset(V[:, :, :, HD:HD + 1], 1.0).then_inc(s_ptl, 1)
            dve.sem_inc(s_carry, 1)
            with dve.Fori(0, GROUPS - 1) as g:
                turn(LOOP, g)
            turn(LAST, GROUPS - 1)
            for part in range(4):
                choose(GROUPS, part)
            dve.wait_ge(s_mm, END["mm"] + 1)
            place(GROUPS, bank[0][0:BM, 0:NSUB * EXPERTS].rearrange("p (s e) -> p s e", s=NSUB), final=True)

            done = [GROUPS * PLACE + 5]

            def step(ins):
                done[0] += 1
                ins.then_inc(s_tb, 1)
                dve.wait_ge(s_tb, done[0])

            dve.wait_ge(s_cnt, 1)
            step(dve.tensor_copy(cnt[:], bank[1][:, 0:EXPERTS]))
            step(dve.tensor_tensor(nbc[:], cnt[:].rearrange("p (e a) -> p e a", a=1)
                                   .broadcast_to([P, EXPERTS, MAXNB]),
                                   steps128[:].rearrange("p (a j) -> p a j", a=1)
                                   .broadcast_to([P, EXPERTS, MAXNB]), ALU.is_gt))
            step(dve.tensor_reduce(nb[:], nbc[:], AX.X, ALU.add))
            step(dve.tensor_tensor(st8[:], before[:], be(nb[:], EXPERTS), ALU.mult))
            step(dve.tensor_reduce(st[:], st8[:], AX.X, ALU.add))
            step(dve.tensor_copy(tab[:, 0, :], cnt[:]))
            step(dve.tensor_copy(tab[:, 1, :], st[:]))
            step(dve.tensor_tensor(nb[:], nb[:], st[:], ALU.add))
            dve.tensor_copy(tab[:, 2, :], nb[:]).then_inc(s_tab, 1)
            choose(GROUPS, 4)
            choose(GROUPS, 5)
            step(dve.scalar_tensor_tensor(out=sty[:], in0=st[:], scalar=float(P), in1=yshift[:],
                                          op0=ALU.mult, op1=ALU.add))
            for g in range(GROUPS):
                step(dve.tensor_tensor(ty[0:BM, g].rearrange("p k s e -> p (k s) e"),
                                       hot[0:BM, g + 1].rearrange("p k s e -> p (k s) e"),
                                       be(sty[:], 2 * NSUB)[0:BM], ALU.mult))
            step(dve.tensor_reduce(posy[0:BM].rearrange("p g k s -> p (g k s)"),
                                   ty[0:BM].rearrange("p g k s e -> p (g k s) e"), AX.X, ALU.add))
            step(dve.tensor_tensor(posy[0:BM].rearrange("p g k s -> p (g k s)"),
                                   posy[0:BM].rearrange("p g k s -> p (g k s)"),
                                   posf[0:BM, 1:].rearrange("p g k s -> p (g k s)"), ALU.add))
            dve.tensor_copy(posy_i[0:BM].rearrange("p g k s -> p (g k s)"),
                            posy[0:BM].rearrange("p g k s -> p (g k s)")).then_inc(s_posy, 1)

            def weights_hi(e, k):
                raw_there(dve, e, k)
                dve.tensor_copy(flat(Wph[k]), raw[k][:, 1024:2048]).then_inc(s_whi_d, 1)
                dve.tensor_copy(Woh[:, bass.ds(e, 1), :].rearrange("p a n -> p (a n)"),
                                raw[k][:, 2048:3072]).then_inc(s_whi_d, 1)

            def rows_lo(n):
                dve.wait_ge(s_bThi, n + 1)
                dve.tensor_tensor(bTl[:], bank[2][:, 0:EMB], bTh[:].bitcast(F32), ALU.subtract
                                  ).then_inc(s_bTlo, 1)

            def add_bo(n, e):
                dve.wait_ge(s_y, n + 1)
                dve.wait_ge(s_yst, n * 16 + 1)
                dve.tensor_tensor(ysb[:], bank[4][:, 0:EMB],
                                  bo[:, bass.ds(e, 1), :].rearrange("p a n -> p (a n)"), ALU.add
                                  ).then_inc(s_ysb, 1)

            def expert(e, k, first, end):
                wait_first(dve, s_bias[k], (e + 2 - k) * 16)
                with dve.Fori(first, end) as j:
                    dve.wait_ge(s_g, j + 1)
                    dve.tensor_tensor(gsum[:], bank[0][:], bgu[k][:, 0, :], ALU.add).then_inc(s_gs, 1)
                    dve.wait_ge(s_u, j + 1)
                    dve.tensor_tensor(usum[:], bank[1][:], bgu[k][:, 1, :], ALU.add).then_inc(s_us, 1)
                    dve.wait_ge(s_us, j + 1)
                    dve.wait_ge(s_silu, j + 1)
                    dve.tensor_tensor(hid[:], gact[:], usum[:], ALU.mult).then_inc(s_hid, 1)
                    rows_lo(j + 1)
                    add_bo(j, expert_before(dve, e, first, j))
                    dve.wait_ge(s_hThi, j + 2)
                    dve.tensor_tensor(hTl[:], bank[3][:], hTh[:].bitcast(F32), ALU.subtract
                                      ).then_inc(s_hTlo, 1)

            dve.memset(hTh[:].bitcast(F32), 0.0)
            dve.memset(hTl[:].bitcast(F32), 0.0).then_inc(s_hTlo, 1)
            rows_lo(0)
            dve.wait_ge(s_bo, 16)
            with dve.Fori(0, EXPERTS // 2 - 1) as ep:
                for k, blocks in enumerate(bounds(dve, ep * 2)):
                    expert(ep * 2 + k, k, *blocks)
                    weights_hi(ep * 2 + k + 2, k)
            for k, blocks in enumerate(bounds(dve, EXPERTS - 2)):
                expert(EXPERTS - 2 + k, k, *blocks)
            add_bo(end_of_all(dve), EXPERTS - 1)
            for k in range(2):
                for b in range(BLOCKS):
                    n, g, s = NS[b % NSUB], b // NSUB, b % NSUB
                    if k == 0:
                        dve.wait_ge(s_gath[k][g], 16 * NSUB)
                    else:
                        dve.wait_ge(s_gath[k][b], 16)
                        dve.wait_ge(s_add, b + 1)
                    dve.scalar_tensor_tensor(out=H[0:n, b, :], in0=gath[k][0:n, b, :],
                                             scalar=wst[0:n, g + 1, k, s:s + 1], in1=H[0:n, b, :],
                                             op0=ALU.mult, op1=ALU.add).then_inc(s_add, 1)


_INS = ['x', 'cls_tok', 'L0_tok_W', 'L0_tok_b', 'L0_tok_class_token', 'L0_tok_pos_emb', 'L0_attn_w_q',
        'L0_attn_w_k', 'L0_attn_w_v', 'L0_attn_w_u', 'L0_attn_b_u', 'L0_ffn_W_router', 'L0_ffn_W_gate',
        'L0_ffn_b_gate', 'L0_ffn_W_up', 'L0_ffn_b_up', 'L0_ffn_W_out', 'L0_ffn_b_out']
_OUTS = [((IMAGES, TOK, EMB), 'float32')]


def kernel(**inputs):
    import numpy as _np
    import concourse.bacc as _bacc
    from concourse import mybir as _mybir
    from concourse.bass_utils import run_bass_kernel_spmd as _run

    nc = _bacc.Bacc("TRN2", target_bir_lowering=False, num_devices=1)
    arrays, args = {}, []
    for name in _INS:
        a = _np.ascontiguousarray(inputs[name])
        arrays[f"in_{name}_dram"] = a
        args.append(nc.dram_tensor(f"in_{name}_dram", a.shape, _mybir.dt.from_np(a.dtype), kind="ExternalInput").ap())
    for i, (shape, dtype) in enumerate(_OUTS):
        dt = _mybir.dt.from_np(_np.dtype(dtype))
        args.append(nc.dram_tensor(f"out_{i}_dram", shape, dt, kind="ExternalOutput").ap())
    vit_tower(nc, *args)
    r = _run(nc, [arrays], core_ids=[0])
    got = tuple(r.results[0][f"out_{i}_dram"] for i in range(len(_OUTS)))
    return got[0]
```
